# Optimizing a Trainium2 kernel written in Bass

```python
import numpy as np
import jax
import jax.numpy as jnp

def _softmax(x, axis=-1):
    return jax.nn.softmax(x, axis=axis)

def _gelu(x):
    return jax.nn.gelu(x, approximate=True)

def _silu(x):
    return jax.nn.silu(x)

def _sigmoid(x):
    return jax.nn.sigmoid(x)

def _layernorm(x, axis=-1, eps=1e-05):
    m = jnp.mean(x, axis=axis, keepdims=True)
    v = jnp.var(x, axis=axis, keepdims=True)
    return (x - m) / jnp.sqrt(v + eps)

def _scatter_add(tgt, idx, src, axis=0):
    return tgt.at[idx].add(src)

def _segment_sum(src, seg, n):
    return jax.ops.segment_sum(src, seg, n)
kernel_name = 'mk_xattn_ffn_d4_seqx_r8_470f25'

def setup_inputs(seed: int=0):
    np.random.seed(seed)
    _w = jnp.asarray

    def _rec_inputs():
        import jax
        import jax.numpy as jnp
        _rk = jax.random.key(seed)
        x = -0.0002928 + 1 * jax.random.normal(jax.random.fold_in(_rk, 1), (4, 512, 128), jnp.float32)
        _lenS = 512 - jax.random.randint(jax.random.fold_in(_rk, 7), (4,), 0, max(1, 512 // 4) + 1, jnp.int32)
        _lenS2 = 77 - jax.random.randint(jax.random.fold_in(_rk, 8), (4,), 0, max(1, 77 // 4) + 1, jnp.int32)
        _ctx_1024P = jax.random.normal(jax.random.fold_in(_rk, 11), (4, 16, 128), jnp.float32)
        _ctx_1024c = jax.random.dirichlet(jax.random.fold_in(_rk, 511), 0.3 * jnp.ones((16,), jnp.float32), (4, 77))
        _ctx_1024t = jnp.einsum('bsk,bkd->bsd', _ctx_1024c, _ctx_1024P)
        _ctx_1024t = _ctx_1024t * jax.lax.rsqrt(jnp.mean(jnp.square(_ctx_1024t)) + 1e-12) * 0.953939
        ctx_1024 = -1.39393e-06 + 0.999914 * (_ctx_1024t + 0.3 * jax.random.normal(jax.random.fold_in(_rk, 611), (4, 77, 128), jnp.float32))
        _validS = jnp.arange(512)[None, :] < _lenS[:, None]
        _validS2 = jnp.arange(77)[None, :] < _lenS2[:, None]
        _causal = jnp.tril(jnp.ones((512, 512), dtype=bool))
        mask_Bx1xSxS2_ik0 = jnp.where(jnp.broadcast_to(_validS2[:, None, None, :], (4, 1, 512, 77)), 0, 1).astype(jnp.int32)
        mask_Bx1xS2_bk0 = jnp.logical_not(jnp.broadcast_to(_validS2[:, None, :], (4, 1, 77)))
        mask_BxSxS2_ik1 = jnp.where(jnp.broadcast_to(_validS2[:, None, :], (4, 512, 77)), 1, 0).astype(jnp.int32)
        return (x, ctx_1024, mask_Bx1xSxS2_ik0, mask_Bx1xS2_bk0, mask_BxSxS2_ik1)
    x, ctx_1024, mask_Bx1xSxS2_ik0, mask_Bx1xS2_bk0, mask_BxSxS2_ik1 = _rec_inputs()

    def _L0_xattn_setup():
        import math
        import jax, jax.numpy as jnp
        import numpy as np
        D_MODEL = 128
        N_HEADS = 16
        D_K = D_MODEL // N_HEADS

        def _build_neighbours(n_heads):
            side = int(math.sqrt(n_heads))
            cols = side + 1 if side * side < n_heads else side
            positions = [divmod(i, cols) for i in range(n_heads)]
            pos_map = {p: j for j, p in enumerate(positions)}
            nb_idx = np.full((n_heads, 8), -1, dtype=np.int64)
            nb_w = np.zeros((n_heads, 8), dtype=np.float32)
            for i, (r, c) in enumerate(positions):
                k = 0
                for dr in (-1, 0, 1):
                    for dc in (-1, 0, 1):
                        if dr == 0 and dc == 0:
                            continue
                        j = pos_map.get((r + dr, c + dc))
                        if j is not None and k < 8:
                            nb_idx[i, k] = j
                            nb_w[i, k] = math.exp(-math.hypot(dr, dc))
                            k += 1
            return (nb_idx, nb_w)

        def _phase_biases(coupling):
            H = coupling.shape[0]
            nb_idx, nb_w = _build_neighbours(H)
            phases = [jnp.asarray(0.0, coupling.dtype) for _ in range(H)]
            two_pi = 2.0 * math.pi
            for h in range(H):
                force = jnp.asarray(0.0, coupling.dtype)
                for k in range(8):
                    j = int(nb_idx[h, k])
                    if j >= 0:
                        force = force + jnp.asarray(nb_w[h, k], coupling.dtype) * jnp.sin(phases[j] - phases[h])
                intrinsic = 1.0 + 0.1 * h
                new_phase = (phases[h] + 0.01 * (intrinsic + coupling[h] * force)) % two_pi
                phases[h] = new_phase
            return 0.1 * jnp.cos(jnp.stack(phases))
        key = jax.random.key(seed)
        ks = jax.random.split(key, 9)
        B, L = (2, 256)
        std = 0.02
        return {'query': jax.random.normal(ks[0], (B, L, D_MODEL), jnp.float32), 'key': jax.random.normal(ks[1], (B, L, D_MODEL), jnp.float32), 'value': jax.random.normal(ks[2], (B, L, D_MODEL), jnp.float32), 'Wq': std * jax.random.normal(ks[3], (N_HEADS, D_MODEL, D_K), jnp.float32), 'Wk': std * jax.random.normal(ks[4], (N_HEADS, D_MODEL, D_K), jnp.float32), 'Wv': std * jax.random.normal(ks[5], (N_HEADS, D_MODEL, D_K), jnp.float32), 'out_w': std * jax.random.normal(ks[6], (D_MODEL, D_MODEL), jnp.float32), 'out_b': jnp.zeros((D_MODEL,), jnp.float32), 'coupling': 0.1 * jnp.ones((N_HEADS,), jnp.float32)}
    _L0_xattn_all = _L0_xattn_setup()
    _L0_xattn_in = {k: v for k, v in _L0_xattn_all.items() if k in ('Wq', 'Wk', 'Wv', 'out_w', 'out_b', 'coupling')}
    del _L0_xattn_all

    def _L0_ffn_setup():
        import jax, jax.numpy as jnp
        import numpy as np

        def _bitlinear(x, w_latent):
            scale = jax.lax.stop_gradient(jnp.clip(jnp.mean(jnp.abs(w_latent), axis=1, keepdims=True), 1e-05, None))
            tern = jnp.clip(jnp.round(w_latent / scale), -1.0, 1.0)
            w = w_latent + jax.lax.stop_gradient(tern - w_latent)
            return x @ (w * scale).T
        key = jax.random.key(seed)
        ks = jax.random.split(key, 6)
        dim, hidden, rank = (128, 512, 16)
        B, S = (4, 512)
        x = jax.random.normal(ks[0], (B, S, dim), dtype=jnp.float32)
        w_fc = 0.02 * jax.random.normal(ks[1], (hidden, dim), dtype=jnp.float32)
        w_proj = 0.02 * jax.random.normal(ks[2], (dim, hidden), dtype=jnp.float32)
        u = 0.02 * jax.random.normal(ks[3], (hidden, rank), dtype=jnp.float32)
        v = 0.02 * jax.random.normal(ks[4], (rank, dim), dtype=jnp.float32)
        fast_b = jax.random.normal(ks[5], (rank, rank), dtype=jnp.float32)
        gate = jnp.float32(0.05)
        return {'x': x, 'fast_b': fast_b, 'w_fc': w_fc, 'w_proj': w_proj, 'u': u, 'v': v, 'gate': gate}
    _L0_ffn_all = _L0_ffn_setup()
    _L0_ffn_in = {k: v for k, v in _L0_ffn_all.items() if k in ('fast_b', 'w_fc', 'w_proj', 'u', 'v', 'gate')}
    del _L0_ffn_all

    def _L1_xattn_setup():
        import jax, jax.numpy as jnp
        import numpy as np
        B, NQ, NKV = (2, 256, 256)
        QUERY_DIM = 128
        CONTEXT_DIM = 128
        HEADS = 16
        DIM_HEAD = 64
        INNER = HEADS * DIM_HEAD
        SCALE = DIM_HEAD ** (-0.5)
        key = jax.random.key(seed)
        ks = jax.random.split(key, 9)
        x = jax.random.normal(ks[0], (B, NQ, QUERY_DIM), dtype=jnp.float32)
        context = jax.random.normal(ks[1], (B, NKV, CONTEXT_DIM), dtype=jnp.float32)
        tgt_mask = jax.random.randint(ks[2], (B, 1, NQ, NKV), 0, 2, dtype=jnp.int32)
        src_mask = jax.random.randint(ks[3], (B, 1, NKV), 0, 2) > 0
        w = 0.02
        Wq = jax.random.normal(ks[4], (INNER, QUERY_DIM), dtype=jnp.float32) * w
        Wk = jax.random.normal(ks[5], (INNER, CONTEXT_DIM), dtype=jnp.float32) * w
        Wv = jax.random.normal(ks[6], (INNER, CONTEXT_DIM), dtype=jnp.float32) * w
        Wo = jax.random.normal(ks[7], (QUERY_DIM, INNER), dtype=jnp.float32) * w
        bo = jax.random.normal(ks[8], (QUERY_DIM,), dtype=jnp.float32) * w
        return {'x': x, 'context': context, 'tgt_mask': tgt_mask, 'src_mask': src_mask, 'Wq': Wq, 'Wk': Wk, 'Wv': Wv, 'Wo': Wo, 'bo': bo}
    _L1_xattn_all = _L1_xattn_setup()
    _L1_xattn_in = {k: v for k, v in _L1_xattn_all.items() if k in ('Wq', 'Wk', 'Wv', 'Wo', 'bo')}
    del _L1_xattn_all

    def _L1_ffn_setup():
        import jax, jax.numpy as jnp
        import numpy as np
        B, S, D = (4, 256, 128)
        O = 128
        E = 8
        K = 2
        key = jax.random.key(seed)
        k1, k2, k3, k4, k5 = jax.random.split(key, 5)
        scale = 1.0 / np.sqrt(D)
        x = jax.random.normal(k1, (B, S, D), dtype=jnp.float32)
        We = jax.random.uniform(k2, (E, D, O), dtype=jnp.float32, minval=-scale, maxval=scale)
        be = jax.random.uniform(k3, (E, O), dtype=jnp.float32, minval=-scale, maxval=scale)
        Wg = jax.random.uniform(k4, (D, E), dtype=jnp.float32, minval=-scale, maxval=scale)
        bg = jax.random.uniform(k5, (E,), dtype=jnp.float32, minval=-scale, maxval=scale)
        return {'x': x, 'We': We, 'be': be, 'Wg': Wg, 'bg': bg}
    _L1_ffn_all = _L1_ffn_setup()
    _L1_ffn_in = {k: v for k, v in _L1_ffn_all.items() if k in ('We', 'be', 'Wg', 'bg')}
    del _L1_ffn_all

    def _L2_xattn_setup():
        import jax, jax.numpy as jnp
        import numpy as np
        D_MODEL = 128
        DK = 64
        N_HEADS = D_MODEL // DK
        MASK = True
        key = jax.random.key(seed)
        ks = jax.random.split(key, 8)
        B, S = (4, 256)
        scale = 1.0 / np.sqrt(D_MODEL)
        return {'query_data': jax.random.normal(ks[0], (B, S, D_MODEL), dtype=jnp.float32), 'key_data': jax.random.normal(ks[1], (B, S, D_MODEL), dtype=jnp.float32), 'value_data': jax.random.normal(ks[2], (B, S, D_MODEL), dtype=jnp.float32), 'Wq': jax.random.normal(ks[3], (D_MODEL, D_MODEL), dtype=jnp.float32) * scale, 'Wk': jax.random.normal(ks[4], (D_MODEL, D_MODEL), dtype=jnp.float32) * scale, 'Wv': jax.random.normal(ks[5], (D_MODEL, D_MODEL), dtype=jnp.float32) * scale, 'Wp': jax.random.normal(ks[6], (D_MODEL, D_MODEL), dtype=jnp.float32) * scale, 'bp': jnp.zeros((D_MODEL,), dtype=jnp.float32)}
    _L2_xattn_all = _L2_xattn_setup()
    _L2_xattn_in = {k: v for k, v in _L2_xattn_all.items() if k in ('Wq', 'Wk', 'Wv', 'Wp', 'bp')}
    del _L2_xattn_all

    def _L2_ffn_setup():
        import jax, jax.numpy as jnp
        import numpy as np
        MICRO_BATCHES = 2
        TOP_K = 2
        LN_EPS = 1e-05
        B, S, D = (4, 512, 128)
        E = 8
        DFF = 4 * D

        def _layernorm(x, g, b):
            mu = jnp.mean(x, axis=-1, keepdims=True)
            var = jnp.mean(jnp.square(x - mu), axis=-1, keepdims=True)
            return (x - mu) * jax.lax.rsqrt(var + LN_EPS) * g + b
        key = jax.random.key(seed)
        ks = jax.random.split(key, 12)
        sd = 1.0 / np.sqrt(D)
        sf = 1.0 / np.sqrt(DFF)
        return {'x': jax.random.normal(ks[0], (B, S, D), dtype=jnp.float32), 'ln_g': jnp.ones((D,), jnp.float32), 'ln_b': jnp.zeros((D,), jnp.float32), 'attn_w': jax.random.normal(ks[1], (D, D), jnp.float32) * sd, 'attn_b': jnp.zeros((D,), jnp.float32), 'gate_w': jax.random.normal(ks[2], (D, E), jnp.float32) * sd, 'w1': jax.random.normal(ks[3], (E, D, DFF), jnp.float32) * sd, 'b1': jnp.zeros((E, DFF), jnp.float32), 'w2': jax.random.normal(ks[4], (E, DFF, D), jnp.float32) * sf, 'b2': jnp.zeros((E, D), jnp.float32), 'next_w': jax.random.normal(ks[5], (D, D), jnp.float32) * sd, 'next_b': jnp.zeros((D,), jnp.float32)}
    _L2_ffn_all = _L2_ffn_setup()
    _L2_ffn_in = {k: v for k, v in _L2_ffn_all.items() if k in ('ln_g', 'ln_b', 'attn_w', 'attn_b', 'gate_w', 'w1', 'b1', 'w2', 'b2', 'next_w', 'next_b')}
    del _L2_ffn_all

    def _L3_xattn_setup():
        import jax, jax.numpy as jnp
        import numpy as np
        N_HEADS = 16
        D_MODEL = 128
        HEAD_D = D_MODEL // N_HEADS
        key = jax.random.key(seed)
        ks = jax.random.split(key, 8)
        B, S, D = (4, 256, D_MODEL)
        scale = 1.0 / np.sqrt(D)
        return {'query': jax.random.normal(ks[0], (B, S, D), jnp.float32), 'key': jax.random.normal(ks[1], (B, S, D), jnp.float32), 'value': jax.random.normal(ks[2], (B, S, D), jnp.float32), 'mask': jax.random.randint(ks[3], (B, S, S), 0, 2, jnp.int32), 'wq': jax.random.normal(ks[4], (D, D), jnp.float32) * scale, 'wk': jax.random.normal(ks[5], (D, D), jnp.float32) * scale, 'wv': jax.random.normal(ks[6], (D, D), jnp.float32) * scale, 'w_out': jax.random.normal(ks[7], (D, D), jnp.float32) * scale}
    _L3_xattn_all = _L3_xattn_setup()
    _L3_xattn_in = {k: v for k, v in _L3_xattn_all.items() if k in ('wq', 'wk', 'wv', 'w_out')}
    del _L3_xattn_all

    def _L3_ffn_setup():
        import math
        import jax, jax.numpy as jnp
        import numpy as np
        HIDDEN = 128
        INTER = 512
        EXPERTS = 8
        B, T = (4, 256)
        EPS = 1e-12
        CAP_FACTOR = 1.0
        MIN_CAP = 4

        def layer_norm(x, g, b, eps=EPS):
            m = jnp.mean(x, axis=-1, keepdims=True)
            v = jnp.var(x, axis=-1, keepdims=True)
            return (x - m) * jax.lax.rsqrt(v + eps) * g + b

        def top1_gate(x, wg, capacity):
            logits = x @ wg
            gates = jax.nn.softmax(logits, axis=-1)
            E = wg.shape[-1]
            idx = jnp.argmax(gates, axis=-1)
            mask1 = jax.nn.one_hot(idx, E, dtype=gates.dtype)
            locations = jnp.cumsum(mask1, axis=0) - mask1
            mask1 = mask1 * (locations < capacity).astype(gates.dtype)
            gates1_s = jnp.sum(gates * mask1, axis=-1)
            loc_s = jnp.sum(locations * mask1, axis=-1).astype(jnp.int32)
            loc_oh = jax.nn.one_hot(loc_s, capacity, dtype=gates.dtype)
            combine = gates1_s[:, None, None] * mask1[:, :, None] * loc_oh[:, None, :]
            dispatch = jax.lax.stop_gradient((combine > 0).astype(x.dtype))
            return (combine, dispatch)
        key = jax.random.key(seed)
        ks = jax.random.split(key, 8)
        s = 0.02
        return {'x': jax.random.normal(ks[0], (B, T, HIDDEN), jnp.float32), 'attn_nw': jnp.ones((HIDDEN,), jnp.float32), 'attn_nb': jnp.zeros((HIDDEN,), jnp.float32), 'wg': jax.random.normal(ks[1], (HIDDEN, EXPERTS), jnp.float32) * s, 'inter_w': jax.random.normal(ks[2], (EXPERTS, HIDDEN, INTER), jnp.float32) * s, 'inter_b': jnp.zeros((EXPERTS, INTER), jnp.float32), 'output_w': jax.random.normal(ks[3], (EXPERTS, INTER, HIDDEN), jnp.float32) * s, 'output_b': jnp.zeros((EXPERTS, HIDDEN), jnp.float32), 'res_inter_w': jax.random.normal(ks[4], (HIDDEN, INTER), jnp.float32) * s, 'res_inter_b': jnp.zeros((INTER,), jnp.float32), 'res_output_w': jax.random.normal(ks[5], (INTER, HIDDEN), jnp.float32) * s, 'res_output_b': jnp.zeros((HIDDEN,), jnp.float32), 'res_coef': jax.random.normal(ks[6], (HIDDEN, 2), jnp.float32) * s}
    _L3_ffn_all = _L3_ffn_setup()
    _L3_ffn_in = {k: v for k, v in _L3_ffn_all.items() if k in ('attn_nw', 'attn_nb', 'wg', 'inter_w', 'inter_b', 'output_w', 'output_b', 'res_inter_w', 'res_inter_b', 'res_output_w', 'res_output_b', 'res_coef')}
    del _L3_ffn_all
    return {'x': x, 'ctx_1024': ctx_1024, 'mask_Bx1xSxS2_ik0': mask_Bx1xSxS2_ik0, 'mask_Bx1xS2_bk0': mask_Bx1xS2_bk0, 'mask_BxSxS2_ik1': mask_BxSxS2_ik1, 'L0_xattn_Wq': _L0_xattn_in['Wq'], 'L0_xattn_Wk': _L0_xattn_in['Wk'], 'L0_xattn_Wv': _L0_xattn_in['Wv'], 'L0_xattn_out_w': _L0_xattn_in['out_w'], 'L0_xattn_out_b': _L0_xattn_in['out_b'], 'L0_xattn_coupling': _L0_xattn_in['coupling'], 'L0_ffn_fast_b': _L0_ffn_in['fast_b'], 'L0_ffn_w_fc': _L0_ffn_in['w_fc'], 'L0_ffn_w_proj': _L0_ffn_in['w_proj'], 'L0_ffn_u': _L0_ffn_in['u'], 'L0_ffn_v': _L0_ffn_in['v'], 'L0_ffn_gate': _L0_ffn_in['gate'], 'L1_xattn_Wq': _L1_xattn_in['Wq'], 'L1_xattn_Wk': _L1_xattn_in['Wk'], 'L1_xattn_Wv': _L1_xattn_in['Wv'], 'L1_xattn_Wo': _L1_xattn_in['Wo'], 'L1_xattn_bo': _L1_xattn_in['bo'], 'L1_ffn_We': _L1_ffn_in['We'], 'L1_ffn_be': _L1_ffn_in['be'], 'L1_ffn_Wg': _L1_ffn_in['Wg'], 'L1_ffn_bg': _L1_ffn_in['bg'], 'L2_xattn_Wq': _L2_xattn_in['Wq'], 'L2_xattn_Wk': _L2_xattn_in['Wk'], 'L2_xattn_Wv': _L2_xattn_in['Wv'], 'L2_xattn_Wp': _L2_xattn_in['Wp'], 'L2_xattn_bp': _L2_xattn_in['bp'], 'L2_ffn_ln_g': _L2_ffn_in['ln_g'], 'L2_ffn_ln_b': _L2_ffn_in['ln_b'], 'L2_ffn_attn_w': _L2_ffn_in['attn_w'], 'L2_ffn_attn_b': _L2_ffn_in['attn_b'], 'L2_ffn_gate_w': _L2_ffn_in['gate_w'], 'L2_ffn_w1': _L2_ffn_in['w1'], 'L2_ffn_b1': _L2_ffn_in['b1'], 'L2_ffn_w2': _L2_ffn_in['w2'], 'L2_ffn_b2': _L2_ffn_in['b2'], 'L2_ffn_next_w': _L2_ffn_in['next_w'], 'L2_ffn_next_b': _L2_ffn_in['next_b'], 'L3_xattn_wq': _L3_xattn_in['wq'], 'L3_xattn_wk': _L3_xattn_in['wk'], 'L3_xattn_wv': _L3_xattn_in['wv'], 'L3_xattn_w_out': _L3_xattn_in['w_out'], 'L3_ffn_attn_nw': _L3_ffn_in['attn_nw'], 'L3_ffn_attn_nb': _L3_ffn_in['attn_nb'], 'L3_ffn_wg': _L3_ffn_in['wg'], 'L3_ffn_inter_w': _L3_ffn_in['inter_w'], 'L3_ffn_inter_b': _L3_ffn_in['inter_b'], 'L3_ffn_output_w': _L3_ffn_in['output_w'], 'L3_ffn_output_b': _L3_ffn_in['output_b'], 'L3_ffn_res_inter_w': _L3_ffn_in['res_inter_w'], 'L3_ffn_res_inter_b': _L3_ffn_in['res_inter_b'], 'L3_ffn_res_output_w': _L3_ffn_in['res_output_w'], 'L3_ffn_res_output_b': _L3_ffn_in['res_output_b'], 'L3_ffn_res_coef': _L3_ffn_in['res_coef']}

def reference(x, ctx_1024, mask_Bx1xSxS2_ik0, mask_Bx1xS2_bk0, mask_BxSxS2_ik1, L0_xattn_Wq, L0_xattn_Wk, L0_xattn_Wv, L0_xattn_out_w, L0_xattn_out_b, L0_xattn_coupling, L0_ffn_fast_b, L0_ffn_w_fc, L0_ffn_w_proj, L0_ffn_u, L0_ffn_v, L0_ffn_gate, L1_xattn_Wq, L1_xattn_Wk, L1_xattn_Wv, L1_xattn_Wo, L1_xattn_bo, L1_ffn_We, L1_ffn_be, L1_ffn_Wg, L1_ffn_bg, L2_xattn_Wq, L2_xattn_Wk, L2_xattn_Wv, L2_xattn_Wp, L2_xattn_bp, L2_ffn_ln_g, L2_ffn_ln_b, L2_ffn_attn_w, L2_ffn_attn_b, L2_ffn_gate_w, L2_ffn_w1, L2_ffn_b1, L2_ffn_w2, L2_ffn_b2, L2_ffn_next_w, L2_ffn_next_b, L3_xattn_wq, L3_xattn_wk, L3_xattn_wv, L3_xattn_w_out, L3_ffn_attn_nw, L3_ffn_attn_nb, L3_ffn_wg, L3_ffn_inter_w, L3_ffn_inter_b, L3_ffn_output_w, L3_ffn_output_b, L3_ffn_res_inter_w, L3_ffn_res_inter_b, L3_ffn_res_output_w, L3_ffn_res_output_b, L3_ffn_res_coef):
    import jax
    import jax.numpy as jnp

    def _L0_xattn_ref(query, key, value, Wq, Wk, Wv, out_w, out_b, coupling):
        import math
        import jax, jax.numpy as jnp
        import numpy as np
        D_MODEL = 128
        N_HEADS = 16
        D_K = D_MODEL // N_HEADS

        def _build_neighbours(n_heads):
            side = int(math.sqrt(n_heads))
            cols = side + 1 if side * side < n_heads else side
            positions = [divmod(i, cols) for i in range(n_heads)]
            pos_map = {p: j for j, p in enumerate(positions)}
            nb_idx = np.full((n_heads, 8), -1, dtype=np.int64)
            nb_w = np.zeros((n_heads, 8), dtype=np.float32)
            for i, (r, c) in enumerate(positions):
                k = 0
                for dr in (-1, 0, 1):
                    for dc in (-1, 0, 1):
                        if dr == 0 and dc == 0:
                            continue
                        j = pos_map.get((r + dr, c + dc))
                        if j is not None and k < 8:
                            nb_idx[i, k] = j
                            nb_w[i, k] = math.exp(-math.hypot(dr, dc))
                            k += 1
            return (nb_idx, nb_w)

        def _phase_biases(coupling):
            H = coupling.shape[0]
            nb_idx, nb_w = _build_neighbours(H)
            phases = [jnp.asarray(0.0, coupling.dtype) for _ in range(H)]
            two_pi = 2.0 * math.pi
            for h in range(H):
                force = jnp.asarray(0.0, coupling.dtype)
                for k in range(8):
                    j = int(nb_idx[h, k])
                    if j >= 0:
                        force = force + jnp.asarray(nb_w[h, k], coupling.dtype) * jnp.sin(phases[j] - phases[h])
                intrinsic = 1.0 + 0.1 * h
                new_phase = (phases[h] + 0.01 * (intrinsic + coupling[h] * force)) % two_pi
                phases[h] = new_phase
            return 0.1 * jnp.cos(jnp.stack(phases))
        d_k = Wq.shape[-1]
        Q = jnp.einsum('bld,hdk->bhlk', query, Wq)
        K = jnp.einsum('bld,hdk->bhlk', key, Wk)
        V = jnp.einsum('bld,hdk->bhlk', value, Wv)
        scale = jnp.asarray(math.sqrt(float(d_k)), query.dtype)
        scores = jnp.einsum('bhlk,bhmk->bhlm', Q, K) / scale
        bias = _phase_biases(coupling)
        scores = scores + bias[None, :, None, None]
        attn = jax.nn.softmax(scores, axis=-1)
        ctx = jnp.einsum('bhlm,bhmk->bhlk', attn, V)
        B, H, L, _ = ctx.shape
        out = ctx.transpose(0, 2, 1, 3).reshape(B, L, H * d_k)
        return out @ out_w + out_b

    def _L0_ffn_ref(x, fast_b, w_fc, w_proj, u, v, gate):
        import jax, jax.numpy as jnp
        import numpy as np

        def _bitlinear(x, w_latent):
            scale = jax.lax.stop_gradient(jnp.clip(jnp.mean(jnp.abs(w_latent), axis=1, keepdims=True), 1e-05, None))
            tern = jnp.clip(jnp.round(w_latent / scale), -1.0, 1.0)
            w = w_latent + jax.lax.stop_gradient(tern - w_latent)
            return x @ (w * scale).T
        h = _bitlinear(x, w_fc) + gate * (x @ v.T @ fast_b.T @ u.T)
        r = jnp.maximum(h, 0.0)
        return _bitlinear(r * r, w_proj)

    def _L1_xattn_ref(x, context, tgt_mask, src_mask, Wq, Wk, Wv, Wo, bo):
        import jax, jax.numpy as jnp
        import numpy as np
        B, NQ, NKV = (2, 256, 256)
        QUERY_DIM = 128
        CONTEXT_DIM = 128
        HEADS = 16
        DIM_HEAD = 64
        INNER = HEADS * DIM_HEAD
        SCALE = DIM_HEAD ** (-0.5)
        b, nq, _ = x.shape
        nkv = context.shape[1]
        q = jnp.einsum('bnc,ec->bne', x, Wq).reshape(b, nq, HEADS, DIM_HEAD).transpose(0, 2, 1, 3)
        k = jnp.einsum('bmc,ec->bme', context, Wk).reshape(b, nkv, HEADS, DIM_HEAD).transpose(0, 2, 1, 3)
        v = jnp.einsum('bmc,ec->bme', context, Wv).reshape(b, nkv, HEADS, DIM_HEAD).transpose(0, 2, 1, 3)
        sim = jnp.einsum('bhid,bhjd->bhij', q, k) * SCALE
        neg = -jnp.finfo(sim.dtype).max
        sim = jnp.where(tgt_mask == 0, neg, sim)
        sim = jnp.where(src_mask[:, None, :], sim, neg)
        attn = jax.nn.softmax(sim, axis=-1)
        out = jnp.einsum('bhij,bhjd->bhid', attn, v)
        out = out.transpose(0, 2, 1, 3).reshape(b, nq, INNER)
        return jnp.einsum('bne,oe->bno', out, Wo) + bo

    def _L1_ffn_ref(x, We, be, Wg, bg):
        import jax, jax.numpy as jnp
        import numpy as np
        B, S, D = (4, 256, 128)
        O = 128
        E = 8
        K = 2
        b, s, d = x.shape
        x_flat = x.reshape(-1, d)
        gates = jax.nn.softmax(x_flat @ Wg + bg, axis=-1)
        topk_gates, topk_idx = jax.lax.top_k(gates, K)
        topk_gates = topk_gates / jnp.sum(topk_gates, axis=1, keepdims=True)
        expert_out = jnp.einsum('nd,edo->neo', x_flat, We) + be
        selected = jnp.take_along_axis(expert_out, topk_idx[:, :, None], axis=1)
        out = jnp.sum(selected * topk_gates[:, :, None], axis=1)
        return out.reshape(b, s, -1)

    def _L2_xattn_ref(query_data, key_data, value_data, Wq, Wk, Wv, Wp, bp):
        import jax, jax.numpy as jnp
        import numpy as np
        D_MODEL = 128
        DK = 64
        N_HEADS = D_MODEL // DK
        MASK = True
        B, S, _ = query_data.shape

        def split_heads(x, W):
            return (x @ W.T).reshape(B, -1, N_HEADS, DK).transpose(0, 2, 1, 3)
        q = split_heads(query_data, Wq)
        k = split_heads(key_data, Wk)
        v = split_heads(value_data, Wv)
        scores = jnp.einsum('bhqd,bhkd->bhqk', q, k) / np.sqrt(DK).astype(np.float32)
        if MASK:
            Sq, Sk = (scores.shape[-2], scores.shape[-1])
            causal = jnp.triu(jnp.ones((Sq, Sk), dtype=scores.dtype), k=1) * jnp.float32(-10000000000000.0)
            scores = scores + causal
        attn = jax.nn.softmax(scores, axis=-1)
        out = jnp.einsum('bhqk,bhkd->bhqd', attn, v)
        out = out.transpose(0, 2, 1, 3).reshape(B, S, D_MODEL)
        return out @ Wp.T + bp

    def _L2_ffn_ref(x, ln_g, ln_b, attn_w, attn_b, gate_w, w1, b1, w2, b2, next_w, next_b):
        import jax, jax.numpy as jnp
        import numpy as np
        MICRO_BATCHES = 2
        TOP_K = 2
        LN_EPS = 1e-05
        B, S, D = (4, 512, 128)
        E = 8
        DFF = 4 * D

        def _layernorm(x, g, b):
            mu = jnp.mean(x, axis=-1, keepdims=True)
            var = jnp.mean(jnp.square(x - mu), axis=-1, keepdims=True)
            return (x - mu) * jax.lax.rsqrt(var + LN_EPS) * g + b
        Bx, Sx, Dx = x.shape
        N = Bx * Sx
        x_flat = x.reshape(N, Dx)
        x_attn = _layernorm(x_flat, ln_g, ln_b) @ attn_w + attn_b + x_flat
        logits = x_attn @ gate_w
        _ = jax.lax.top_k(logits, TOP_K)
        tpe = N // (MICRO_BATCHES * E)
        g = x_attn.reshape(MICRO_BATCHES, E, tpe, Dx)
        h = jax.nn.gelu(jnp.einsum('metd,edf->metf', g, w1) + b1[None, :, None, :], approximate=False)
        y = jnp.einsum('metf,efd->metd', h, w2) + b2[None, :, None, :]
        out = jax.nn.gelu(y @ next_w + next_b, approximate=False)
        return out.reshape(Bx, Sx, Dx)

    def _L3_xattn_ref(query, key, value, mask, wq, wk, wv, w_out):
        import jax, jax.numpy as jnp
        import numpy as np
        N_HEADS = 16
        D_MODEL = 128
        HEAD_D = D_MODEL // N_HEADS
        B, Sq, D = query.shape
        H, hd = (N_HEADS, HEAD_D)

        def split(x):
            return x.reshape(B, -1, H, hd).transpose(0, 2, 1, 3)
        Q = split(jnp.einsum('bsd,ed->bse', query, wq))
        K = split(jnp.einsum('bsd,ed->bse', key, wk))
        V = split(jnp.einsum('bsd,ed->bse', value, wv))
        scores = jnp.einsum('bhqd,bhkd->bhqk', Q, K) / np.sqrt(hd)
        scores = jnp.where(mask[:, None, :, :] == 1, jnp.float32(-1000000000.0), scores)
        attn = jax.nn.softmax(scores, axis=-1)
        out = jnp.einsum('bhqk,bhkd->bhqd', attn, V)
        out = out.transpose(0, 2, 1, 3).reshape(B, Sq, D)
        return jnp.einsum('bsd,ed->bse', out, w_out)

    def _L3_ffn_ref(x, attn_nw, attn_nb, wg, inter_w, inter_b, output_w, output_b, res_inter_w, res_inter_b, res_output_w, res_output_b, res_coef):
        import math
        import jax, jax.numpy as jnp
        import numpy as np
        HIDDEN = 128
        INTER = 512
        EXPERTS = 8
        B, T = (4, 256)
        EPS = 1e-12
        CAP_FACTOR = 1.0
        MIN_CAP = 4

        def layer_norm(x, g, b, eps=EPS):
            m = jnp.mean(x, axis=-1, keepdims=True)
            v = jnp.var(x, axis=-1, keepdims=True)
            return (x - m) * jax.lax.rsqrt(v + eps) * g + b

        def top1_gate(x, wg, capacity):
            logits = x @ wg
            gates = jax.nn.softmax(logits, axis=-1)
            E = wg.shape[-1]
            idx = jnp.argmax(gates, axis=-1)
            mask1 = jax.nn.one_hot(idx, E, dtype=gates.dtype)
            locations = jnp.cumsum(mask1, axis=0) - mask1
            mask1 = mask1 * (locations < capacity).astype(gates.dtype)
            gates1_s = jnp.sum(gates * mask1, axis=-1)
            loc_s = jnp.sum(locations * mask1, axis=-1).astype(jnp.int32)
            loc_oh = jax.nn.one_hot(loc_s, capacity, dtype=gates.dtype)
            combine = gates1_s[:, None, None] * mask1[:, :, None] * loc_oh[:, None, :]
            dispatch = jax.lax.stop_gradient((combine > 0).astype(x.dtype))
            return (combine, dispatch)
        Bx, Tx, M = x.shape
        S = Bx * Tx
        E = wg.shape[-1]
        capacity = max(MIN_CAP, math.ceil(S / E * CAP_FACTOR))
        residual = x.reshape(S, M)
        attn_out = layer_norm(residual, attn_nw, attn_nb)
        combine, dispatch = top1_gate(attn_out, wg, capacity)
        dispatched = jnp.einsum('sec,sm->ecm', dispatch, attn_out)
        h = jax.nn.gelu(jnp.einsum('ecm,emi->eci', dispatched, inter_w) + inter_b[:, None, :], approximate=True)
        expert_out = jnp.einsum('eci,eim->ecm', h, output_w) + output_b[:, None, :]
        moe_out = jnp.einsum('sec,ecm->sm', combine, expert_out)
        rh = jax.nn.gelu(attn_out @ res_inter_w + res_inter_b, approximate=True)
        res_mlp_out = rh @ res_output_w + res_output_b
        coef = jax.nn.softmax(attn_out @ res_coef, axis=-1)
        out = res_mlp_out * coef[:, :1] + moe_out * coef[:, 1:]
        out = out + residual
        return out.reshape(Bx, Tx, M)
    x = x + _L0_xattn_ref(_layernorm(x, axis=-1), ctx_1024, ctx_1024, L0_xattn_Wq, L0_xattn_Wk, L0_xattn_Wv, L0_xattn_out_w, L0_xattn_out_b, L0_xattn_coupling)
    x = x + _L0_ffn_ref(_layernorm(x, axis=-1), L0_ffn_fast_b, L0_ffn_w_fc, L0_ffn_w_proj, L0_ffn_u, L0_ffn_v, L0_ffn_gate)
    x = x + _L1_xattn_ref(_layernorm(x, axis=-1), ctx_1024, mask_Bx1xSxS2_ik0, mask_Bx1xS2_bk0, L1_xattn_Wq, L1_xattn_Wk, L1_xattn_Wv, L1_xattn_Wo, L1_xattn_bo)
    x = x + _L1_ffn_ref(_layernorm(x, axis=-1), L1_ffn_We, L1_ffn_be, L1_ffn_Wg, L1_ffn_bg)
    x = x + _L2_xattn_ref(_layernorm(x, axis=-1), ctx_1024, ctx_1024, L2_xattn_Wq, L2_xattn_Wk, L2_xattn_Wv, L2_xattn_Wp, L2_xattn_bp)
    x = x + _L2_ffn_ref(_layernorm(x, axis=-1), L2_ffn_ln_g, L2_ffn_ln_b, L2_ffn_attn_w, L2_ffn_attn_b, L2_ffn_gate_w, L2_ffn_w1, L2_ffn_b1, L2_ffn_w2, L2_ffn_b2, L2_ffn_next_w, L2_ffn_next_b)
    x = x + _L3_xattn_ref(_layernorm(x, axis=-1), ctx_1024, ctx_1024, mask_BxSxS2_ik1, L3_xattn_wq, L3_xattn_wk, L3_xattn_wv, L3_xattn_w_out)
    x = x + _L3_ffn_ref(_layernorm(x, axis=-1), L3_ffn_attn_nw, L3_ffn_attn_nb, L3_ffn_wg, L3_ffn_inter_w, L3_ffn_inter_b, L3_ffn_output_w, L3_ffn_output_b, L3_ffn_res_inter_w, L3_ffn_res_inter_b, L3_ffn_res_output_w, L3_ffn_res_output_b, L3_ffn_res_coef)
    return x

_drawn_inputs = setup_inputs


def setup_inputs(seed=0):
    import zlib

    import numpy as np

    out = dict(_drawn_inputs(seed))
    spreads = {'L0_xattn_out_b': (0.0, 0.1),
     'L0_xattn_coupling': (0.10000000149011612, 0.6),
     'L2_xattn_bp': (0.0, 0.1),
     'L2_ffn_ln_g': (1.0, 0.2),
     'L2_ffn_ln_b': (0.0, 0.3),
     'L2_ffn_attn_b': (0.0, 0.1),
     'L2_ffn_b1': (0.0, 0.1),
     'L2_ffn_b2': (0.0, 0.1),
     'L2_ffn_next_b': (0.0, 0.1),
     'L3_ffn_attn_nw': (1.0, 0.6),
     'L3_ffn_attn_nb': (0.0, 0.8),
     'L3_ffn_inter_b': (0.0, 0.8),
     'L3_ffn_output_b': (0.0, 0.8),
     'L3_ffn_res_inter_b': (0.0, 0.8),
     'L3_ffn_res_output_b': (0.0, 1.137)}
    factors = {'L0_xattn_Wq': 7.368,
     'L0_xattn_Wk': 6.499,
     'L0_ffn_fast_b': 8.0,
     'L0_ffn_u': 8.0,
     'L0_ffn_v': 7.81,
     'L1_xattn_Wq': 4.216,
     'L1_xattn_Wk': 3.962,
     'L3_ffn_wg': 8.0,
     'L3_ffn_inter_w': 8.0,
     'L3_ffn_output_w': 8.0,
     'L3_ffn_res_inter_w': 4.785,
     'L3_ffn_res_output_w': 4.254,
     'L3_ffn_res_coef': 8.0}
    for name, (base, spread) in spreads.items():
        noise = np.random.default_rng([zlib.crc32(name.encode()), seed]).standard_normal(out[name].shape)
        drawn = base * np.exp(spread * noise) if base else spread * noise
        out[name] = jnp.asarray(drawn.astype(out[name].dtype))
    for name, factor in factors.items():
        out[name] = (out[name] * factor).astype(out[name].dtype)
    return out
```

```python
import math
from contextlib import ExitStack

import numpy as np

import concourse.bass as bass
from concourse import mybir

F32 = mybir.dt.float32
BF16 = mybir.dt.bfloat16
I32 = mybir.dt.int32
U32 = mybir.dt.uint32
U8 = mybir.dt.uint8
ALU = mybir.AluOpType
ACT = mybir.ActivationFunctionType
AX = mybir.AxisListType

P = 128
NB = 4
NT = 4
NTOK = NB * NT * P
CK = 77
NE = 8
FF = 512
NC = FF // P
CAP = NTOK // NE
EPS = 1e-5
EPS3 = 1e-12
MASKED = -float(2.0 ** 100)
TWO_PI = 2.0 * math.pi
ROUND = 1.5 * 2.0 ** 23

H16 = 16
BANK_HEADS = [(0, 6), (6, 12), (12, 16)]
ROWS16 = H16 * CK
CHUNKS16 = [(s, min(P, ROWS16 - s)) for s in range(0, ROWS16, P)]
CHUNKS2 = [(0, CK), (CK, CK)]


def head_pieces(chunks):
    return [(c, h) for c, (s, n) in enumerate(chunks) for h in range(s // CK, (s + n - 1) // CK + 1)]


PIECES16 = head_pieces(CHUNKS16)
PIECES2 = head_pieces(CHUNKS2)
PAD = P
T_UNITS = [(0, 4), (4, 8), (8, 10)]


class Event:

    def __init__(self, nc, ctx, name, credit=0):
        self.sem = ctx.enter_context(nc.semaphore(name))
        self.credit = credit
        self.total = credit
        self.base = {}

    def plan(self, phase, per, reps=1):
        self.base[phase] = (self.total, per)
        self.total += per * reps

    def after(self, phase, j=0, b=0):
        base, per = self.base[phase]
        return b * per + (base + j + 1)


class Bank:
    def __init__(self, nc, ctx, name):
        self.t = ctx.enter_context(nc.psum_tensor(name, [P, 512], F32))
        self.full = Event(nc, ctx, name + "_full")
        self.drained = Event(nc, ctx, name + "_drained", credit=1)

    def plan(self, phase, per, reps=1):
        self.full.plan(phase, per, reps)
        self.drained.plan(phase, per, reps)

    def wait_empty(self, pe, phase, j=0, b=0):
        pe.wait_ge(self.drained.sem, self.drained.after(phase, j - 1, b))

    def wait_full(self, eng, phase, j=0, b=0):
        eng.wait_ge(self.full.sem, self.full.after(phase, j, b))

    def wait_drained(self, eng, phase, j=0, b=0):
        eng.wait_ge(self.drained.sem, self.drained.after(phase, j, b))


def spread(ap, axis, n):
    v = ap.unsqueeze(axis)
    shape = list(v.shape)
    shape[axis] = n
    return v.broadcast_to(shape)


STOP = 8


def four_layers(nc, a, out):
    ctx = ExitStack()
    with ctx:
        def sb(name, shape, dt=F32):
            return ctx.enter_context(nc.sbuf_tensor(name, shape, dt))

        def event(name, credit=0):
            return Event(nc, ctx, name, credit)

        S = [Bank(nc, ctx, f"scores{i}") for i in range(3)]
        TB = [Bank(nc, ctx, f"probsT{i}") for i in range(2)]
        O = Bank(nc, ctx, "mixed")
        X = Bank(nc, ctx, "transposed")
        Y = Bank(nc, ctx, "result")
        BANKS = S + TB + [O, X, Y]

        x = sb("x", [P, NB * NT, P])
        xn = sb("xn", [P, NT, P])
        z = sb("z", [P, NT, P])
        xnT = sb("xnT", [P, NT * P])
        stats = sb("stats", [P, NT, 6])
        mv = sb("mv", [P, NT, 2])
        ve = sb("ve", [P, NT])
        rstd = sb("rstd", [P, NT])
        minus_half = sb("minus_half", [P, NT])
        eps5 = sb("eps5", [P, NT])
        eps12 = sb("eps12", [P, NT])
        prob = sb("prob", [P, NT, ROWS16])
        probT = sb("probT", [P, 10 * P])
        mx = sb("mx", [P, 2, H16])
        rden = sb("rden", [P, 2, H16])
        mix = sb("mix", [P, NT, P])
        mixT = sb("mixT", [P, NT * P])
        hT = sb("hT", [P, NC, 512])
        ident = sb("ident", [P, P])
        identb = sb("identb", [P, P], BF16)
        ones = sb("ones", [1, P])
        blk = sb("blk", [P, H16])
        grid = sb("grid", [P, 10, H16])
        ctx_all = sb("ctx_tok", [P, NB, P])
        ctx_tok = ctx_all[0:CK, :, :]
        ctxT = sb("ctxT", [P, NB, PAD + CK + PAD])
        keysT = ctxT[:, :, PAD:PAD + CK]
        GA = sb("GA", [P, NB, H16, CK])
        GB = sb("GB", [P, NB, H16, CK])
        G2 = sb("G2", [P, NB, 2, CK])
        V03 = sb("V03", [P, NB, len(PIECES16), 9])
        V1 = sb("V1", [P, NB, 10, P])
        V2 = sb("V2", [P, NB, 2, 65])
        mask1 = sb("mask1", [P, NB * NT, CK], BF16)
        mask3 = sb("mask3", [P, NB * NT, CK], BF16)
        mask_raw = sb("mask_raw", [P, NB * NT, CK], I32)
        src_raw = sb("src_raw", [P, NB, CK], U8)
        src_bias = sb("src_bias", [P, NB, CK], BF16)
        causal = sb("causal", [P, CK])
        w0 = sb("w0", [P, 4, P])
        w3 = sb("w3", [P, 4, P])
        w2 = sb("w2", [P, 4, P])
        wT = sb("wT", [P, 3, P])
        out_wT = sb("out_wT", [P, 2, P])
        rows = sb("rows", [1, 6, P])
        head_bias = sb("head_bias", [P, H16])
        wfc = sb("wfc", [P, NC, P])
        wpr = sb("wpr", [P, NC * P])
        wt1 = sb("wt1", [P, NC, P])
        wt2 = sb("wt2", [P, NC, P])
        wfcT = sb("wfcT", [P, NC * P])
        wprT = sb("wprT", [P, NC, P])
        lr = sb("lr", [P, NC, 16])
        lrT = sb("lrT", [16, FF])
        fbT = sb("fbT", [16, 16])
        vlow = sb("vlow", [16, P])
        gate = sb("gate", [16, 1])
        bv = sb("bv", [16, P])
        wsc = sb("wsc", [P, 2, 16])
        we = sb("we", [P, NE, P])
        be = sb("be", [NE, P])
        wg1 = sb("wg1", [P, NE])
        bg1 = sb("bg1", [P, NE])
        attn_w = sb("attn_w", [P, P])
        next_w = sb("next_w", [P, P])
        cols2 = sb("cols2", [P, 3])
        b1c = sb("b1c", [P, NE, NC])
        b2c = sb("b2c", [P, NE])
        big = sb("big", [P, 2, NE * FF])
        lg = sb("lg", [P, NT, 16])
        ex = sb("ex", [P, NT, 16])
        iota8 = sb("iota8", [P, NE])
        ph = sb("ph", [H16, 24])
        phw = sb("phw", [H16, H16 + 2])
        dg = sb("dg", [H16, H16])
        ones16 = sb("ones16", [H16, P])
        gsel = sb("gsel", [P, NT, NE])
        gtmp = sb("gtmp", [P, NT, NE])
        top8 = sb("top8", [P, NT, 8])
        idx8 = sb("idx8", [P, NT, 8], U32)
        idxf = sb("idxf", [P, NT, 8])
        gT = sb("gT", [NE, NT * P])
        gs = sb("gs", [P, 4, NT])
        a2 = sb("a2", [P, 2, P])
        xaT = wt1[:, :, :].rearrange("p c d -> p (c d)")
        gout = wt2[:, :, :].rearrange("p c d -> p (c d)")

        wgc = sb("wgc", [P, NE + 2])
        cols3 = sb("cols3", [P, 2 + NC])
        route = ctx_all[:, :, :].rearrange("p b d -> p (b d)")
        earlier = route[:, 0:64].bitcast(BF16)
        onesb = route[:, 64:128].bitcast(BF16)
        chosen = route[:, 128:192].bitcast(BF16).rearrange("p (g e) -> p g e", e=NE)
        expert_of, weight_of, coef0, place, kept, slot = (route[:, 192 + 16 * i:208 + 16 * i] for i in range(6))
        slot_put = route[:, 288:304].bitcast(U32)
        slot_get = route[:, 304:320].bitcast(U32)
        counted = route[:, 320:448].rearrange("p (g e) -> p g e", e=NE)
        v1f = V1[:, :, :, :].rearrange("p b c d -> p (b c d)")
        gbf = GB[:, :, :, :].rearrange("p b h k -> p (b h k)")
        normed = v1f[:, 0:2048].rearrange("p (g d) -> p g d", d=P)
        expert_out = v1f[:, 2048:4096].rearrange("p (g d) -> p g d", d=P)
        nw_all, nb_all = v1f[:, 4096:4224], v1f[:, 4224:4352]
        sent = gbf[:, 0:2048].rearrange("p (g d) -> p g d", d=P)
        sentT = gbf[:, 2048:4096]
        got = prob[:, :, :].rearrange("p t n -> p (t n)")[:, 0:2048].rearrange("p (g d) -> p g d", d=P)
        res_w1 = w0[:, :, :].rearrange("p c d -> p (c d)")
        res_w2 = w2
        out_b_row = we[0:1, :, :]
        dispatched_d = nc.dram_tensor("dispatched", [NTOK, P], F32, kind="Internal").ap()
        expert_out_d = nc.dram_tensor("expert_out", [NTOK, P], F32, kind="Internal").ap()

        w1q = big[:, 0, 0:1024].rearrange("p (c d) -> p c d", c=8)
        w1k = big[:, 0, 1024:2048].rearrange("p (c d) -> p c d", c=8)
        w1v = big[:, 0, 2048:3072].rearrange("p (c d) -> p c d", c=8)
        w1o = big[:, 0, 3072:4096]
        w1oT = big[:, 1, 0:1024].rearrange("p (c d) -> p c d", c=8)
        head_mat = big[:, 1, 1024:3072].rearrange("p (q c d) -> p q c d", q=2, c=8)

        loaded = {}
        for n in ("x", "const", "w0", "ctx", "mask1", "mask3", "ffn0", "attn1", "ffn1", "attn2", "ffn2", "attn3", "ffn3"):
            loaded[n] = event("loaded_" + n)
        made = event("constants_made")
        pool_step = event("pool_step")
        stats_ready = event("stats_ready")
        passed = event("passed")
        pool_passed = event("pool_passed")
        mv_ready = event("mv_ready")
        ve_ready = event("ve_ready")
        rstd_ready = event("rstd_ready")
        xn_ready = event("xn_ready")
        z_ready = event("z_ready")
        max_ready = event("max_ready")
        exp_ready = event("exp_ready")
        den_ready = event("den_ready")
        scaled_ready = event("scaled_ready")
        square_ready = event("square_ready")
        dve_prep = event("dve_prep")
        act_prep = event("act_prep")
        out_done = event("out_done")
        x_done = event("x_done")
        gelu_ready = event("gelu_ready")
        gate_step = event("gate_step")
        gate_exp = event("gate_exp")
        xa_ready = event("xa_ready")
        chain = event("chain")
        logits_in = event("logits_in")
        mask_made = event("mask_made")
        zeroed = event("dispatched_zeroed")
        zeros_made = event("zeros_made")
        base_added = event("base_added")
        normed_ready = event("normed_ready")
        res_step = event("res_step")
        res_exp = event("res_exp")
        route_made = event("route_made")
        route_step = event("route_step")
        scattered = event("scattered")
        sent_loaded = event("sent_loaded")
        stored = event("expert_out_stored")
        gathered = [event(f"gathered{b}") for b in range(NB)]
        tern = event("tern")

        loads = {n: 0 for n in loaded}

        def load(eng, group, dst, src, **kw):
            loads[group] += 16
            eng.dma_start(dst, src, **kw).then_inc(loaded[group].sem, 16)

        ATT = {
            "L0x": dict(H=16, G=GA, V=V03, dv=8, scale=8 ** -0.5, mask=None, row=0, wout=w0[:, 3, :], fold=False, bias=True),
            "L1x": dict(H=16, G=GB, V=V1, dv=P, scale=64 ** -0.5, mask=mask1, row=1, wout=None, fold=True, bias=False),
            "L2x": dict(H=2, G=G2, V=V2, dv=64, scale=64 ** -0.5, mask="causal", row=2, wout=out_wT[:, 0, :], fold=False, bias=False),
            "L3x": dict(H=16, G=GA, V=V03, dv=8, scale=8 ** -0.5, mask=mask3, row=None, wout=out_wT[:, 1, :], fold=False, bias=False),
        }
        LAYERS = ["L0x", "L0f", "L1x", "L1f", "L2x", "L2f", "L3x", "L3f"][:STOP]

        def plan_norm(L):
            for e in (stats_ready, mv_ready, ve_ready, rstd_ready):
                e.plan(L, 2 if L in ("L2f", "L3f") else 1, NB)
            xn_ready.plan(L, 1, NB)
            if L in ("L2f", "L3f"):
                z_ready.plan(L, 1, NB)

        def plan_attention(L):
            c = ATT[L]
            plan_norm(L)
            if c["H"] == 16:
                for bk in S:
                    bk.plan(L, NT, NB)
                TB[0].plan(L, 2 * NT, NB)
                TB[1].plan(L, NT, NB)
            else:
                S[0].plan(L, 2, NB); S[1].plan(L, 2, NB)
                TB[0].plan(L, 2, NB); TB[1].plan(L, 2, NB)
            max_ready.plan(L, 3 if c["bias"] else 1, NB * NT)
            exp_ready.plan(L, NT, NB)
            den_ready.plan(L, 2 if c["fold"] else 1, NB * NT)
            if c["fold"]:
                scaled_ready.plan(L, NT, NB)
                O.plan(L, 2, NB); Y.plan(L, 2, NB); X.plan(L, 1, NB)
            else:
                O.plan(L, NT + 1, NB); Y.plan(L, 1, NB); X.plan(L, 1, NB)
            x_done.plan(L, 1, NB)

        def prev_of(L, b):
            i = LAYERS.index(L)
            return None if i == 0 else LAYERS[i - 1]

        INNER = {"L2f", "L3f"}

        def ln_stats_dve(dve, L, b, j=0):
            if j == 0:
                p = prev_of(L, b)
                if p is None:
                    dve.wait_ge(loaded["x"].sem, 16)
                else:
                    dve.wait_ge(x_done.sem, x_done.after(p, 0, b))
            else:
                dve.wait_ge(xn_ready.sem, xn_ready.after(L, 0, b))
            for t in range(NT):
                last = dve.bn_stats(stats[:, t, :], x[:, b * NT + t, :] if j == 0 else xn[:, t, :])
            last.then_inc(stats_ready.sem, 1)
            dve.wait_ge(stats_ready.sem, stats_ready.after(L, j, b))
            dve.sem_inc(passed.sem, 1)
            for t in range(NT):
                last = dve.bn_aggr(mv[:, t, :], stats[:, t, :])
            last.then_inc(mv_ready.sem, 1)

        def ln_rstd_pool(pool, L, b, j=0):
            eps = eps12 if (L == "L3f" and j == 1) else eps5
            pool.wait_ge(mv_ready.sem, mv_ready.after(L, j, b))
            pool.tensor_tensor(ve[:, :], mv[:, :, 1], eps[:, :], ALU.add).then_inc(ve_ready.sem, 1)
            pool.wait_ge(ve_ready.sem, ve_ready.after(L, j, b))
            pool.tensor_tensor(rstd[:, :], ve[:, :], minus_half[:, :], ALU.pow).then_inc(rstd_ready.sem, 1)

        def ln_apply_dve(dve, L, b, j=0):
            dve.wait_ge(rstd_ready.sem, rstd_ready.after(L, j, b))
            if j == 0:
                wait_xn_free(dve, L, b)
            src = (lambda t: x[:, b * NT + t, :]) if j == 0 else (lambda t: xn[:, t, :])
            dst, ev = (xn, xn_ready) if j == 0 else (z, z_ready)
            for t in range(NT):
                last = dve.tensor_scalar(dst[:, t, :], src(t), mv[:, t, 0:1], rstd[:, t:t + 1],
                                         ALU.subtract, ALU.mult)
            last.then_inc(ev.sem, 1)

        def wait_xn_free(dve, L, b):
            xt = XT_UNIT[L]
            if isinstance(b, int) and b == 0:
                i = LAYERS.index(L)
                if i:
                    q = LAYERS[i - 1]
                    X.wait_full(dve, q, XT_UNIT[q], NB - 1)
            else:
                X.wait_full(dve, L, xt, b - 1)

        XT_UNIT = {L: 0 for L in LAYERS}

        def front_dve(dve, L, b):
            for j in range(2 if L in INNER else 1):
                ln_stats_dve(dve, L, b, j)
                ln_apply_dve(dve, L, b, j)

        def front_pool(pool, L, b):
            for j in range(2 if L in INNER else 1):
                ln_rstd_pool(pool, L, b, j)

        def front_pe(pe, L, b):
            pe.wait_ge(xn_ready.sem, xn_ready.after(L, 0, b))
            X.wait_empty(pe, L, XT_UNIT[L], b)
            for t in range(NT):
                last = pe.transpose(X.t[:, t * P:(t + 1) * P], xn[:, t, :], ident[:, :])
            last.then_inc(X.full.sem, 1)

        def front_act(act, L, b, free=None):
            X.wait_full(act, L, XT_UNIT[L], b)
            if free is not None:
                free(act)
            act.activation(xnT[:, :], X.t[:, :], ACT.Copy).then_inc(X.drained.sem, 1)

        def scores_pe(pe, L, b, t):
            c = ATT[L]
            if t == 0:
                X.wait_drained(pe, L, 0, b)
            lhs = xnT[:, t * P:(t + 1) * P]
            if c["H"] == 16:
                for j, (h0, h1) in enumerate(BANK_HEADS):
                    n = (h1 - h0) * CK
                    S[j].wait_empty(pe, L, t, b)
                    o = S[j].t[:, 0:n]
                    if c["mask"] is not None:
                        pe.matmul(o, identb[:, :], spread(c["mask"][:, b * NT + t, :], 1, h1 - h0),
                                  start=True, stop=False)
                    pe.matmul(o, lhs, c["G"][:, b, h0:h1, :], start=c["mask"] is None, stop=True)\
                        .then_inc(S[j].full.sem, 1)
            else:
                bk = S[t % 2]
                bk.wait_empty(pe, L, t // 2, b)
                o = bk.t[:, 0:2 * CK]
                if t == 0:
                    pe.matmul(o, ident[:, :], spread(causal[:, :], 1, 2), start=True, stop=False)
                pe.matmul(o, lhs, c["G"][:, b, :, :], start=t != 0, stop=True).then_inc(bk.full.sem, 1)

        def shift_dve(dve, L, b, t):
            c = ATT[L]
            k = 3 if c["bias"] else 1
            H = c["H"]
            m = mx[:, t % 2, 0:H]
            parts = [(S[j], h0, h1) for j, (h0, h1) in enumerate(BANK_HEADS)] if H == 16 else [(S[t % 2], 0, 2)]
            unit = t if H == 16 else t // 2
            for bk, h0, h1 in parts:
                bk.wait_full(dve, L, unit, b)
                last = dve.tensor_reduce(m[:, h0:h1], bk.t[:, 0:(h1 - h0) * CK].rearrange("p (h k) -> p h k", k=CK),
                                         AX.X, ALU.max)
            last.then_inc(max_ready.sem, 1)
            dve.wait_ge(max_ready.sem, max_ready.after(L, k * t, 0) + b * (k * NT))
            if c["bias"]:
                dve.tensor_tensor(m, m, head_bias[:, :], ALU.add).then_inc(max_ready.sem, 1)
                dve.wait_ge(max_ready.sem, max_ready.after(L, k * t + 1, 0) + b * (k * NT))
                dve.tensor_tensor(m, m, head_bias[:, :], ALU.subtract).then_inc(max_ready.sem, 1)
                dve.wait_ge(max_ready.sem, max_ready.after(L, k * t + 2, 0) + b * (k * NT))
            for bk, h0, h1 in parts:
                dve.tensor_tensor(prob[:, t, h0 * CK:h1 * CK].rearrange("p (h k) -> p h k", k=CK),
                                  bk.t[:, 0:(h1 - h0) * CK].rearrange("p (h k) -> p h k", k=CK),
                                  spread(m[:, h0:h1], 2, CK), ALU.subtract).then_inc(bk.drained.sem, 1)

        def exp_act(act, L, b, t):
            c = ATT[L]
            if c["H"] == 16:
                S[2].wait_drained(act, L, t, b)
            else:
                S[t % 2].wait_drained(act, L, t // 2, b)
            n = c["H"] * CK
            act.activation(prob[:, t, 0:n], prob[:, t, 0:n], ACT.Exp, scale=c["scale"]).then_inc(exp_ready.sem, 1)

        def normalise_dve(dve, L, b, t):
            dve.wait_ge(exp_ready.sem, exp_ready.after(L, t, b))
            r = rden[:, t % 2, :]
            dve.tensor_reduce(r, prob[:, t, :].rearrange("p (h k) -> p h k", k=CK), AX.X, ALU.add)\
                .then_inc(den_ready.sem, 1)
            dve.wait_ge(den_ready.sem, den_ready.after(L, 2 * t, 0) + b * (2 * NT))
            dve.reciprocal(r, r).then_inc(den_ready.sem, 1)

        def normalise_pool(pool, L, b, t):
            pool.wait_ge(den_ready.sem, den_ready.after(L, 2 * t + 1, 0) + b * (2 * NT))
            v = prob[:, t, :].rearrange("p (h k) -> p h k", k=CK)
            pool.tensor_tensor(v, v, spread(rden[:, t % 2, :], 2, CK), ALU.mult).then_inc(scaled_ready.sem, 1)

        def t_units(L, t):
            if ATT[L]["H"] == 16:
                return [(TB[0], 2 * t, 0, 4), (TB[1], t, 4, 8), (TB[0], 2 * t + 1, 8, 10)]
            return [(TB[t % 2], t // 2, 0, 2)]

        def mix_pe(pe, L, b, t):
            c = ATT[L]
            chunks = CHUNKS16 if c["H"] == 16 else CHUNKS2
            pieces = PIECES16 if c["H"] == 16 else PIECES2
            if c["fold"]:
                pe.wait_ge(scaled_ready.sem, scaled_ready.after(L, t, b))
            else:
                pe.wait_ge(exp_ready.sem, exp_ready.after(L, t, b))
            for bk, u, c0, c1 in t_units(L, t):
                bk.wait_empty(pe, L, u, b)
                for i in range(c0, c1):
                    s, n = chunks[i]
                    last = pe.transpose(bk.t[0:n, (i - c0) * P:(i - c0 + 1) * P], prob[:, t, s:s + n], ident[:, :])
                last.then_inc(bk.full.sem, 1)
            first = True
            if c["fold"]:
                dst, u = (O, Y)[t % 2], t // 2
                dst.wait_empty(pe, L, u, b)
                pe.matmul(dst.t[:, 0:P], ones[0:1, :], rows[0:1, c["row"], :], start=True, stop=False)
                for bk, tu, c0, c1 in t_units(L, t):
                    bk.wait_drained(pe, L, tu, b)
                    for i in range(c0, c1):
                        n = chunks[i][1]
                        last = pe.matmul(dst.t[:, 0:P], probT[0:n, i * P:(i + 1) * P], c["V"][0:n, b, i, :],
                                         start=False, stop=i == len(chunks) - 1)
                last.then_inc(dst.full.sem, 1)
            else:
                w = c["dv"] + 1
                O.wait_empty(pe, L, t, b)
                for bk, tu, c0, c1 in t_units(L, t):
                    bk.wait_drained(pe, L, tu, b)
                    for i in range(c0, c1):
                        n = chunks[i][1]
                        q = [k for k, (cc, _) in enumerate(pieces) if cc == i]
                        h0 = pieces[q[0]][1]
                        last = pe.matmul(O.t[:, h0 * w:(h0 + len(q)) * w], probT[0:n, i * P:(i + 1) * P],
                                         c["V"][0:n, b, q[0]:q[0] + len(q), :],
                                         start=first, stop=i == len(chunks) - 1, skip_group_check=True)
                        first = False
                last.then_inc(O.full.sem, 1)

        def probT_act(act, L, b, t):
            c = ATT[L]
            for bk, u, c0, c1 in t_units(L, t):
                n = P if c["H"] == 16 else CK
                bk.wait_full(act, L, u, b)
                if c1 == 10:
                    r = CHUNKS16[9][1]
                    act.activation(probT[:, c0 * P:(c0 + 1) * P], bk.t[:, 0:P], ACT.Copy)
                    act.activation(probT[0:r, (c0 + 1) * P:c1 * P], bk.t[0:r, P:2 * P], ACT.Copy)\
                        .then_inc(bk.drained.sem, 1)
                else:
                    act.activation(probT[0:n, c0 * P:c1 * P], bk.t[0:n, 0:(c1 - c0) * P], ACT.Copy)\
                        .then_inc(bk.drained.sem, 1)

        def mixed_dve(dve, L, b, t):
            c = ATT[L]
            if c["fold"]:
                bk, u = (O, Y)[t % 2], t // 2
                bk.wait_full(dve, L, u, b)
                ins = dve.tensor_tensor(x[:, b * NT + t, :], x[:, b * NT + t, :], bk.t[:, 0:P], ALU.add)
                ins.then_inc(bk.drained.sem, 1)
                return
            H, dv = c["H"], c["dv"]
            O.wait_full(dve, L, t, b)
            v = O.t[:, 0:H * (dv + 1)].rearrange("p (h e) -> p h e", e=dv + 1)
            r = rden[:, t % 2, 0:H]
            dve.reciprocal(r, v[:, :, dv]).then_inc(den_ready.sem, 1)
            dve.wait_ge(den_ready.sem, den_ready.after(L, t, 0) + b * NT)
            dve.tensor_tensor(mix[:, t, :].rearrange("p (h e) -> p h e", e=dv), v[:, :, 0:dv],
                              spread(r, 2, dv), ALU.mult).then_inc(O.drained.sem, 1)

        def tail_pe(pe, L, b):
            c = ATT[L]
            if c["fold"]:
                return
            O.wait_drained(pe, L, NT - 1, b)
            O.wait_empty(pe, L, NT, b)
            for t in range(NT):
                last = pe.transpose(O.t[:, t * P:(t + 1) * P], mix[:, t, :], ident[:, :])
            last.then_inc(O.full.sem, 1)
            Y.wait_empty(pe, L, 0, b)
            if c["row"] is not None:
                pe.matmul(Y.t[:, :], ones[0:1, :], spread(rows[0:1, c["row"], :], 1, NT), start=True, stop=False,
                          skip_group_check=True)
            O.wait_drained(pe, L, NT, b)
            for t in range(NT):
                last = pe.matmul(Y.t[:, t * P:(t + 1) * P], mixT[:, t * P:(t + 1) * P], c["wout"],
                                 start=c["row"] is None and t == 0, stop=t == NT - 1, skip_group_check=True)
            last.then_inc(Y.full.sem, 1)

        def tail_act(act, L, b):
            if ATT[L]["fold"]:
                return
            O.wait_full(act, L, NT, b)
            act.activation(mixT[:, :], O.t[:, :], ACT.Copy).then_inc(O.drained.sem, 1)

        def tail_dve(dve, L, b):
            if ATT[L]["fold"]:
                dve.wait_ge(Y.drained.sem, Y.drained.after(L, 1, b))
                dve.wait_ge(O.drained.sem, O.drained.after(L, 1, b))
                dve.sem_inc(x_done.sem, 1)
                return
            Y.wait_full(dve, L, 0, b)
            xb = x[:, bass.ds(b * NT, NT), :] if not isinstance(b, int) else x[:, b * NT:(b + 1) * NT, :]
            dve.tensor_tensor(xb, xb, Y.t[:, :].rearrange("p (t d) -> p t d", t=NT), ALU.add)\
                .then_inc(Y.drained.sem, 1)
            dve.wait_ge(Y.drained.sem, Y.drained.after(L, 0, b))
            dve.sem_inc(x_done.sem, 1)

        def run_attention(eng, name, L, after_last=None):
            def front(b):
                {"pe": front_pe, "dve": front_dve, "act": front_act, "pool": front_pool}[name](eng, L, b)

            def head(b, t):
                if name == "pe":
                    scores_pe(eng, L, b, t)
                elif name == "dve":
                    shift_dve(eng, L, b, t)
                elif name == "act":
                    exp_act(eng, L, b, t)

            def back(b, t):
                if name == "pe":
                    mix_pe(eng, L, b, t)
                elif name == "act":
                    probT_act(eng, L, b, t)
                elif name == "dve":
                    mixed_dve(eng, L, b, t)

            def norm(b, t):
                if ATT[L]["fold"]:
                    if name == "dve":
                        normalise_dve(eng, L, b, t)
                    elif name == "pool":
                        normalise_pool(eng, L, b, t)

            def body(b, last):
                for t in range(NT):
                    if t < 2:
                        steps = [lambda: head(b, t + 2)]
                    elif not last:
                        steps = [lambda: head(b + 1, t - 2)]
                    else:
                        steps = []
                    if t == 1 and not last and name in ("act",):
                        head(b, 3)
                        front(b + 1)
                        back(b, t)
                        continue
                    if t == 1 and not last and name == "pe":
                        head(b, 3)
                        front(b + 1)
                        norm(b, t)
                        back(b, t)
                        continue
                    if t == 0 and not last and name in ("dve", "pool"):
                        front(b + 1)
                    if name == "act":
                        back(b, t)
                        for s in steps:
                            s()
                    else:
                        norm(b, t)
                        for s in steps:
                            s()
                        back(b, t)
                if name == "pe":
                    tail_pe(eng, L, b)
                elif name == "act":
                    tail_act(eng, L, b)
                elif name == "dve":
                    tail_dve(eng, L, b)

            front(0)
            head(0, 0)
            head(0, 1)
            with eng.Fori(0, NB - 1) as b:
                body(b, False)
            body(NB - 1, True)

        WINDOW = lambda b, c, h, n: ctxT[:, b, PAD + P * c - CK * h:PAD + P * c - CK * h + n]

        def plan_prep03(L):
            X.plan("prep" + L, 2)
            O.plan("prep" + L, 1)
            Y.plan("prep" + L, 1)
            for bk in S:
                bk.plan("prep" + L, NB)
            TB[0].plan("prep" + L, 2)
            TB[1].plan("prep" + L, 2)
            dve_prep.plan("prep" + L, NB)

        def prep03_pe(pe, L):
            ph_ = "prep" + L
            if L == "L0x":
                pe.wait_ge(made.sem, MADE)
                pe.wait_ge(loaded["ctx"].sem, 16)
                X.wait_empty(pe, ph_, 0)
                for b in range(NB):
                    last = pe.transpose(X.t[:, b * CK:(b + 1) * CK], ctx_tok[:, b, :], ident[0:CK, 0:CK])
                last.then_inc(X.full.sem, 1)
                pe.wait_ge(loaded["w0"].sem, LOADS["w0"])
                O.wait_empty(pe, ph_, 0)
                pe.transpose(O.t[:, 0:P], w0[:, 0, :], ident[:, :]).then_inc(O.full.sem, 1)
                wk, wq, wv = w0[:, 1, :], wT[:, 0, :], w0[:, 2, :]
                X.wait_empty(pe, ph_, 1)
                pe.transpose(X.t[:, 0:P], w0[:, 0, :], ident[:, :]).then_inc(X.full.sem, 1)
            else:
                pe.wait_ge(loaded["attn3"].sem, LOADS["attn3"])
                X.wait_empty(pe, ph_, 0)
                for i in range(3):
                    last = pe.transpose(X.t[:, i * P:(i + 1) * P], w3[:, 1 + i, :], ident[:, :])
                last.then_inc(X.full.sem, 1)
                O.wait_empty(pe, ph_, 0)
                pe.transpose(O.t[:, 0:P], w3[:, 0, :], ident[:, :]).then_inc(O.full.sem, 1)
                X.wait_empty(pe, ph_, 1)
                pe.transpose(X.t[:, 0:P], w3[:, 0, :], ident[:, :]).then_inc(X.full.sem, 1)
                wk, wq, wv = wT[:, 1, :], w3[:, 0, :], wT[:, 2, :]
            Y.wait_empty(pe, ph_, 0)
            X.wait_drained(pe, ph_, 0)
            pe.matmul(Y.t[:, 0:NB * CK], wk, keysT, start=True, stop=True).then_inc(Y.full.sem, 1)
            for b in range(NB):
                bk = TB[b % 2]
                bk.wait_empty(pe, ph_, b // 2)
                for i, (c, h) in enumerate(PIECES16):
                    n = CHUNKS16[c][1]
                    last = pe.matmul(bk.t[0:n, i * 8:(i + 1) * 8], WINDOW(b, c, h, n), wv[:, h * 8:(h + 1) * 8],
                                     start=True, stop=True)
                last.then_inc(bk.full.sem, 1)
            O.wait_drained(pe, ph_, 0)
            for b in range(NB):
                pe.wait_ge(dve_prep.sem, dve_prep.after(ph_, b))
                for j, (h0, h1) in enumerate(BANK_HEADS):
                    S[j].wait_empty(pe, ph_, b)
                    pe.matmul(S[j].t[:, 0:(h1 - h0) * CK], wq, prob[:, b, h0 * CK:h1 * CK], start=True, stop=True)\
                        .then_inc(S[j].full.sem, 1)

        def prep03_act(act, L):
            ph_ = "prep" + L
            if L == "L0x":
                act.wait_ge(made.sem, MADE)
                X.wait_full(act, ph_, 0)
                act.activation(keysT, X.t[:, 0:NB * CK].rearrange("p (b k) -> p b k", b=NB), ACT.Copy)\
                    .then_inc(X.drained.sem, 1)
            else:
                X.wait_full(act, ph_, 0)
                act.activation(wT[:, 1:3, :], X.t[:, 0:2 * P].rearrange("p (i d) -> p i d", i=2), ACT.Copy)
                act.activation(out_wT[:, 1, :], X.t[:, 2 * P:3 * P], ACT.Copy).then_inc(X.drained.sem, 1)
            O.wait_full(act, ph_, 0)
            act.activation(wT[:, 0, :], O.t[:, 0:P], ACT.Copy).then_inc(O.drained.sem, 1)
            X.wait_full(act, ph_, 1)
            act.activation(z[:, 0, :], X.t[:, 0:P], ACT.Copy).then_inc(X.drained.sem, 1)
            for b in range(NB):
                for j, (h0, h1) in enumerate(BANK_HEADS):
                    S[j].wait_full(act, ph_, b)
                    act.activation(GA[:, b, h0:h1, :], S[j].t[:, 0:(h1 - h0) * CK].rearrange("p (h k) -> p h k", k=CK),
                                   ACT.Copy).then_inc(S[j].drained.sem, 1)

        def prep03_dve(dve, L):
            ph_ = "prep" + L
            if L == "L0x":
                dve.wait_ge(made.sem, MADE)
            Y.wait_full(dve, ph_, 0)
            for b in range(NB):
                dve.tensor_tensor(prob[:, b, :].rearrange("p (h k) -> p h k", k=CK),
                                  spread(Y.t[:, b * CK:(b + 1) * CK], 1, H16), spread(blk[:, :], 2, CK), ALU.mult)\
                    .then_inc(dve_prep.sem, 1)
            dve.wait_ge(dve_prep.sem, dve_prep.after(ph_, NB - 1))
            dve.sem_inc(Y.drained.sem, 1)
            for b in range(NB):
                bk = TB[b % 2]
                bk.wait_full(dve, ph_, b // 2)
                n_full = sum(1 for c, h in PIECES16 if CHUNKS16[c][1] == P)
                r = CHUNKS16[9][1]
                dve.tensor_copy(V03[:, b, 0:n_full, 0:8], bk.t[:, 0:8 * n_full].rearrange("p (i e) -> p i e", e=8))
                dve.tensor_copy(V03[0:r, b, n_full:, 0:8],
                                bk.t[0:r, 8 * n_full:8 * len(PIECES16)].rearrange("p (i e) -> p i e", e=8))\
                    .then_inc(bk.drained.sem, 1)

        def plan_prep1():
            L = "prepL1x"
            for bk in (S[1], S[2], TB[0]):
                bk.plan(L, 2)
            S[0].plan(L, 2 + NB)
            X.plan(L, 1 + NB)
            Y.plan(L, 1 + NB)
            TB[1].plan(L, 8)
            O.plan(L, 8)

        def pair_banks(p):
            return (S[0], S[2]) if p < 4 else (S[1], TB[0])

        def prep1_pe(pe):
            L = "prepL1x"
            pe.wait_ge(loaded["attn1"].sem, LOADS["attn1"])

            def pairs(lhs, rhs, unit):
                for p in range(8):
                    for par, bk in enumerate(pair_banks(p)):
                        if p % 4 == 0:
                            bk.wait_empty(pe, L, unit)
                        r = slice(64 * par, 64 * par + 64)
                        last = pe.matmul(bk.t[:, (p % 4) * P:(p % 4 + 1) * P], lhs[r, p, :], rhs[r, p, :],
                                         start=True, stop=True)
                        if p % 4 == 3:
                            last.then_inc(bk.full.sem, 1)

            pairs(w1k, w1q, 0)
            for i, bk in enumerate((X, Y)):
                bk.wait_empty(pe, L, 0)
                for c in range(4):
                    last = pe.transpose(bk.t[:, c * P:(c + 1) * P], w1o[:, (4 * i + c) * P:(4 * i + c + 1) * P],
                                        ident[:, :])
                last.then_inc(bk.full.sem, 1)
            for bk in (S[0], S[1], S[2], TB[0]):
                bk.wait_drained(pe, L, 0)
            for h in range(H16):
                bk = (TB[1], O)[h % 2]
                bk.wait_empty(pe, L, h // 2)
                pe.matmul(bk.t[:, 0:NB * CK], head_mat[:, h % 2, h // 2, :], keysT, start=True, stop=True)\
                    .then_inc(bk.full.sem, 1)
            X.wait_drained(pe, L, 0)
            Y.wait_drained(pe, L, 0)
            pairs(w1v, w1oT, 1)
            for bk in (S[0], S[1], S[2], TB[0]):
                bk.wait_drained(pe, L, 1)
            for b in range(NB):
                for bk, u, c0, c1 in ((X, 1 + b, 0, 4), (Y, 1 + b, 4, 8), (S[0], 2 + b, 8, 10)):
                    bk.wait_empty(pe, L, u)
                    for c in range(c0, c1):
                        hs = [h for cc, h in PIECES16 if cc == c]
                        n = CHUNKS16[c][1]
                        for h in hs:
                            last = pe.matmul(bk.t[0:n, (c - c0) * P:(c - c0 + 1) * P], WINDOW(b, c, h, n),
                                             head_mat[:, h % 2, h // 2, :], start=h == hs[0], stop=h == hs[-1])
                    last.then_inc(bk.full.sem, 1)

        def prep1_act(act):
            L = "prepL1x"

            def halves(unit):
                for i in range(2):
                    S[i].wait_full(act, L, unit)
                    act.activation(head_mat[:, 0, 4 * i:4 * i + 4, :], S[i].t[:, :].rearrange("p (c d) -> p c d", c=4),
                                   ACT.Copy).then_inc(S[i].drained.sem, 1)

            halves(0)
            for i, bk in enumerate((X, Y)):
                bk.wait_full(act, L, 0)
                act.activation(w1oT[:, 4 * i:4 * i + 4, :], bk.t[:, :].rearrange("p (c d) -> p c d", c=4), ACT.Copy)\
                    .then_inc(bk.drained.sem, 1)
            for h in range(1, H16, 2):
                O.wait_full(act, L, h // 2)
                act.activation(GB[:, :, h, :], O.t[:, 0:NB * CK].rearrange("p (b k) -> p b k", b=NB), ACT.Copy)\
                    .then_inc(O.drained.sem, 1)
            halves(1)
            r = CHUNKS16[9][1]
            for b in range(NB):
                X.wait_full(act, L, 1 + b)
                act.activation(V1[:, b, 0:4, :], X.t[:, :].rearrange("p (c d) -> p c d", c=4), ACT.Copy)\
                    .then_inc(X.drained.sem, 1)
                S[0].wait_full(act, L, 2 + b)
                act.activation(V1[:, b, 8, :], S[0].t[:, 0:P], ACT.Copy)
                act.activation(V1[0:r, b, 9, :], S[0].t[0:r, P:2 * P], ACT.Copy).then_inc(S[0].drained.sem, 1)

        def prep1_dve(dve):
            L = "prepL1x"
            dve.wait_ge(loaded["mask1"].sem, LOADS["mask1"])
            dve.tensor_scalar(mask1[:, :, :], mask_raw[:, :, :], 0.0, MASKED, ALU.is_equal, ALU.mult)\
                .then_inc(mask_made.sem, 1)
            dve.tensor_scalar(src_bias[:, :, :], src_raw[:, :, :], 0.0, MASKED, ALU.is_equal, ALU.mult)\
                .then_inc(mask_made.sem, 1)
            dve.wait_ge(mask_made.sem, 2)
            for b in range(NB):
                v = mask1[:, b * NT:(b + 1) * NT, :]
                dve.tensor_tensor(v, v, spread(src_bias[:, b, :], 1, NT), ALU.min).then_inc(mask_made.sem, 1)

            def halves(unit):
                for i, bk in enumerate((S[2], TB[0])):
                    bk.wait_full(dve, L, unit)
                    dve.tensor_copy(head_mat[:, 1, 4 * i:4 * i + 4, :], bk.t[:, :].rearrange("p (c d) -> p c d", c=4))\
                        .then_inc(bk.drained.sem, 1)

            halves(0)
            for h in range(0, H16, 2):
                TB[1].wait_full(dve, L, h // 2)
                dve.tensor_copy(GB[:, :, h, :], TB[1].t[:, 0:NB * CK].rearrange("p (b k) -> p b k", b=NB))\
                    .then_inc(TB[1].drained.sem, 1)
            halves(1)
            for b in range(NB):
                Y.wait_full(dve, L, 1 + b)
                dve.tensor_copy(V1[:, b, 4:8, :], Y.t[:, :].rearrange("p (c d) -> p c d", c=4))\
                    .then_inc(Y.drained.sem, 1)

        def plan_prep2():
            L = "prepL2x"
            for bk in (Y, O, X, S[0], S[1], TB[0]):
                bk.plan(L, 1)

        def prep2_pe(pe):
            L = "prepL2x"
            pe.wait_ge(loaded["attn2"].sem, LOADS["attn2"])
            for h, bk in enumerate((Y, O)):
                r = slice(64 * h, 64 * h + 64)
                bk.wait_empty(pe, L)
                pe.matmul(bk.t[:, 0:P], w2[r, 1, :], w2[r, 0, :], start=True, stop=True).then_inc(bk.full.sem, 1)
            X.wait_empty(pe, L)
            for i in range(2):
                last = pe.transpose(X.t[:, i * P:(i + 1) * P], w2[:, 2 + i, :], ident[:, :])
            last.then_inc(X.full.sem, 1)
            for h, (bk, src) in enumerate(((S[0], Y), (S[1], O))):
                src.wait_drained(pe, L)
                bk.wait_empty(pe, L)
                pe.matmul(bk.t[:, 0:NB * CK], a2[:, h, :], keysT, start=True, stop=True).then_inc(bk.full.sem, 1)
            X.wait_drained(pe, L)
            TB[0].wait_empty(pe, L)
            for b in range(NB):
                last = pe.matmul(TB[0].t[0:CK, b * P:(b + 1) * P], keysT[:, b, :], wT[:, 0, :], start=True, stop=True)
            last.then_inc(TB[0].full.sem, 1)

        def prep2_act(act):
            L = "prepL2x"
            for h, bk in enumerate((Y, O)):
                bk.wait_full(act, L)
                act.activation(a2[:, h, :], bk.t[:, 0:P], ACT.Copy).then_inc(bk.drained.sem, 1)
            X.wait_full(act, L)
            act.activation(wT[:, 0, :], X.t[:, 0:P], ACT.Copy)
            act.activation(out_wT[:, 0, :], X.t[:, P:2 * P], ACT.Copy).then_inc(X.drained.sem, 1)

        def prep2_dve(dve):
            L = "prepL2x"
            for h in range(2):
                S[h].wait_full(dve, L)
                dve.tensor_copy(G2[:, :, h, :], S[h].t[:, 0:NB * CK].rearrange("p (b k) -> p b k", b=NB))\
                    .then_inc(S[h].drained.sem, 1)
            TB[0].wait_full(dve, L)
            for b in range(NB):
                last = dve.tensor_copy(V2[0:CK, b, :, 0:64],
                                       TB[0].t[0:CK, b * P:(b + 1) * P].rearrange("p (h e) -> p h e", h=2))
            last.then_inc(TB[0].drained.sem, 1)

        FC_BANKS = [S[0], S[1], S[2], TB[0]]

        def plan_ffn0():
            for bk in (TB[0], TB[1], X, Y):
                bk.plan("prepL0f", 1)
            L = "L0f"
            plan_norm(L)
            X.plan(L, 1, NB)
            for bk in FC_BANKS:
                bk.plan(L, 1, NB)
            Y.plan(L, 1, NB)
            square_ready.plan(L, NC, NB)
            x_done.plan(L, 1, NB)

        def prep_ffn0_dve(dve):
            dve.wait_ge(loaded["ffn0"].sem, LOADS["ffn0"])
            n = 0

            def step(ins):
                nonlocal n
                n += 1
                ins.then_inc(tern.sem, 1)
                dve.wait_ge(tern.sem, n)

            mean, scale, hi, lo = wsc[:, 0, 0:5], wsc[:, 0, 8:13], wsc[:, 1, 0:5], wsc[:, 1, 8:13]
            wp = wpr[:, :].rearrange("p (c d) -> p c d", c=NC)
            dve.tensor_reduce(mean[:, 0:NC], wfc[:, :, :], AX.X, ALU.add, apply_absolute_value=True)
            step(dve.tensor_reduce(mean[:, NC:NC + 1], wpr[:, :], AX.X, ALU.add, apply_absolute_value=True))
            step(dve.tensor_scalar(scale[:, 0:NC], mean[:, 0:NC], 1.0 / P, 1e-5, ALU.mult, ALU.max))
            step(dve.tensor_scalar(scale[:, NC:NC + 1], mean[:, NC:NC + 1], 1.0 / FF, 1e-5, ALU.mult, ALU.max))
            step(dve.tensor_scalar(hi, scale, 0.5, None, ALU.mult))
            step(dve.tensor_scalar(lo, scale, -0.5, None, ALU.mult))
            for w, col in ((wfc, lambda c: c), (wp, lambda c: NC)):
                for c in range(NC):
                    k = col(c)
                    dve.tensor_scalar(wt1[:, c, :], w[:, c, :], hi[:, k:k + 1], None, ALU.is_gt)
                    last = dve.tensor_scalar(wt2[:, c, :], w[:, c, :], lo[:, k:k + 1], None, ALU.is_lt)
                step(last)
                step(dve.tensor_tensor(wt1[:, :, :], wt1[:, :, :], wt2[:, :, :], ALU.subtract))
                step(dve.tensor_tensor(wt1[:, :, :], wt1[:, :, :], w[:, :, :], ALU.subtract))
                step(dve.tensor_tensor(w[:, :, :], w[:, :, :], wt1[:, :, :], ALU.add))
                for c in range(NC):
                    last = dve.tensor_scalar(w[:, c, :], w[:, c, :], scale[:, col(c):col(c) + 1], None, ALU.mult)
                step(last)
            assert n == TERN_STEPS
            TB[1].wait_full(dve, "prepL0f")
            dve.tensor_scalar(bv[:, :], TB[1].t[0:16, 0:P], gate[:, 0:1], None, ALU.mult).then_inc(TB[1].drained.sem, 1)

        TERN_STEPS = 15

        def prep_ffn0_pe(pe):
            L = "prepL0f"
            pe.wait_ge(loaded["ffn0"].sem, LOADS["ffn0"])
            TB[0].wait_empty(pe, L)
            for c in range(NC):
                last = pe.transpose(TB[0].t[0:16, c * P:(c + 1) * P], lr[:, c, :], ident[:, :])
            last.then_inc(TB[0].full.sem, 1)
            TB[1].wait_empty(pe, L)
            pe.matmul(TB[1].t[0:16, 0:P], fbT[:, :], vlow[:, :], start=True, stop=True).then_inc(TB[1].full.sem, 1)
            TB[0].wait_drained(pe, L)
            TB[1].wait_drained(pe, L)
            pe.wait_ge(tern.sem, TERN_STEPS)
            X.wait_empty(pe, L)
            for c in range(NC):
                o = X.t[:, c * P:(c + 1) * P]
                pe.matmul(o, wfc[:, c, :], ident[:, :], start=True, stop=False)
                last = pe.matmul(o, bv[:, :], lrT[:, c * P:(c + 1) * P], start=False, stop=True)
            last.then_inc(X.full.sem, 1)
            Y.wait_empty(pe, L)
            for c in range(NC):
                last = pe.transpose(Y.t[:, c * P:(c + 1) * P], wpr[:, c * P:(c + 1) * P], ident[:, :])
            last.then_inc(Y.full.sem, 1)
            X.wait_drained(pe, L)
            Y.wait_drained(pe, L)

        def prep_ffn0_act(act):
            L = "prepL0f"
            TB[0].wait_full(act, L)
            act.activation(lrT[:, :], TB[0].t[0:16, :], ACT.Copy).then_inc(TB[0].drained.sem, 1)
            X.wait_full(act, L)
            act.activation(wfcT[:, :], X.t[:, :], ACT.Copy).then_inc(X.drained.sem, 1)
            Y.wait_full(act, L)
            act.activation(wprT[:, :, :], Y.t[:, :].rearrange("p (c d) -> p c d", c=NC), ACT.Copy)\
                .then_inc(Y.drained.sem, 1)

        def fc_pe(pe, L, b, w):
            X.wait_drained(pe, L, 0, b)
            for c, bk in enumerate(FC_BANKS):
                bk.wait_empty(pe, L, 0, b)
                pe.matmul(bk.t[:, :], w[:, c * P:(c + 1) * P], xnT[:, :], start=True, stop=True)\
                    .then_inc(bk.full.sem, 1)

        def proj_pe(pe, L, b, w, row, ready):
            Y.wait_empty(pe, L, 0, b)
            if row is not None:
                pe.matmul(Y.t[:, :], ones[0:1, :], spread(rows[0:1, row, :], 1, NT), start=True, stop=False,
                          skip_group_check=True)
            for c in range(NC):
                ready(pe, b, c)
                for t in range(NT):
                    last = pe.matmul(Y.t[:, t * P:(t + 1) * P], hT[:, c, t * P:(t + 1) * P], w[:, c, :],
                                     start=row is None and c == 0 and t == 0, stop=c == NC - 1,
                                     skip_group_check=True)
            last.then_inc(Y.full.sem, 1)

        def x_rows(b):
            return x[:, b * NT:(b + 1) * NT, :] if isinstance(b, int) else x[:, bass.ds(b * NT, NT), :]

        def add_result_dve(dve, L, b):
            Y.wait_full(dve, L, 0, b)
            dve.tensor_tensor(x_rows(b), x_rows(b), Y.t[:, :].rearrange("p (t d) -> p t d", t=NT), ALU.add)\
                .then_inc(Y.drained.sem, 1)
            Y.wait_drained(dve, L, 0, b)
            dve.sem_inc(x_done.sem, 1)

        def run_ffn0(eng, name):
            L = "L0f"

            def squares(b):
                for c, bk in enumerate(FC_BANKS):
                    bk.wait_drained(eng, L, 0, b)
                    eng.tensor_tensor(hT[:, c, :], hT[:, c, :], hT[:, c, :], ALU.mult).then_inc(square_ready.sem, 1)

            if name == "act":
                eng.wait_ge(zeroed.sem, 16)

            def relus(b):
                for c, bk in enumerate(FC_BANKS):
                    bk.wait_full(eng, L, 0, b)
                    eng.activation(hT[:, c, :], bk.t[:, :], ACT.Relu).then_inc(bk.drained.sem, 1)

            def squared(pe, b, c):
                pe.wait_ge(square_ready.sem, square_ready.after(L, c, b))

            def start(b):
                if name == "pe":
                    fc_pe(eng, L, b, wfcT)
                elif name == "act":
                    relus(b)
                elif name == "dve":
                    squares(b)

            def finish(b):
                if name == "pe":
                    proj_pe(eng, L, b, wprT, None, squared)
                elif name == "dve":
                    add_result_dve(eng, L, b)

            fronts(eng, name, L, 0)
            start(0)
            with eng.Fori(0, NB - 1) as b:
                fronts(eng, name, L, b + 1)
                finish(b)
                start(b + 1)
            finish(NB - 1)

        def fronts(eng, name, L, b):
            {"pe": front_pe, "dve": front_dve, "act": front_act, "pool": front_pool}[name](eng, L, b)

        def plan_ffn1():
            L = "L1f"
            plan_norm(L)
            X.plan(L, 1, NB)
            O.plan(L, 1, NB)
            Y.plan(L, 1, NB)
            TB[0].plan(L, 1, NB)
            for bk in (S[0], S[1], S[2], TB[1]):
                bk.plan(L, 2, NB)
            logits_in.plan(L, 1, NB)
            gate_step.plan(L, GATE_STEPS, NB)
            gate_exp.plan(L, 1, NB)
            chain.plan(L, 6 * NT, NB)
            x_done.plan(L, 1, NB)

        GATE_STEPS = 13

        def tile_banks(t):
            return (S[0], S[1]) if t % 2 == 0 else (S[2], TB[1])

        def run_ffn1(eng, name):
            L = "L1f"

            def logits_pe(b):
                logits_wait(b)
                O.wait_empty(eng, L, 0, b)
                for t in range(NT):
                    last = eng.matmul(O.t[:, t * NE:(t + 1) * NE], xnT[:, t * P:(t + 1) * P], wg1[:, :],
                                      start=True, stop=True)
                last.then_inc(O.full.sem, 1)

            def logits_wait(b):
                eng.wait_ge(logits_in.sem, logits_in.after(L, 0, b))

            def experts_pe(b, t):
                if t == 0:
                    X.wait_drained(eng, L, 0, b)
                for i, bk in enumerate(tile_banks(t)):
                    bk.wait_empty(eng, L, t // 2, b)
                    eng.matmul(bk.t[:, :], mixT[:, t * P:(t + 1) * P], we[:, 4 * i:4 * i + 4, :],
                               start=True, stop=True).then_inc(bk.full.sem, 1)

            def gates_transposed_pe(b):
                eng.wait_ge(gate_step.sem, gate_step.after(L, GATE_STEPS - 1, b))
                TB[0].wait_empty(eng, L, 0, b)
                for t in range(NT):
                    last = eng.transpose(TB[0].t[0:NE, t * P:(t + 1) * P], gsel[:, t, :], ident[:, :])
                last.then_inc(TB[0].full.sem, 1)

            def biases_pe(b):
                TB[0].wait_drained(eng, L, 0, b)
                Y.wait_empty(eng, L, 0, b)
                for t in range(NT):
                    last = eng.matmul(Y.t[:, t * P:(t + 1) * P], gT[:, t * P:(t + 1) * P], be[:, :],
                                      start=True, stop=True)
                last.then_inc(Y.full.sem, 1)

            def gate_dve_a(b, k):
                O.wait_full(eng, L, 0, b)
                eng.tensor_tensor(lg[:, :, 0:NE], O.t[:, 0:NT * NE].rearrange("p (t e) -> p t e", t=NT),
                                  spread(bg1[:, :], 1, NT), ALU.add).then_inc(O.drained.sem, 1)
                O.wait_drained(eng, L, 0, b)
                k(eng.tensor_reduce(gs[:, 0, :], lg[:, :, 0:NE], AX.X, ALU.max))
                k(eng.tensor_tensor(lg[:, :, 0:NE], lg[:, :, 0:NE], spread(gs[:, 0, :], 2, NE), ALU.subtract))

            def gate_dve_b(b, k):
                eng.wait_ge(gate_exp.sem, gate_exp.after(L, 0, b))
                eng.sem_inc(passed.sem, 1)
                for t in range(NT):
                    last = eng.max(top8[:, t, :], ex[:, t, 0:NE])
                k(last)
                eng.sem_inc(passed.sem, 1)
                for t in range(NT):
                    last = eng.max_index(idx8[:, t, :], top8[:, t, :], ex[:, t, 0:NE])
                k(last)
                k(eng.tensor_copy(idxf[:, :, :], idx8[:, :, :]))
                k(eng.tensor_tensor(gs[:, 1, :], top8[:, :, 0], top8[:, :, 1], ALU.add))
                k(eng.reciprocal(gs[:, 2, :], gs[:, 1, :]))
                k(eng.tensor_tensor(gs[:, 0, :], top8[:, :, 0], gs[:, 2, :], ALU.mult))
                k(eng.tensor_tensor(gs[:, 3, :], top8[:, :, 1], gs[:, 2, :], ALU.mult))
                io = spread(iota8[:, :], 1, NT)
                eng.tensor_tensor(gsel[:, :, :], io, spread(idxf[:, :, 0], 2, NE), ALU.is_equal)
                k(eng.tensor_tensor(gtmp[:, :, :], io, spread(idxf[:, :, 1], 2, NE), ALU.is_equal))
                k(eng.tensor_tensor(gsel[:, :, :], gsel[:, :, :], spread(gs[:, 0, :], 2, NE), ALU.mult))
                k(eng.tensor_tensor(gtmp[:, :, :], gtmp[:, :, :], spread(gs[:, 3, :], 2, NE), ALU.mult))
                k(eng.tensor_tensor(gsel[:, :, :], gsel[:, :, :], gtmp[:, :, :], ALU.add))

            def stepper(b):
                n = [0]

                def k(ins):
                    ins.then_inc(gate_step.sem, 1)
                    eng.wait_ge(gate_step.sem, gate_step.after(L, n[0], b))
                    n[0] += 1
                return k, n

            def combine_dve(b, t):
                xt = x[:, b * NT + t, :]
                m = 6 * t
                for i, bk in enumerate(tile_banks(t)):
                    bk.wait_full(eng, L, t // 2, b)
                    for e in range(4):
                        ins = eng.scalar_tensor_tensor(xt, bk.t[:, e * P:(e + 1) * P], gsel[:, t, 4 * i + e:4 * i + e + 1],
                                                       xt, ALU.mult, ALU.add)
                        if e < 3:
                            ins.then_inc(chain.sem, 1)
                            eng.wait_ge(chain.sem, chain.after(L, m, b))
                            m += 1
                        else:
                            ins.then_inc(bk.drained.sem, 1)
                            bk.wait_drained(eng, L, t // 2, b)

            def first(b):
                if name == "pe":
                    front_pe(eng, L, b)
                    logits_pe(b)
                elif name == "act":
                    X.wait_full(eng, L, 0, b)
                    eng.activation(xnT[:, :], X.t[:, :], ACT.Copy).then_inc(logits_in.sem, 1)

            def body(b, last):
                nxt = None if last else b + 1
                if name == "pe":
                    if not last:
                        first(nxt)
                    experts_pe(b, 0)
                    gates_transposed_pe(b)
                    experts_pe(b, 1)
                    experts_pe(b, 2)
                    biases_pe(b)
                    experts_pe(b, 3)
                elif name == "act":
                    if not last:
                        first(nxt)
                    TB[0].wait_full(eng, L, 0, b)
                    eng.activation(gT[:, :], TB[0].t[0:NE, :], ACT.Copy).then_inc(TB[0].drained.sem, 1)
                    if not last:
                        eng.wait_ge(gate_step.sem, gate_step.after(L, 1, nxt))
                        eng.activation(ex[:, :, 0:NE], lg[:, :, 0:NE], ACT.Exp).then_inc(gate_exp.sem, 1)
                        TB[1].wait_full(eng, L, 1, b)
                        eng.activation(mixT[:, :], X.t[:, :], ACT.Copy).then_inc(X.drained.sem, 1)
                elif name == "dve":
                    if not last:
                        front_dve(eng, L, nxt)
                    combine_dve(b, 0)
                    combine_dve(b, 1)
                    if not last:
                        k, n = stepper(nxt)
                        gate_dve_a(nxt, k)
                    combine_dve(b, 2)
                    combine_dve(b, 3)
                    add_result_dve(eng, L, b)
                    if not last:
                        gate_dve_b(nxt, k)
                        assert n[0] == GATE_STEPS, n
                elif name == "pool":
                    if not last:
                        front_pool(eng, L, nxt)

            if name in ("pe", "act"):
                first(0)
                if name == "act":
                    eng.wait_ge(gate_step.sem, gate_step.after(L, 1, 0))
                    eng.activation(ex[:, :, 0:NE], lg[:, :, 0:NE], ACT.Exp).then_inc(gate_exp.sem, 1)
                    eng.activation(mixT[:, :], X.t[:, :], ACT.Copy).then_inc(X.drained.sem, 1)
            elif name == "dve":
                front_dve(eng, L, 0)
                k, n = stepper(0)
                gate_dve_a(0, k)
                gate_dve_b(0, k)
            else:
                front_pool(eng, L, 0)
            with eng.Fori(0, NB - 1) as b:
                body(b, False)
            body(NB - 1, True)

        def plan_ffn2():
            L = "L2f"
            plan_norm(L)
            X.plan(L, 1, NB)
            O.plan(L, 2, NB)
            Y.plan(L, 1, NB)
            for bk in (S[0], S[1], TB[0], TB[1]):
                bk.plan(L, 2, NB)
            xa_ready.plan(L, 1, NB)
            gelu_ready.plan(L, 1, NB)
            x_done.plan(L, 1, NB)

        w1e = big[:, 0, :].rearrange("p (e f) -> p e f", e=NE)
        w2e = big[:, 1, :].rearrange("p (e c d) -> p e c d", e=NE, c=NC)

        def run_ffn2(eng, name):
            L = "L2f"

            def front(b):
                if name == "pe":
                    front_pe(eng, L, b)
                    eng.wait_ge(z_ready.sem, z_ready.after(L, 0, b))
                    O.wait_empty(eng, L, 0, b)
                    for t in range(NT):
                        last = eng.transpose(O.t[:, t * P:(t + 1) * P], z[:, t, :], ident[:, :])
                    last.then_inc(O.full.sem, 1)
                elif name == "act":
                    front_act(eng, L, b)
                    O.wait_full(eng, L, 0, b)
                    eng.activation(mixT[:, :], O.t[:, :], ACT.Identity, scale=cols2[:, 0:1], bias=cols2[:, 1:2])\
                        .then_inc(O.drained.sem, 1)
                else:
                    fronts(eng, name, L, b)

            def attn_linear(b):
                if name == "pe":
                    O.wait_drained(eng, L, 0, b)
                    eng.matmul(O.t[:, :], attn_w[:, :], mixT[:, :], start=True, stop=True).then_inc(O.full.sem, 1)
                elif name == "dve":
                    O.wait_full(eng, L, 1, b)
                    X.wait_drained(eng, L, 0, b)
                    eng.scalar_tensor_tensor(xaT[:, :], O.t[:, :], cols2[:, 2:3], xnT[:, :], ALU.add, ALU.add)\
                        .then_inc(O.drained.sem, 1)

            def hidden(b, t):
                e = (b * NT + t) % NE
                bk = S[t % 2]
                if name == "pe":
                    if t == 0:
                        O.wait_drained(eng, L, 1, b)
                    bk.wait_empty(eng, L, t // 2, b)
                    for c in range(NC):
                        last = eng.matmul(bk.t[:, c * P:(c + 1) * P], w1e[:, e, c * P:(c + 1) * P],
                                          xaT[:, t * P:(t + 1) * P], start=True, stop=True)
                    last.then_inc(bk.full.sem, 1)
                elif name == "act":
                    bk.wait_full(eng, L, t // 2, b)
                    for c in range(NC):
                        last = eng.activation(hT[:, c, (t % 2) * P:(t % 2 + 1) * P], bk.t[:, c * P:(c + 1) * P],
                                              ACT.Gelu, bias=b1c[:, e, c:c + 1])
                    last.then_inc(bk.drained.sem, 1)

            def down(b, t):
                e = (b * NT + t) % NE
                bk = TB[t % 2]
                if name == "pe":
                    S[t % 2].wait_drained(eng, L, t // 2, b)
                    bk.wait_empty(eng, L, t // 2, b)
                    for c in range(NC):
                        last = eng.matmul(bk.t[:, 0:P], w2e[:, e, c, :], hT[:, c, (t % 2) * P:(t % 2 + 1) * P],
                                          start=c == 0, stop=c == NC - 1)
                    last.then_inc(bk.full.sem, 1)
                elif name == "dve":
                    bk.wait_full(eng, L, t // 2, b)
                    eng.tensor_scalar(mix[:, t, :], bk.t[:, 0:P], b2c[:, e:e + 1], None, ALU.add)\
                        .then_inc(bk.drained.sem, 1)

            def last_linear(b):
                if name == "pe":
                    TB[0].wait_drained(eng, L, 1, b)
                    TB[1].wait_drained(eng, L, 1, b)
                    Y.wait_empty(eng, L, 0, b)
                    eng.matmul(Y.t[:, :], ones[0:1, :], spread(rows[0:1, 3, :], 1, NT), start=True, stop=False,
                               skip_group_check=True)
                    for t in range(NT):
                        last = eng.matmul(Y.t[:, t * P:(t + 1) * P], mix[:, t, :], next_w[:, :], start=False,
                                          stop=True, skip_group_check=True)
                    last.then_inc(Y.full.sem, 1)
                elif name == "act":
                    Y.wait_full(eng, L, 0, b)
                    if b:
                        eng.wait_ge(x_done.sem, x_done.after(L, 0, b - 1))
                    eng.activation(gout[:, :], Y.t[:, :], ACT.Gelu).then_inc(Y.drained.sem, 1)
                elif name == "dve":
                    Y.wait_drained(eng, L, 0, b)
                    eng.tensor_tensor(x_rows(b), x_rows(b), gout[:, :].rearrange("p (t d) -> p t d", t=NT), ALU.add)\
                        .then_inc(x_done.sem, 1)

            if name == "pe":
                eng.wait_ge(loaded["ffn2"].sem, LOADS["ffn2"])
            if name == "act":
                eng.wait_ge(loaded["ffn2"].sem, LOADS["ffn2"])
            if name == "dve":
                eng.wait_ge(loaded["ffn2"].sem, LOADS["ffn2"])
            front(0)
            attn_linear(0)
            hidden(0, 0)
            for b in range(NB):
                if name in ("dve", "pool") and b < NB - 1:
                    front(b + 1)
                for t in range(NT - 1):
                    hidden(b, t + 1)
                    if t == 2 and b < NB - 1 and name in ("pe", "act"):
                        front(b + 1)
                    down(b, t)
                if b < NB - 1:
                    attn_linear(b + 1)
                    hidden(b + 1, 0)
                down(b, NT - 1)
                last_linear(b)

        RES_STEPS = 15

        def plan_ffn3():
            L = "L3f"
            plan_norm(L)
            X.plan(L, 1, NB)
            O.plan(L, 1, NB)
            Y.plan(L, 1, NB)
            for bk in FC_BANKS:
                bk.plan(L, 1, NB)
            base_added.plan(L, 1, NB)
            normed_ready.plan(L, 2, NB)
            res_step.plan(L, RES_STEPS, NB)
            res_exp.plan(L, 1, NB)
            for bk in (TB[1],):
                bk.plan("place", 1)
            for bk in (S[0], S[1], S[2], TB[0]):
                bk.plan("sent", 1)
                bk.plan("experts", NE // 2)
            O.plan("experts", NE // 2)
            Y.plan("experts", NE // 2)
            x_done.plan(L, 1, NB)

        def run_ffn3(eng, name):
            L = "L3f"

            def front(b):
                if name == "dve":
                    ln_stats_dve(eng, L, b, 0)
                    ln_apply_dve(eng, L, b, 0)
                    ln_stats_dve(eng, L, b, 1)
                    eng.tensor_tensor(x_rows(b), x_rows(b), xn[:, :, :], ALU.add).then_inc(base_added.sem, 1)
                    if not (isinstance(b, int) and b == 0):
                        X.wait_full(eng, L, 0, b - 1)
                        eng.wait_ge(normed_ready.sem, normed_ready.after(L, 0, b - 1))
                    ln_apply_dve(eng, L, b, 1)
                elif name == "pool":
                    ln_rstd_pool(eng, L, b, 0)
                    ln_rstd_pool(eng, L, b, 1)
                    dst = normed[:, b * NT:(b + 1) * NT, :] if isinstance(b, int) else normed[:, bass.ds(b * NT, NT), :]
                    eng.wait_ge(z_ready.sem, z_ready.after(L, 0, b))
                    eng.sem_inc(pool_passed.sem, 1)
                    eng.tensor_tensor(dst, z[:, :, :], spread(nw_all, 1, NT), ALU.mult).then_inc(normed_ready.sem, 1)
                    eng.wait_ge(normed_ready.sem, normed_ready.after(L, 0, b))
                    eng.sem_inc(pool_passed.sem, 1)
                    eng.tensor_tensor(dst, dst, spread(nb_all, 1, NT), ALU.add).then_inc(normed_ready.sem, 1)
                elif name == "pe":
                    eng.wait_ge(z_ready.sem, z_ready.after(L, 0, b))
                    X.wait_empty(eng, L, 0, b)
                    for t in range(NT):
                        last = eng.transpose(X.t[:, t * P:(t + 1) * P], z[:, t, :], ident[:, :])
                    last.then_inc(X.full.sem, 1)
                elif name == "act":
                    X.wait_full(eng, L, 0, b)
                    eng.activation(xnT[:, :], X.t[:, :], ACT.Identity, scale=cols3[:, 0:1], bias=cols3[:, 1:2])\
                        .then_inc(X.drained.sem, 1)

            def logits_pe(b):
                X.wait_drained(eng, L, 0, b)
                O.wait_empty(eng, L, 0, b)
                for t in range(NT):
                    last = eng.matmul(O.t[:, t * 10:(t + 1) * 10], xnT[:, t * P:(t + 1) * P], wgc[:, :],
                                      start=True, stop=True)
                last.then_inc(O.full.sem, 1)

            def rows_of(v, b):
                return v[:, b * NT:(b + 1) * NT] if isinstance(b, int) else v[:, bass.ds(b * NT, NT)]

            def gate_dve(b):
                n = [0]

                def k(ins):
                    ins.then_inc(res_step.sem, 1)
                    eng.wait_ge(res_step.sem, res_step.after(L, n[0], b))
                    n[0] += 1

                O.wait_full(eng, L, 0, b)
                eng.tensor_copy(lg[:, :, 0:10], O.t[:, 0:NT * 10].rearrange("p (t e) -> p t e", t=NT))\
                    .then_inc(O.drained.sem, 1)
                O.wait_drained(eng, L, 0, b)
                for i, (c0, c1) in enumerate(((0, NE), (NE, NE + 2))):
                    k(eng.tensor_reduce(gs[:, i, :], lg[:, :, c0:c1], AX.X, ALU.max))
                    k(eng.tensor_tensor(lg[:, :, c0:c1], lg[:, :, c0:c1], spread(gs[:, i, :], 2, c1 - c0), ALU.subtract))
                eng.sem_inc(passed.sem, 1)
                for t in range(NT):
                    last = eng.max(top8[:, t, :], lg[:, t, 0:NE])
                k(last)
                eng.sem_inc(passed.sem, 1)
                for t in range(NT):
                    last = eng.max_index(idx8[:, t, :], top8[:, t, :], lg[:, t, 0:NE])
                k(last)
                k(eng.tensor_copy(rows_of(expert_of, b), idx8[:, :, 0]))
                k(eng.tensor_tensor(rows_of(chosen, b) if isinstance(b, int) else chosen[:, bass.ds(b * NT, NT), :],
                                    spread(iota8[:, :], 1, NT), spread(rows_of(expert_of, b), 2, NE), ALU.is_equal))
                eng.wait_ge(res_exp.sem, res_exp.after(L, 0, b))
                k(eng.tensor_reduce(gs[:, 0, :], ex[:, :, 0:NE], AX.X, ALU.add))
                k(eng.reciprocal(gs[:, 2, :], gs[:, 0, :]))
                k(eng.tensor_reduce(gs[:, 1, :], ex[:, :, NE:NE + 2], AX.X, ALU.add))
                k(eng.reciprocal(gs[:, 3, :], gs[:, 1, :]))
                k(eng.tensor_tensor(rows_of(coef0, b), ex[:, :, NE], gs[:, 3, :], ALU.mult))
                k(eng.tensor_tensor(gs[:, 0, :], ex[:, :, NE + 1], gs[:, 3, :], ALU.mult))
                k(eng.tensor_tensor(rows_of(weight_of, b), gs[:, 0, :], gs[:, 2, :], ALU.mult))
                return n, k

            def gate_act(b):
                eng.wait_ge(res_step.sem, res_step.after(L, 3, b))
                eng.activation(ex[:, :, 0:10], lg[:, :, 0:10], ACT.Exp).then_inc(res_exp.sem, 1)

            def gelus(b):
                for c, bk in enumerate(FC_BANKS):
                    bk.wait_full(eng, L, 0, b)
                    eng.activation(hT[:, c, :], bk.t[:, :], ACT.Gelu_apprx_tanh, bias=cols3[:, 2 + c:3 + c])\
                        .then_inc(bk.drained.sem, 1)

            def activated(pe, b, c):
                FC_BANKS[c].wait_drained(pe, L, 0, b)

            def start(b):
                if name == "pe":
                    logits_pe(b)
                    fc_pe(eng, L, b, res_w1)
                elif name == "act":
                    gate_act(b)
                    gelus(b)
                elif name == "dve":
                    n, k = gate_dve(b)
                    assert n[0] == RES_STEPS, n

            def finish(b):
                if name == "pe":
                    proj_pe(eng, L, b, res_w2, 4, activated)
                elif name == "dve":
                    Y.wait_full(eng, L, 0, b)
                    for t in range(NT):
                        xt = x[:, b * NT + t, :]
                        ins = eng.scalar_tensor_tensor(xt, Y.t[:, t * P:(t + 1) * P],
                                                       coef0[:, b * NT + t:b * NT + t + 1] if isinstance(b, int)
                                                       else coef0[:, bass.ds(b * NT + t, 1)], xt, ALU.mult, ALU.add)
                    ins.then_inc(Y.drained.sem, 1)

            if name != "pool":
                eng.wait_ge(loaded["ffn3"].sem, LOADS["ffn3"])
            else:
                eng.wait_ge(loaded["ffn3"].sem, LOADS["ffn3"])
            front(0)
            start(0)
            with eng.Fori(0, NB - 1) as b:
                front(b + 1)
                finish(b)
                start(b + 1)
            finish(NB - 1)

            tile_hidden = lambda e: (S[0], S[1]) if e % 2 == 0 else (S[2], TB[0])
            tile_out = lambda e: O if e % 2 == 0 else Y
            if name == "pe":
                eng.wait_ge(route_made.sem, 2)
                eng.wait_ge(res_step.sem, res_step.after(L, RES_STEPS - 1, NB - 1))
                TB[1].wait_empty(eng, "place")
                o = TB[1].t[:, 0:P].rearrange("p (g e) -> p g e", e=NE)
                eng.matmul(o, earlier, chosen, start=True, stop=False, skip_group_check=True)
                G = NB * NT
                for g in range(G - 1):
                    last = eng.matmul(o[:, g + 1:G, :], onesb, spread(chosen[:, g, :], 1, G - 1 - g),
                                      start=False, stop=g == G - 2, skip_group_check=True)
                last.then_inc(TB[1].full.sem, 1)
                eng.wait_ge(sent_loaded.sem, 16)
                for i, bk in enumerate((S[0], S[1], S[2], TB[0])):
                    bk.wait_empty(eng, "sent")
                    for t in range(4):
                        last = eng.transpose(bk.t[:, t * P:(t + 1) * P], sent[:, 4 * i + t, :], ident[:, :])
                    last.then_inc(bk.full.sem, 1)
                for e in range(NE + 1):
                    if e < NE:
                        if e % 2 == 0:
                            (S[0], S[1], S[2], TB[0])[e // 2].wait_drained(eng, "sent")
                        for i, bk in enumerate(tile_hidden(e)):
                            bk.wait_empty(eng, "experts", e // 2)
                            for c in range(2):
                                f = (2 * i + c) * P
                                last = eng.matmul(bk.t[:, c * 256:(c + 1) * 256], w1e[:, e, f:f + P],
                                                  sentT[:, e * CAP:(e + 1) * CAP], start=True, stop=True)
                            last.then_inc(bk.full.sem, 1)
                    if e > 0:
                        q = e - 1
                        bo = tile_out(q)
                        bo.wait_empty(eng, "experts", q // 2)
                        eng.matmul(bo.t[:, 0:256], ones[0:1, :], spread(out_b_row[0:1, q, :], 1, 2), start=True,
                                   stop=False, skip_group_check=True)
                        for bk in tile_hidden(q):
                            bk.wait_drained(eng, "experts", q // 2)
                        for c in range(NC):
                            for j in range(2):
                                col = (q % 2) * 256 + j * P
                                last = eng.matmul(bo.t[:, j * P:(j + 1) * P], hT[:, c, col:col + P], w2e[:, q, c, :],
                                                  start=False, stop=c == NC - 1, skip_group_check=True)
                        last.then_inc(bo.full.sem, 1)
            elif name == "act":
                for i, bk in enumerate((S[0], S[1], S[2], TB[0])):
                    bk.wait_full(eng, "sent")
                    eng.activation(sentT[:, i * 512:(i + 1) * 512], bk.t[:, :], ACT.Copy).then_inc(bk.drained.sem, 1)
                for e in range(NE):
                    for i, bk in enumerate(tile_hidden(e)):
                        bk.wait_full(eng, "experts", e // 2)
                        for c in range(2):
                            col = (e % 2) * 256
                            last = eng.activation(hT[:, 2 * i + c, col:col + 256], bk.t[:, c * 256:(c + 1) * 256],
                                                  ACT.Gelu_apprx_tanh, bias=b1c[:, e, 2 * i + c:2 * i + c + 1])
                        last.then_inc(bk.drained.sem, 1)
            elif name == "dve":
                n = 0

                def step(ins):
                    nonlocal n
                    n += 1
                    ins.then_inc(route_step.sem, 1)
                    eng.wait_ge(route_step.sem, n)

                TB[1].wait_full(eng, "place")
                eng.tensor_tensor(counted, TB[1].t[:, 0:P].rearrange("p (g e) -> p g e", e=NE), chosen, ALU.mult)\
                    .then_inc(TB[1].drained.sem, 1)
                TB[1].wait_drained(eng, "place")
                step(eng.tensor_reduce(place, counted, AX.X, ALU.add))
                step(eng.tensor_scalar(kept, place, float(CAP), None, ALU.is_lt))
                step(eng.scalar_tensor_tensor(slot, expert_of, float(CAP), place, ALU.mult, ALU.add))
                eng.tensor_tensor(weight_of, weight_of, kept, ALU.mult)
                step(eng.tensor_tensor(slot_get, slot, kept, ALU.mult))
                step(eng.tensor_scalar(kept, kept, -float(2 * NTOK), float(2 * NTOK), ALU.mult, ALU.add))
                step(eng.tensor_tensor(slot_put, slot, kept, ALU.add))
                for e in range(NE):
                    bo = tile_out(e)
                    bo.wait_full(eng, "experts", e // 2)
                    eng.tensor_copy(expert_out[:, 2 * e:2 * e + 2, :], bo.t[:, 0:256].rearrange("p (j d) -> p j d", j=2))\
                        .then_inc(bo.drained.sem, 1)
                for b in range(NB):
                    eng.wait_ge(gathered[b].sem, 16 * NT)
                    for t in range(NT):
                        g = b * NT + t
                        last = eng.scalar_tensor_tensor(x[:, g, :], got[:, g, :], weight_of[:, g:g + 1], x[:, g, :],
                                                        ALU.mult, ALU.add)
                    last.then_inc(x_done.sem, 1)
            elif name == "pool":
                eng.wait_ge(route_step.sem, 6)
                eng.wait_ge(zeroed.sem, 16)
                eng.wait_ge(normed_ready.sem, normed_ready.after(L, 1, NB - 1))
                for g in range(NB * NT):
                    eng.indirect_dma_start(out=dispatched_d, out_offset=bass.IndirectOffsetOnAxis(ap=slot_put[:, g:g + 1], axis=0),
                                           in_=normed[:, g, :], in_offset=None, bounds_check=NTOK - 1,
                                           oob_is_err=False).then_inc(scattered.sem, 16)
                eng.wait_ge(stored.sem, 16 * NE)
                for g in range(NB * NT):
                    eng.indirect_dma_start(out=got[:, g, :], out_offset=None, in_=expert_out_d,
                                           in_offset=bass.IndirectOffsetOnAxis(ap=slot_get[:, g:g + 1], axis=0))\
                        .then_inc(gathered[g // NT].sem, 16)

        def route_constants_pool(pool):
            pool.wait_ge(x_done.sem, x_done.after("L2f", 0, NB - 1))
            pool.memset(earlier, 1.0).then_inc(pool_step.sem, 1)
            pool.wait_ge(pool_step.sem, POOL_STEPS + 1)
            pool.affine_select(out=earlier, in_=earlier, compare_op=ALU.is_gt, fill=0.0, base=0,
                               pattern=[[1, P]], channel_multiplier=-1).then_inc(route_made.sem, 1)
            pool.memset(onesb, 1.0).then_inc(route_made.sem, 1)

        POOL_STEPS = 9

        LOADS = {}
        MADE = 1

        Y.plan("phase", 11)
        plan_prep03("L0x")
        plan_attention("L0x")
        plan_ffn0()
        plan_prep1()
        plan_attention("L1x")
        plan_ffn1()
        plan_prep2()
        plan_attention("L2x")
        plan_ffn2()
        plan_prep03("L3x")
        plan_attention("L3x")
        plan_ffn3()

        WAVES = 10
        phase_d = event("phase_dve")
        phase_a = event("phase_act")

        def phase_pe(pe):
            pe.wait_ge(loaded["const"].sem, LOADS["const"])
            for i in range(WAVES):
                if i:
                    pe.wait_ge(phase_a.sem, i)
                else:
                    pe.wait_ge(phase_d.sem, 1)
                Y.wait_empty(pe, "phase", i)
                pe.matmul(Y.t[0:H16, 0:1], phw[:, 0:H16], ph[:, 0:1], start=True, stop=True).then_inc(Y.full.sem, 1)
            pe.wait_ge(phase_d.sem, 1 + 5 * WAVES + 4)
            Y.wait_empty(pe, "phase", WAVES)
            pe.matmul(Y.t[:, 0:H16], ones16[:, :], dg[:, :], start=True, stop=True).then_inc(Y.full.sem, 1)

        def phase_dve(dve):
            dve.memset(ph[:, 0:1], 0.0).then_inc(phase_d.sem, 1)
            dve.memset(ones16[:, :], 1.0)
            dve.wait_ge(loaded["const"].sem, LOADS["const"])
            dve.wait_ge(made.sem, MADE)
            n = 1

            def step(ins):
                nonlocal n
                n += 1
                ins.then_inc(phase_d.sem, 1)
                dve.wait_ge(phase_d.sem, n)

            for i in range(WAVES):
                Y.wait_full(dve, "phase", i)
                dve.tensor_scalar(ph[:, 1:2], Y.t[0:H16, 0:1], ph[:, 7:8], phw[:, 16:17], ALU.mult, ALU.add)\
                    .then_inc(Y.drained.sem, 1)
                Y.wait_drained(dve, "phase", i)
                step(dve.tensor_scalar(ph[:, 2:3], ph[:, 1:2], 0.01, None, ALU.mult))
                step(dve.tensor_scalar(ph[:, 3:4], ph[:, 2:3], 1.0 / TWO_PI, None, ALU.mult))
                step(dve.tensor_scalar(ph[:, 4:5], ph[:, 3:4], ROUND, None, ALU.add))
                step(dve.tensor_scalar(ph[:, 5:6], ph[:, 4:5], ROUND, -TWO_PI, ALU.subtract, ALU.mult))
                if i:
                    dve.wait_ge(phase_a.sem, i)
                step(dve.tensor_tensor(ph[:, 6:7], ph[:, 5:6], ph[:, 2:3], ALU.add))
            step(dve.tensor_scalar(ph[:, 3:4], ph[:, 6:7], -1.0, None, ALU.mult))
            step(dve.tensor_tensor(ph[:, 1:2], ph[:, 6:7], ph[:, 3:4], ALU.min))
            step(dve.tensor_scalar(ph[:, 2:3], ph[:, 1:2], math.pi / 2, None, ALU.add))
            dve.wait_ge(phase_a.sem, WAVES + 1)
            step(dve.tensor_scalar(dg[:, :], ident[0:H16, 0:H16], ph[:, 8:9], 0.1, ALU.mult, ALU.mult))
            Y.wait_full(dve, "phase", WAVES)
            dve.tensor_copy(head_bias[:, :], Y.t[:, 0:H16]).then_inc(Y.drained.sem, 1)
            Y.wait_drained(dve, "phase", WAVES)

        def phase_act(act):
            for i in range(WAVES):
                act.wait_ge(phase_d.sem, 1 + 5 * (i + 1))
                act.activation(ph[:, 0:1], ph[:, 6:7], ACT.Sin).then_inc(phase_a.sem, 1)
            act.wait_ge(phase_d.sem, 1 + 5 * WAVES + 3)
            act.activation(ph[:, 8:9], ph[:, 2:3], ACT.Sin).then_inc(phase_a.sem, 1)

        def neighbours_loaded():
            pass

        LOADS.update({"const": 48, "w0": 80, "ctx": 16, "ffn0": 96, "attn1": 80, "mask1": 32, "ffn1": 64,
                      "attn2": 80, "attn3": 64, "ffn2": 160, "mask3": 16, "ffn3": 14 * 16})

        block = ctx.enter_context(nc.Block())

        @block.sync
        def _(sp):
            load(sp, "x", x[:, :, :], a["x"].rearrange("b (t p) d -> p (b t) d", p=P))
            load(sp, "ctx", ctx_tok[:, :, :], a["ctx_1024"].rearrange("b k d -> k b d"))
            for i, n in enumerate(("Wq", "Wk", "Wv")):
                load(sp, "w0", w0[:, i, :].rearrange("d (h k) -> d h k", h=H16),
                     a["L0_xattn_" + n].rearrange("h d k -> d h k"))
            load(sp, "w0", w0[:, 3, :], a["L0_xattn_out_w"])
            load(sp, "w0", rows[0:1, 0, :], a["L0_xattn_out_b"].rearrange("(a n) -> a n", a=1))
            load(sp, "const", phw[:, 0:H16], a["phase_weights"])
            load(sp, "const", phw[:, 16:17], a["phase_intrinsic"])
            load(sp, "const", ph[:, 7:8], a["L0_xattn_coupling"].rearrange("(n a) -> n a", a=1))
            sp.wait_ge(zeros_made.sem, 1)
            sp.dma_start(dispatched_d.rearrange("(p r) d -> p (r d)", p=P), hT[:, :, :].rearrange("p c n -> p (c n)"))\
                .then_inc(zeroed.sem, 16)
            load(sp, "ffn0", wfc[:, :, :], a["L0_ffn_w_fc"].rearrange("(c p) d -> p c d", p=P))
            load(sp, "ffn0", wpr[:, :], a["L0_ffn_w_proj"])
            load(sp, "ffn0", lr[:, :, :], a["L0_ffn_u"].rearrange("(c p) r -> p c r", p=P))
            with nc.allow_non_contiguous_dma(reason="a 16x16 transpose"):
                load(sp, "ffn0", fbT[:, :], a["L0_ffn_fast_b"].rearrange("i j -> j i"))
            load(sp, "ffn0", vlow[:, :], a["L0_ffn_v"])
            load(sp, "ffn0", gate[:, :], a["L0_ffn_gate"].rearrange("(a n) -> a n", a=1).broadcast_to([16, 1]))
            for n, dst in (("Wq", w1q), ("Wk", w1k), ("Wv", w1v)):
                load(sp, "attn1", dst, a["L1_xattn_" + n].rearrange("(c p) d -> p c d", p=P))
            load(sp, "attn1", w1o, a["L1_xattn_Wo"])
            load(sp, "attn1", rows[0:1, 1, :], a["L1_xattn_bo"].rearrange("(a n) -> a n", a=1))
            load(sp, "mask1", mask_raw[:, :, :], a["mask_Bx1xSxS2_ik0"].rearrange("b o (t p) k -> p (b o t) k", p=P))
            load(sp, "mask1", src_raw[:, :, :].rearrange("p b k -> p (b k)"),
                 a["mask_Bx1xS2_bk0"].bitcast(U8).rearrange("(a n) -> a n", a=1).broadcast_to([P, NB * CK]))
            load(sp, "ffn1", we[:, :, :], a["L1_ffn_We"].rearrange("e d o -> d e o"))
            load(sp, "ffn1", be[:, :], a["L1_ffn_be"])
            load(sp, "ffn1", wg1[:, :], a["L1_ffn_Wg"])
            load(sp, "ffn1", bg1[:, :], a["L1_ffn_bg"].rearrange("(a n) -> a n", a=1).broadcast_to([P, NE]))
            for i, n in enumerate(("Wq", "Wk", "Wv", "Wp")):
                load(sp, "attn2", w2[:, i, :], a["L2_xattn_" + n])
            load(sp, "attn2", rows[0:1, 2, :], a["L2_xattn_bp"].rearrange("(a n) -> a n", a=1))
            for i, n in enumerate(("wq", "wk", "wv", "w_out")):
                load(sp, "attn3", w3[:, i, :], a["L3_xattn_" + n])
            load(sp, "ffn2", attn_w[:, :], a["L2_ffn_attn_w"])
            load(sp, "ffn2", next_w[:, :], a["L2_ffn_next_w"])
            load(sp, "ffn2", rows[0:1, 3, :], a["L2_ffn_next_b"].rearrange("(a n) -> a n", a=1))
            with nc.allow_non_contiguous_dma(reason="biases as columns"):
                for i, n in enumerate(("ln_g", "ln_b", "attn_b")):
                    load(sp, "ffn2", cols2[:, i:i + 1], a["L2_ffn_" + n].rearrange("(n a) -> n a", a=1))
                load(sp, "ffn2", b1c[:, :, :], a["L2_ffn_b1"].rearrange("e (c p) -> p e c", p=P))
                load(sp, "ffn2", b2c[:, :], a["L2_ffn_b2"].rearrange("e d -> d e"))
            if len(LAYERS) > 2:
                sp.wait_ge(mask_made.sem, 2 + NB)
            load(sp, "mask3", mask_raw[:, :, :], a["mask_BxSxS2_ik1"].rearrange("b (t p) k -> p (b t) k", p=P))
            if len(LAYERS) > 2:
                S[0].wait_full(sp, "prepL1x", 1 + NB)
                load(sp, "ffn2", w1e, a["L2_ffn_w1"].rearrange("e d f -> d e f"))
                load(sp, "ffn2", w2e, a["L2_ffn_w2"].rearrange("e (c p) d -> p e c d", p=P))
            if len(LAYERS) > 7:
                sp.wait_ge(x_done.sem, x_done.after("L2f", 0, NB - 1))
                load(sp, "ffn3", w1e, a["L3_ffn_inter_w"].rearrange("e d f -> d e f"))
                load(sp, "ffn3", w2e, a["L3_ffn_output_w"].rearrange("e (c p) d -> p e c d", p=P))
                load(sp, "ffn3", res_w1, a["L3_ffn_res_inter_w"])
                load(sp, "ffn3", res_w2[:, :, :], a["L3_ffn_res_output_w"].rearrange("(c p) d -> p c d", p=P))
                load(sp, "ffn3", rows[0:1, 4, :], a["L3_ffn_res_output_b"].rearrange("(a n) -> a n", a=1))
                load(sp, "ffn3", out_b_row, a["L3_ffn_output_b"].rearrange("(a e) d -> a e d", a=1))
                load(sp, "ffn3", wgc[:, 0:NE], a["L3_ffn_wg"])
                load(sp, "ffn3", wgc[:, NE:NE + 2], a["L3_ffn_res_coef"])
                load(sp, "ffn3", nw_all, a["L3_ffn_attn_nw"].rearrange("(a n) -> a n", a=1).broadcast_to([P, P]))
                load(sp, "ffn3", nb_all, a["L3_ffn_attn_nb"].rearrange("(a n) -> a n", a=1).broadcast_to([P, P]))
                with nc.allow_non_contiguous_dma(reason="biases as columns"):
                    load(sp, "ffn3", b1c[:, :, :], a["L3_ffn_inter_b"].rearrange("e (c p) -> p e c", p=P))
                    load(sp, "ffn3", cols3[:, 0:1], a["L3_ffn_attn_nw"].rearrange("(n a) -> n a", a=1))
                    load(sp, "ffn3", cols3[:, 1:2], a["L3_ffn_attn_nb"].rearrange("(n a) -> n a", a=1))
                    load(sp, "ffn3", cols3[:, 2:2 + NC], a["L3_ffn_res_inter_b"].rearrange("(c p) -> p c", p=P))
            assert len(LAYERS) < 8 or all(loads[k] == v for k, v in LOADS.items()), loads
            if len(LAYERS) > 7:
                sp.wait_ge(scattered.sem, 16 * NB * NT)
                sp.dma_start(sent, dispatched_d.rearrange("(g p) d -> p g d", p=P)).then_inc(sent_loaded.sem, 16)
                for e in range(NE):
                    bo = O if e % 2 == 0 else Y
                    bo.wait_drained(sp, "experts", e // 2)
                    sp.dma_start(expert_out_d[e * CAP:(e + 1) * CAP, :].rearrange("(j p) d -> p j d", p=P),
                                 expert_out[:, 2 * e:2 * e + 2, :]).then_inc(stored.sem, 16)
            for b in range(NB):
                sp.wait_ge(x_done.sem, x_done.after(LAYERS[-1], 0, b))
                sp.dma_start(out[b].rearrange("(t p) d -> p t d", p=P), x[:, b * NT:(b + 1) * NT, :])\
                    .then_inc(out_done.sem, 16)
            sp.wait_ge(out_done.sem, 16 * NB)
            if len(LAYERS) < 8:
                sp.wait_ge(zeroed.sem, 16)
            for n in loaded:
                if loads[n]:
                    sp.wait_ge(loaded[n].sem, loads[n])

        @block.gpsimd
        def _(pool):
            for bk in BANKS:
                pool.sem_inc(bk.drained.sem, 1)
            k = [0]

            def step(ins):
                k[0] += 1
                ins.then_inc(pool_step.sem, 1)
                pool.wait_ge(pool_step.sem, k[0])

            pool.memset(ident[:, :], 0.0)
            pool.memset(minus_half[:, :], -0.5)
            pool.memset(eps5[:, :], EPS)
            pool.memset(eps12[:, :], EPS3)
            pool.memset(ones[:, :], 1.0)
            pool.memset(blk[:, :], 1.0)
            pool.memset(grid[:, :, :], 1.0)
            step(pool.memset(ctxT[:, :, :], 0.0))
            step(pool.affine_select(out=ident[:, :], in_=ident[:, :], compare_op=ALU.not_equal, fill=1.0, base=0,
                                    pattern=[[-1, P]], channel_multiplier=1))
            pool.tensor_copy(identb[:, :], ident[:, :])
            pool.memset(V2[:, :, :, 64], 1.0)
            step(pool.memset(causal[:, :], 0.0))
            step(pool.affine_select(out=causal[:, :], in_=causal[:, :], compare_op=ALU.is_ge, fill=-1e13, base=0,
                                    pattern=[[-1, CK]], channel_multiplier=1))
            step(pool.iota(iota8[:, :], pattern=[[1, NE]], base=0, channel_multiplier=0,
                           allow_small_or_imprecise_dtypes=True))
            step(pool.affine_select(out=blk[:, :], in_=blk[:, :], compare_op=ALU.is_ge, fill=0.0, base=0,
                                    pattern=[[-8, H16]], channel_multiplier=1))
            step(pool.affine_select(out=blk[:, :], in_=blk[:, :], compare_op=ALU.is_ge, fill=0.0, base=7,
                                    pattern=[[8, H16]], channel_multiplier=-1))
            step(pool.affine_select(out=grid[:, :, :], in_=grid[:, :, :], compare_op=ALU.is_ge, fill=0.0, base=0,
                                    pattern=[[P, 10], [-CK, H16]], channel_multiplier=1))
            step(pool.affine_select(out=grid[:, :, :], in_=grid[:, :, :], compare_op=ALU.is_ge, fill=0.0, base=CK - 1,
                                    pattern=[[-P, 10], [CK, H16]], channel_multiplier=-1))
            for c in range(10):
                q = [i for i, (cc, _) in enumerate(PIECES16) if cc == c]
                h0 = PIECES16[q[0]][1]
                last = pool.tensor_copy(V03[:, :, q[0]:q[0] + len(q), 8], spread(grid[:, c, h0:h0 + len(q)], 1, NB))
            last.then_inc(made.sem, 1)
            assert k[0] == POOL_STEPS, k
            pool.memset(hT[:, :, :], 0.0).then_inc(zeros_made.sem, 1)
            for L in LAYERS:
                if L in ATT:
                    run_attention(pool, "pool", L)
                if L == "L0f":
                    run_ffn0(pool, "pool")
                if L == "L1f":
                    run_ffn1(pool, "pool")
                if L == "L2f":
                    run_ffn2(pool, "pool")
                if L == "L3f":
                    route_constants_pool(pool)
                    run_ffn3(pool, "pool")

        @block.scalar
        def _(act):
            phase_act(act)
            for L in LAYERS:
                if L in ("L0x", "L3x"):
                    prep03_act(act, L)
                if L == "L1x":
                    prep1_act(act)
                if L == "L2x":
                    prep2_act(act)
                if L == "L0f":
                    prep_ffn0_act(act)
                if L in ATT:
                    run_attention(act, "act", L)
                if L == "L0f":
                    run_ffn0(act, "act")
                if L == "L1f":
                    run_ffn1(act, "act")
                if L == "L2f":
                    run_ffn2(act, "act")
                if L == "L3f":
                    run_ffn3(act, "act")

        @block.vector
        def _(dve):
            phase_dve(dve)
            for L in LAYERS:
                if L in ("L0x", "L3x"):
                    prep03_dve(dve, L)
                if L == "L1x":
                    prep1_dve(dve)
                if L == "L2x":
                    prep2_dve(dve)
                if L == "L0f":
                    prep_ffn0_dve(dve)
                if L == "L3x":
                    dve.wait_ge(loaded["mask3"].sem, LOADS["mask3"])
                    dve.tensor_scalar(mask3[:, :, :], mask_raw[:, :, :], 1.0, MASKED, ALU.is_equal, ALU.mult)\
                        .then_inc(mask_made.sem, 1)
                if L == "L1f":
                    dve.wait_ge(loaded["ffn1"].sem, LOADS["ffn1"])
                if L in ATT:
                    run_attention(dve, "dve", L)
                if L == "L0f":
                    run_ffn0(dve, "dve")
                if L == "L1f":
                    run_ffn1(dve, "dve")
                if L == "L2f":
                    run_ffn2(dve, "dve")
                if L == "L3f":
                    run_ffn3(dve, "dve")

        @block.tensor
        def _(pe):
            phase_pe(pe)
            for L in LAYERS:
                if L in ("L0x", "L3x"):
                    prep03_pe(pe, L)
                if L == "L1x":
                    prep1_pe(pe)
                if L == "L2x":
                    prep2_pe(pe)
                if L == "L0f":
                    prep_ffn0_pe(pe)
                if L == "L1x":
                    pe.wait_ge(mask_made.sem, 2 + NB)
                if L == "L3x":
                    pe.wait_ge(mask_made.sem, 3 + NB)
                if L == "L1f":
                    pe.wait_ge(loaded["ffn1"].sem, LOADS["ffn1"])
                if L in ATT:
                    run_attention(pe, "pe", L)
                if L == "L0f":
                    run_ffn0(pe, "pe")
                if L == "L1f":
                    run_ffn1(pe, "pe")
                if L == "L2f":
                    run_ffn2(pe, "pe")
                if L == "L3f":
                    run_ffn3(pe, "pe")


def phase_tables():
    side = 4
    w = np.zeros((H16, H16), np.float32)
    for i in range(H16):
        for j in range(i):
            dr, dc = j // side - i // side, j % side - i % side
            if abs(dr) <= 1 and abs(dc) <= 1:
                w[j, i] = math.exp(-math.hypot(dr, dc))
    f = np.asarray([[1.0 + 0.1 * h] for h in range(H16)], np.float32)
    return w, f


_INS = ['x', 'ctx_1024', 'mask_Bx1xSxS2_ik0', 'mask_Bx1xS2_bk0', 'mask_BxSxS2_ik1', 'L0_xattn_Wq', 'L0_xattn_Wk', 'L0_xattn_Wv', 'L0_xattn_out_w', 'L0_xattn_out_b', 'L0_xattn_coupling', 'L0_ffn_fast_b', 'L0_ffn_w_fc', 'L0_ffn_w_proj', 'L0_ffn_u', 'L0_ffn_v', 'L0_ffn_gate', 'L1_xattn_Wq', 'L1_xattn_Wk', 'L1_xattn_Wv', 'L1_xattn_Wo', 'L1_xattn_bo', 'L1_ffn_We', 'L1_ffn_be', 'L1_ffn_Wg', 'L1_ffn_bg', 'L2_xattn_Wq', 'L2_xattn_Wk', 'L2_xattn_Wv', 'L2_xattn_Wp', 'L2_xattn_bp', 'L2_ffn_ln_g', 'L2_ffn_ln_b', 'L2_ffn_attn_w', 'L2_ffn_attn_b', 'L2_ffn_w1', 'L2_ffn_b1', 'L2_ffn_w2', 'L2_ffn_b2', 'L2_ffn_next_w', 'L2_ffn_next_b', 'L3_xattn_wq', 'L3_xattn_wk', 'L3_xattn_wv', 'L3_xattn_w_out', 'L3_ffn_attn_nw', 'L3_ffn_attn_nb', 'L3_ffn_wg', 'L3_ffn_inter_w', 'L3_ffn_inter_b', 'L3_ffn_output_w', 'L3_ffn_output_b', 'L3_ffn_res_inter_w', 'L3_ffn_res_inter_b', 'L3_ffn_res_output_w', 'L3_ffn_res_output_b', 'L3_ffn_res_coef']


def kernel(**inputs):
    import numpy as _np
    import concourse.bacc as _bacc
    from concourse import mybir as _mybir
    from concourse.bass_utils import run_bass_kernel_spmd as _run

    nc = _bacc.Bacc("TRN2", target_bir_lowering=False, num_devices=1)
    arrays, args = {}, {}

    def give(name, a):
        arrays[f"in_{name}_dram"] = a
        args[name] = nc.dram_tensor(f"in_{name}_dram", a.shape, _mybir.dt.from_np(a.dtype), kind="ExternalInput").ap()

    for name in _INS:
        a = _np.ascontiguousarray(inputs[name])
        if a.dtype == _np.bool_:
            a = a.reshape(-1).view(_np.int32)
        if a.shape == ():
            a = a.reshape(1)
        give(name, a)
    w, f = phase_tables()
    give("phase_weights", w)
    give("phase_intrinsic", f)
    o = nc.dram_tensor("out_0_dram", (NB, NT * P, P), _mybir.dt.float32, kind="ExternalOutput").ap()
    four_layers(nc, args, o)
    r = _run(nc, [arrays], core_ids=[0])
    return r.results[0]["out_0_dram"]
```

```python
import math
from contextlib import ExitStack

import numpy as np

import concourse.bass as bass
from concourse import mybir

F32 = mybir.dt.float32
BF16 = mybir.dt.bfloat16
I32 = mybir.dt.int32
U32 = mybir.dt.uint32
U8 = mybir.dt.uint8
ALU = mybir.AluOpType
ACT = mybir.ActivationFunctionType
AX = mybir.AxisListType

P = 128
NB = 4
NT = 4
NTOK = NB * NT * P
CK = 77
NE = 8
FF = 512
NC = FF // P
CAP = NTOK // NE
EPS = 1e-5
EPS3 = 1e-12
MASKED = -float(2.0 ** 100)
TWO_PI = 2.0 * math.pi
ROUND = 1.5 * 2.0 ** 23

H16 = 16
BANK_HEADS = [(0, 6), (6, 12), (12, 16)]
ROWS16 = H16 * CK
CHUNKS16 = [(s, min(P, ROWS16 - s)) for s in range(0, ROWS16, P)]


def head_pieces(chunks):
    return [(c, h) for c, (s, n) in enumerate(chunks) for h in range(s // CK, (s + n - 1) // CK + 1)]


PIECES16 = head_pieces(CHUNKS16)
CHUNK_HEAD = [min(s // CK, H16 - 3) for s, _ in CHUNKS16]
PAD = P


class Event:

    def __init__(self, nc, ctx, name, credit=0):
        self.sem = ctx.enter_context(nc.semaphore(name))
        self.credit = credit
        self.total = credit
        self.base = {}

    def plan(self, phase, per, reps=1):
        self.base[phase] = (self.total, per)
        self.total += per * reps

    def after(self, phase, j=0, b=0):
        base, per = self.base[phase]
        return b * per + (base + j + 1)


class Bank:
    def __init__(self, nc, ctx, name):
        self.t = ctx.enter_context(nc.psum_tensor(name, [P, 512], F32))
        self.full = Event(nc, ctx, name + "_full")
        self.drained = Event(nc, ctx, name + "_drained", credit=1)

    def plan(self, phase, per, reps=1):
        self.full.plan(phase, per, reps)
        self.drained.plan(phase, per, reps)

    def wait_empty(self, pe, phase, j=0, b=0):
        pe.wait_ge(self.drained.sem, self.drained.after(phase, j - 1, b))

    def wait_full(self, eng, phase, j=0, b=0):
        eng.wait_ge(self.full.sem, self.full.after(phase, j, b))

    def wait_drained(self, eng, phase, j=0, b=0):
        eng.wait_ge(self.drained.sem, self.drained.after(phase, j, b))


def spread(ap, axis, n):
    v = ap.unsqueeze(axis)
    shape = list(v.shape)
    shape[axis] = n
    return v.broadcast_to(shape)


STOP = 8


def four_layers(nc, a, out):
    ctx = ExitStack()
    with ctx:
        def sb(name, shape, dt=F32):
            return ctx.enter_context(nc.sbuf_tensor(name, shape, dt))

        def event(name, credit=0):
            return Event(nc, ctx, name, credit)

        S = [Bank(nc, ctx, f"scores{i}") for i in range(3)]
        TB = [Bank(nc, ctx, f"probsT{i}") for i in range(2)]
        O = Bank(nc, ctx, "mixed")
        X = Bank(nc, ctx, "transposed")
        Y = Bank(nc, ctx, "result")
        BANKS = S + TB + [O, X, Y]

        x = sb("x", [P, NB * NT, P])
        xn = sb("xn", [P, NT, P])
        z = sb("z", [P, NT, P])
        xnT = sb("xnT", [P, NT * P])
        stats = sb("stats", [P, NT, 6])
        mv = sb("mv", [P, NT, 2])
        ve = sb("ve", [P, NT])
        rstd = sb("rstd", [P, NT])
        stats_z = sb("stats_z", [P, NT, 6])
        mv_z = sb("mv_z", [P, NT, 2])
        ve_z = sb("ve_z", [P, NT])
        rstd_z = sb("rstd_z", [P, NT])
        minus_half = sb("minus_half", [P, NT])
        eps5 = sb("eps5", [P, NT])
        eps12 = sb("eps12", [P, NT])
        prob = sb("prob", [P, NT, ROWS16])
        probT = sb("probT", [P, 10 * P])
        mx = sb("mx", [P, 2, H16])
        rden = sb("rden", [P, 2, H16])
        mix = sb("mix", [P, NT, P])
        mixT = sb("mixT", [P, NT * P])
        hT = sb("hT", [P, NC, 512])
        ident = sb("ident", [P, P])
        identb = sb("identb", [P, P], BF16)
        ones = sb("ones", [1, P])
        blk = sb("blk", [P, H16])
        grid = sb("grid", [P, 10, 3])
        key_of_row = sb("key_of_row", [P, 3 * CK])
        ctx_all = sb("ctx_tok", [P, NB, P])
        ctx_tok = ctx_all[0:CK, :, :]
        ctxT = sb("ctxT", [P, NB, PAD + CK + PAD])
        keysT = ctxT[:, :, PAD:PAD + CK]
        GA = sb("GA", [P, NB, H16, CK])
        GB = sb("GB", [P, NB, H16, CK])
        G2 = sb("G2", [P, NB, 2, CK])
        V03 = sb("V03", [P, NB, 10, 3, 9])
        V1 = sb("V1", [P, NB, 10, P])
        V2 = sb("V2", [P, NB, 2, 65])
        mask1 = sb("mask1", [P, NB * NT, CK], BF16)
        mask3 = sb("mask3", [P, NB * NT, CK], BF16)
        mask_raw = sb("mask_raw", [P, NB * NT, CK], I32)
        src_raw = sb("src_raw", [P, NB, CK], U8)
        src_bias = sb("src_bias", [P, NB, CK], BF16)
        causal = sb("causal", [P, CK])
        w0 = sb("w0", [P, 4, P])
        w3 = sb("w3", [P, 4, P])
        w2 = sb("w2", [P, 4, P])
        wT = sb("wT", [P, 3, P])
        out_wT = sb("out_wT", [P, 2, P])
        rows = sb("rows", [1, 6, P])
        head_bias = sb("head_bias", [P, H16])
        wfc = sb("wfc", [P, NC, P])
        wpr = sb("wpr", [P, NC * P])
        wt1 = sb("wt1", [P, NC, P])
        wt2 = sb("wt2", [P, NC, P])
        wfcT = sb("wfcT", [P, NC * P])
        wprT = sb("wprT", [P, NC, P])
        lr = sb("lr", [P, NC, 16])
        lrT = sb("lrT", [16, FF])
        fbT = sb("fbT", [16, 16])
        vlow = sb("vlow", [16, P])
        gate = sb("gate", [16, 1])
        bv = sb("bv", [16, P])
        wsc = sb("wsc", [P, 2, 16])
        we = sb("we", [P, NE, P])
        be = sb("be", [NE, P])
        wg1 = sb("wg1", [P, NE])
        bg1 = sb("bg1", [P, NE])
        attn_w = sb("attn_w", [P, P])
        next_w = sb("next_w", [P, P])
        cols2 = sb("cols2", [P, 3])
        b1c = sb("b1c", [P, NE, NC])
        b2c = sb("b2c", [P, NE])
        big = sb("big", [P, 2, NE * FF])
        iota8 = sb("iota8", [P, NE])
        ph = sb("ph", [H16, 24])
        phw = sb("phw", [H16, H16 + 2])
        dg = sb("dg", [H16, H16])
        ones16 = sb("ones16", [H16, P])
        gsel = sb("gsel", [P, NT, NE])
        gT = sb("gT", [NE, NT * P])
        a2 = sb("a2", [P, 2, P])
        xaT = wt1[:, :, :].rearrange("p c d -> p (c d)")
        gout = wt2[:, :, :].rearrange("p c d -> p (c d)")

        wgc = sb("wgc", [P, NE + 2])
        cols3 = sb("cols3", [P, 2 + NC])
        route = ctx_all[:, :, :].rearrange("p b d -> p (b d)")
        earlier = route[:, 0:64].bitcast(BF16)
        onesb = route[:, 64:128].bitcast(BF16)
        chosen = route[:, 128:192].bitcast(BF16).rearrange("p (g e) -> p g e", e=NE)
        expert_of, weight_of, coef0, place, kept, slot = (route[:, 192 + 16 * i:208 + 16 * i] for i in range(6))
        slot_put = route[:, 288:304].bitcast(U32)
        slot_get = route[:, 304:320].bitcast(U32)
        dropped = route[:, 448:464]
        counted = route[:, 320:448].rearrange("p (g e) -> p g e", e=NE)
        v1f = V1[:, :, :, :].rearrange("p b c d -> p (b c d)")
        gbf = GB[:, :, :, :].rearrange("p b h k -> p (b h k)")
        normed = v1f[:, 0:2048].rearrange("p (g d) -> p g d", d=P)
        expert_out = v1f[:, 2048:4096].rearrange("p (g d) -> p g d", d=P)
        nw_all, nb_all = v1f[:, 4096:4224], v1f[:, 4224:4352]
        sent = gbf[:, 0:2048].rearrange("p (g d) -> p g d", d=P)
        sentT = gbf[:, 2048:4096]
        got = prob[:, :, :].rearrange("p t n -> p (t n)")[:, 0:2048].rearrange("p (g d) -> p g d", d=P)
        res_w1 = w0[:, :, :].rearrange("p c d -> p (c d)")
        res_w2 = w2
        out_b_all = GA[:, :, :, :].rearrange("p b h k -> p (b h k)")[:, 0:NE * P].rearrange("p (e d) -> p e d", d=P)
        dispatched_d = nc.dram_tensor("dispatched", [NTOK, P], F32, kind="Internal").ap()
        expert_out_d = nc.dram_tensor("expert_out", [NTOK, P], F32, kind="Internal").ap()

        w1q = big[:, 0, 0:1024].rearrange("p (c d) -> p c d", c=8)
        w1k = big[:, 0, 1024:2048].rearrange("p (c d) -> p c d", c=8)
        w1v = big[:, 0, 2048:3072].rearrange("p (c d) -> p c d", c=8)
        w1o = big[:, 0, 3072:4096]
        w1oT = big[:, 1, 0:1024].rearrange("p (c d) -> p c d", c=8)
        head_mat = big[:, 1, 1024:3072].rearrange("p (q c d) -> p q c d", q=2, c=8)

        loaded = {}
        for n in ("x", "const", "w0", "ctx", "mask1", "mask3", "ffn0", "attn1", "ffn1", "attn2", "ffn2", "attn3", "small3", "ffn3"):
            loaded[n] = event("loaded_" + n)
        made = event("constants_made")
        rep_made = event("key_of_row_made")
        grid_made = event("grid_made")
        lhs_ready = event("tiles_staged")
        selected = event("gates_selected")
        pool_sum = event("pool_sum", credit=6)
        pool_step = event("pool_step")
        stats_ready = event("stats_ready")
        passed = event("passed")
        pool_passed = event("pool_passed")
        mv_ready = event("mv_ready")
        ve_ready = event("ve_ready")
        rstd_ready = event("rstd_ready")
        xn_ready = event("xn_ready")
        z_ready = event("z_ready")
        max_ready = event("max_ready")
        exp_ready = event("exp_ready")
        den_ready = event("den_ready")
        scaled_ready = event("scaled_ready")
        square_ready = [event(f"square_ready{c}") for c in range(NC)]
        dve_prep = event("dve_prep")
        act_prep = event("act_prep")
        out_done = event("out_done")
        x_done = event("x_done")
        gelu_ready = event("gelu_ready")
        gate_step = event("gate_step")
        gate_exp = event("gate_exp")
        xa_ready = event("xa_ready")
        chain = event("chain")
        mask_made = event("mask_made")
        zeroed = event("dispatched_zeroed")
        zeros_made = event("zeros_made")
        base_added = event("base_added")
        normed_ready = event("normed_ready", credit=2)
        res_step = event("res_step")
        res_exp = event("res_exp")
        route_made = event("route_made")
        route_step = event("route_step")
        scattered = event("scattered")
        sent_loaded = event("sent_loaded")
        stored = event("expert_out_stored")
        gathered = [event(f"gathered{b}") for b in range(NB)]
        tern_scale = event("ternary_scale")
        tern = event("ternary_step")

        loads = {n: 0 for n in loaded}

        def load(eng, group, dst, src, **kw):
            loads[group] += 16
            eng.dma_start(dst, src, **kw).then_inc(loaded[group].sem, 16)

        ATT = {
            "L0x": dict(H=16, G=GA, V=V03, dv=8, scale=8 ** -0.5, mask=None, row=0, wout=w0[:, 3, :], fold=False, bias=True),
            "L1x": dict(H=16, G=GB, V=V1, dv=P, scale=64 ** -0.5, mask=mask1, row=1, wout=None, fold=True, bias=False),
            "L2x": dict(H=2, G=G2, V=V2, dv=64, scale=64 ** -0.5, mask="causal", row=2, wout=out_wT[:, 0, :], fold=False, bias=False),
            "L3x": dict(H=16, G=GA, V=V03, dv=8, scale=8 ** -0.5, mask=mask3, row=None, wout=out_wT[:, 1, :], fold=False, bias=False),
        }
        LAYERS = ["L0x", "L0f", "L1x", "L1f", "L2x", "L2f", "L3x", "L3f"][:STOP]

        def plan_norm(L):
            for e in (stats_ready, mv_ready, ve_ready, rstd_ready):
                e.plan(L, 2 if L in ("L2f", "L3f") else 1, NB)
            xn_ready.plan(L, 1, NB)
            if L in ("L2f", "L3f"):
                z_ready.plan(L, 1, NB)

        def plan_attention(L):
            c = ATT[L]
            plan_norm(L)
            if c["H"] == 2:
                for bk in (S[0], S[1], S[2], TB[0], TB[1], X, Y):
                    bk.plan(L, 1, NB)
                O.plan(L, 2, NB)
                for e in (max_ready, exp_ready, den_ready):
                    e.plan(L, 2, NB)
                x_done.plan(L, 1, NB)
                return
            for bk in S:
                bk.plan(L, NT, NB)
            TB[0].plan(L, 2 * NT, NB)
            TB[1].plan(L, NT, NB)
            max_ready.plan(L, 3 if c["bias"] else 1, NB * NT)
            exp_ready.plan(L, NT, NB)
            den_ready.plan(L, 2 if c["fold"] else 1, NB * NT)
            if c["fold"]:
                scaled_ready.plan(L, NT, NB)
                O.plan(L, 2, NB); Y.plan(L, 2, NB); X.plan(L, 1, NB)
            else:
                O.plan(L, NT + 1, NB); Y.plan(L, 1, NB); X.plan(L, 1, NB)
            x_done.plan(L, 1, NB)

        def prev_of(L, b):
            i = LAYERS.index(L)
            return None if i == 0 else LAYERS[i - 1]

        INNER = {"L2f", "L3f"}

        def ln_stats_dve(dve, L, b, j=0, stats=stats, mv=mv):
            if j == 0:
                p = prev_of(L, b)
                if p is None:
                    dve.wait_ge(loaded["x"].sem, 16)
                else:
                    dve.wait_ge(x_done.sem, x_done.after(p, 0, b))
            else:
                dve.wait_ge(xn_ready.sem, xn_ready.after(L, 0, b))
            for t in range(NT):
                last = dve.bn_stats(stats[:, t, :], x[:, b * NT + t, :] if j == 0 else xn[:, t, :])
            last.then_inc(stats_ready.sem, 1)
            dve.wait_ge(stats_ready.sem, stats_ready.after(L, j, b))
            dve.sem_inc(passed.sem, 1)
            for t in range(NT):
                last = dve.bn_aggr(mv[:, t, :], stats[:, t, :])
            last.then_inc(mv_ready.sem, 1)

        def ln_rstd_pool(pool, L, b, j=0, mv=mv, ve=ve, rstd=rstd):
            eps = eps12 if (L == "L3f" and j == 1) else eps5
            pool.wait_ge(mv_ready.sem, mv_ready.after(L, j, b))
            pool.tensor_tensor(ve[:, :], mv[:, :, 1], eps[:, :], ALU.add).then_inc(ve_ready.sem, 1)
            pool.wait_ge(ve_ready.sem, ve_ready.after(L, j, b))
            pool.tensor_tensor(rstd[:, :], ve[:, :], minus_half[:, :], ALU.pow).then_inc(rstd_ready.sem, 1)

        def ln_apply_dve(dve, L, b, j=0, mv=mv, rstd=rstd):
            dve.wait_ge(rstd_ready.sem, rstd_ready.after(L, j, b))
            if j == 0:
                wait_xn_free(dve, L, b)
            src = (lambda t: x[:, b * NT + t, :]) if j == 0 else (lambda t: xn[:, t, :])
            dst, ev = (xn, xn_ready) if j == 0 else (z, z_ready)
            for t in range(NT):
                last = dve.tensor_scalar(dst[:, t, :], src(t), mv[:, t, 0:1], rstd[:, t:t + 1],
                                         ALU.subtract, ALU.mult)
            last.then_inc(ev.sem, 1)

        def wait_xn_free(dve, L, b):
            xt = XT_UNIT[L]
            if isinstance(b, int) and b == 0:
                i = LAYERS.index(L)
                if i:
                    q = LAYERS[i - 1]
                    X.wait_full(dve, q, XT_UNIT[q], NB - 1)
            else:
                X.wait_full(dve, L, xt, b - 1)

        XT_UNIT = {L: 0 for L in LAYERS}

        def front_dve(dve, L, b):
            for j in range(2 if L in INNER else 1):
                ln_stats_dve(dve, L, b, j)
                ln_apply_dve(dve, L, b, j)

        def front_pool(pool, L, b):
            for j in range(2 if L in INNER else 1):
                ln_rstd_pool(pool, L, b, j)

        def early_norm(eng, name, L):
            i = LAYERS.index(L) + 1
            if i == len(LAYERS) or name not in ("dve", "pool"):
                return
            if LAYERS[i] != "L3f":
                (front_dve if name == "dve" else front_pool)(eng, LAYERS[i], 0)
            elif name == "dve":
                ffn3_stats(eng, 0, 0)
                ffn3_base(eng, 0)
            else:
                ffn3_rstd(eng, 0, 0)

        def front_pe(pe, L, b):
            pe.wait_ge(xn_ready.sem, xn_ready.after(L, 0, b))
            X.wait_empty(pe, L, XT_UNIT[L], b)
            for t in range(NT):
                last = pe.transpose(X.t[:, t * P:(t + 1) * P], xn[:, t, :], ident[:, :])
            last.then_inc(X.full.sem, 1)

        def front_act(act, L, b, free=None):
            X.wait_full(act, L, XT_UNIT[L], b)
            if free is not None:
                free(act)
            act.activation(xnT[:, :], X.t[:, :], ACT.Copy).then_inc(X.drained.sem, 1)

        def scores_pe(pe, L, b, t, banks=(0, 1, 2)):
            c = ATT[L]
            if t == 0 and 0 in banks:
                X.wait_drained(pe, L, 0, b)
            lhs = xnT[:, t * P:(t + 1) * P]
            for j in banks:
                h0, h1 = BANK_HEADS[j]
                n = (h1 - h0) * CK
                S[j].wait_empty(pe, L, t, b)
                o = S[j].t[:, 0:n]
                if c["mask"] is not None:
                    pe.matmul(o, identb[:, :], spread(c["mask"][:, b * NT + t, :], 1, h1 - h0),
                              start=True, stop=False)
                pe.matmul(o, lhs, c["G"][:, b, h0:h1, :], start=c["mask"] is None, stop=True)\
                    .then_inc(S[j].full.sem, 1)

        def shift_dve(dve, L, b, t):
            c = ATT[L]
            k = 3 if c["bias"] else 1
            m = mx[:, t % 2, :]
            parts = [(S[j], h0, h1) for j, (h0, h1) in enumerate(BANK_HEADS)]
            for bk, h0, h1 in parts:
                bk.wait_full(dve, L, t, b)
                last = dve.tensor_reduce(m[:, h0:h1], bk.t[:, 0:(h1 - h0) * CK].rearrange("p (h k) -> p h k", k=CK),
                                         AX.X, ALU.max)
            last.then_inc(max_ready.sem, 1)
            dve.wait_ge(max_ready.sem, max_ready.after(L, k * t, 0) + b * (k * NT))
            if c["bias"]:
                dve.tensor_tensor(m, m, head_bias[:, :], ALU.add).then_inc(max_ready.sem, 1)
                dve.wait_ge(max_ready.sem, max_ready.after(L, k * t + 1, 0) + b * (k * NT))
                dve.tensor_tensor(m, m, head_bias[:, :], ALU.subtract).then_inc(max_ready.sem, 1)
                dve.wait_ge(max_ready.sem, max_ready.after(L, k * t + 2, 0) + b * (k * NT))
            for bk, h0, h1 in parts:
                dve.tensor_tensor(prob[:, t, h0 * CK:h1 * CK].rearrange("p (h k) -> p h k", k=CK),
                                  bk.t[:, 0:(h1 - h0) * CK].rearrange("p (h k) -> p h k", k=CK),
                                  spread(m[:, h0:h1], 2, CK), ALU.subtract).then_inc(bk.drained.sem, 1)

        def exp_act(act, L, b, t):
            c = ATT[L]
            S[2].wait_drained(act, L, t, b)
            act.activation(prob[:, t, :], prob[:, t, :], ACT.Exp, scale=c["scale"]).then_inc(exp_ready.sem, 1)

        def normalise_dve(dve, L, b, t):
            dve.wait_ge(exp_ready.sem, exp_ready.after(L, t, b))
            r = rden[:, t % 2, :]
            dve.tensor_reduce(r, prob[:, t, :].rearrange("p (h k) -> p h k", k=CK), AX.X, ALU.add)\
                .then_inc(den_ready.sem, 1)
            dve.wait_ge(den_ready.sem, den_ready.after(L, 2 * t, 0) + b * (2 * NT))
            dve.reciprocal(r, r).then_inc(den_ready.sem, 1)

        def normalise_pool(pool, L, b, t):
            pool.wait_ge(den_ready.sem, den_ready.after(L, 2 * t + 1, 0) + b * (2 * NT))
            v = prob[:, t, :].rearrange("p (h k) -> p h k", k=CK)
            pool.tensor_tensor(v, v, spread(rden[:, t % 2, :], 2, CK), ALU.mult).then_inc(scaled_ready.sem, 1)

        def t_units(L, t):
            return [(TB[0], 2 * t, 0, 4), (TB[1], t, 4, 8), (TB[0], 2 * t + 1, 8, 10)]

        def transposes_pe(pe, L, b, t, units):
            c = ATT[L]
            chunks = CHUNKS16
            if 0 not in units:
                pass
            elif c["fold"]:
                pe.wait_ge(scaled_ready.sem, scaled_ready.after(L, t, b))
            else:
                pe.wait_ge(exp_ready.sem, exp_ready.after(L, t, b))
            for k in units:
                bk, u, c0, c1 = t_units(L, t)[k]
                bk.wait_empty(pe, L, u, b)
                for i in range(c0, c1):
                    s, n = chunks[i]
                    last = pe.transpose(bk.t[0:n, (i - c0) * P:(i - c0 + 1) * P], prob[:, t, s:s + n], ident[:, :])
                last.then_inc(bk.full.sem, 1)

        def mix_pe(pe, L, b, t):
            c = ATT[L]
            chunks = CHUNKS16
            first = True
            if c["fold"]:
                dst, u = (O, Y)[t % 2], t // 2
                dst.wait_empty(pe, L, u, b)
                pe.matmul(dst.t[:, 0:P], ones[0:1, :], rows[0:1, c["row"], :], start=True, stop=False)
                for bk, tu, c0, c1 in t_units(L, t):
                    bk.wait_drained(pe, L, tu, b)
                    for i in range(c0, c1):
                        n = chunks[i][1]
                        last = pe.matmul(dst.t[:, 0:P], probT[0:n, i * P:(i + 1) * P], c["V"][0:n, b, i, :],
                                         start=False, stop=i == len(chunks) - 1)
                last.then_inc(dst.full.sem, 1)
            else:
                w = c["dv"] + 1
                O.wait_empty(pe, L, t, b)
                for bk, tu, c0, c1 in t_units(L, t):
                    bk.wait_drained(pe, L, tu, b)
                    for i in range(c0, c1):
                        n = chunks[i][1]
                        h0 = CHUNK_HEAD[i]
                        last = pe.matmul(O.t[:, h0 * w:(h0 + 3) * w], probT[0:n, i * P:(i + 1) * P],
                                         c["V"][0:n, b, i, :, :],
                                         start=first, stop=i == len(chunks) - 1, skip_group_check=True)
                        first = False
                last.then_inc(O.full.sem, 1)

        def probT_act(act, L, b, t, units=(0,)):
            c = ATT[L]
            for k in units:
                bk, u, c0, c1 = t_units(L, t)[k]
                bk.wait_full(act, L, u, b)
                if c1 == 10:
                    r = CHUNKS16[9][1]
                    act.activation(probT[:, c0 * P:(c0 + 1) * P], bk.t[:, 0:P], ACT.Copy)
                    act.activation(probT[0:r, (c0 + 1) * P:c1 * P], bk.t[0:r, P:2 * P], ACT.Copy)\
                        .then_inc(bk.drained.sem, 1)
                else:
                    act.activation(probT[:, c0 * P:c1 * P], bk.t[:, 0:(c1 - c0) * P], ACT.Copy)\
                        .then_inc(bk.drained.sem, 1)

        def mixed_dve(dve, L, b, t):
            c = ATT[L]
            if c["fold"]:
                bk, u = (O, Y)[t % 2], t // 2
                bk.wait_full(dve, L, u, b)
                ins = dve.tensor_tensor(x[:, b * NT + t, :], x[:, b * NT + t, :], bk.t[:, 0:P], ALU.add)
                ins.then_inc(bk.drained.sem, 1)
                return
            H, dv = c["H"], c["dv"]
            O.wait_full(dve, L, t, b)
            v = O.t[:, 0:H * (dv + 1)].rearrange("p (h e) -> p h e", e=dv + 1)
            r = rden[:, t % 2, 0:H]
            dve.reciprocal(r, v[:, :, dv]).then_inc(den_ready.sem, 1)
            dve.wait_ge(den_ready.sem, den_ready.after(L, t, 0) + b * NT)
            dve.tensor_tensor(mix[:, t, :].rearrange("p (h e) -> p h e", e=dv), v[:, :, 0:dv],
                              spread(r, 2, dv), ALU.mult).then_inc(O.drained.sem, 1)

        def tail_transposes_pe(pe, L, b, done=NT - 1):
            O.wait_drained(pe, L, done, b)
            for t in range(NT):
                last = pe.transpose(O.t[:, t * P:(t + 1) * P], mix[:, t, :], ident[:, :])
            last.then_inc(O.full.sem, 1)

        def tail_bias_pe(pe, L, b):
            c = ATT[L]
            Y.wait_empty(pe, L, 0, b)
            if c["row"] is not None:
                pe.matmul(Y.t[:, :], ones[0:1, :], spread(rows[0:1, c["row"], :], 1, NT), start=True, stop=False,
                          skip_group_check=True)

        def tail_project_pe(pe, L, b, unit=NT):
            c = ATT[L]
            O.wait_drained(pe, L, unit, b)
            for t in range(NT):
                last = pe.matmul(Y.t[:, t * P:(t + 1) * P], mixT[:, t * P:(t + 1) * P], c["wout"],
                                 start=c["row"] is None and t == 0, stop=t == NT - 1, skip_group_check=True)
            last.then_inc(Y.full.sem, 1)

        def tail_act(act, L, b, unit=NT):
            O.wait_full(act, L, unit, b)
            act.activation(mixT[:, :], O.t[:, :], ACT.Copy).then_inc(O.drained.sem, 1)

        def tail_dve(dve, L, b):
            if ATT[L]["fold"]:
                dve.wait_ge(Y.drained.sem, Y.drained.after(L, 1, b))
                dve.wait_ge(O.drained.sem, O.drained.after(L, 1, b))
                dve.sem_inc(x_done.sem, 1)
                return
            Y.wait_full(dve, L, 0, b)
            xb = x[:, bass.ds(b * NT, NT), :] if not isinstance(b, int) else x[:, b * NT:(b + 1) * NT, :]
            dve.tensor_tensor(xb, xb, Y.t[:, :].rearrange("p (t d) -> p t d", t=NT), ALU.add)\
                .then_inc(Y.drained.sem, 1)
            dve.wait_ge(Y.drained.sem, Y.drained.after(L, 0, b))
            dve.sem_inc(x_done.sem, 1)

        def attention_step(eng, name, L, b, t, before=None, ahead=None, front=None, stats=None, tail=None):
            fold = ATT[L]["fold"]
            if name == "pe":
                transposes_pe(eng, L, b, t, (0, 1))
                if front is not None:
                    front_pe(eng, L, front)
                if ahead is not None:
                    scores_pe(eng, L, *ahead, (0,))
                if tail is not None:
                    tail_transposes_pe(eng, L, tail)
                if ahead is not None:
                    scores_pe(eng, L, *ahead, (1, 2))
                transposes_pe(eng, L, b, t, (2,))
                if tail is not None:
                    tail_bias_pe(eng, L, tail)
                    tail_project_pe(eng, L, tail)
                mix_pe(eng, L, b, t)
            elif name == "act":
                probT_act(eng, L, b, t, (0, 1))
                if front is not None:
                    front_act(eng, L, front)
                if tail is not None:
                    tail_act(eng, L, tail)
                probT_act(eng, L, b, t, (2,))
                if ahead is not None:
                    exp_act(eng, L, *ahead)
            elif name == "dve":
                if before is not None:
                    mixed_dve(eng, L, *before)
                    if fold and before[1] == NT - 1:
                        tail_dve(eng, L, before[0])
                if stats is not None:
                    ln_stats_dve(eng, L, stats)
                if fold:
                    if t < NT - 1:
                        normalise_dve(eng, L, b, t + 1)
                    elif ahead is not None:
                        normalise_dve(eng, L, b + 1, 0)
                if ahead is not None:
                    shift_dve(eng, L, *ahead)
                if stats is not None:
                    ln_apply_dve(eng, L, stats)
                if tail is not None and not fold:
                    tail_dve(eng, L, tail)
            elif name == "pool":
                if stats is not None:
                    ln_rstd_pool(eng, L, stats)
                if fold:
                    if t < NT - 1:
                        normalise_pool(eng, L, b, t + 1)
                    elif ahead is not None:
                        normalise_pool(eng, L, b + 1, 0)

        def prepared_pe(pe, L):
            for bk in BANKS:
                if "prep" + L in bk.drained.base:
                    bk.wait_drained(pe, "prep" + L, bk.drained.base["prep" + L][1] - 1)

        def run_attention16(eng, name, L):
            fold = ATT[L]["fold"]
            head = {"pe": scores_pe, "dve": shift_dve, "act": exp_act}.get(name)
            if name in ("pe", "act") or (name == "pool" and L == LAYERS[0]):
                fronts(eng, name, L, 0)
            for t in range(2):
                if head:
                    head(eng, L, 0, t)
            if fold and name in ("dve", "pool"):
                (normalise_dve if name == "dve" else normalise_pool)(eng, L, 0, 0)
            if L == "L1x" and name != "pool":
                {"pe": folded_values_pe, "act": folded_values_act, "dve": folded_values_dve}[name](eng)
            if L == "L3x" and name in ("pe", "act"):
                for part in range(5, PREP03_PARTS):
                    {"pe": prep03_pe, "act": prep03_act}[name](eng, L, part)
            if L != "L0x" and name == "pe":
                prepared_pe(eng, L)
            attention_step(eng, name, L, 0, 0, ahead=(0, 2))
            with eng.Fori(0, NB - 1) as b:
                attention_step(eng, name, L, b, 1, before=(b, 0), ahead=(b, 3), stats=b + 1)
                attention_step(eng, name, L, b, 2, before=(b, 1), ahead=(b + 1, 0), front=b + 1)
                attention_step(eng, name, L, b, 3, before=(b, 2), ahead=(b + 1, 1))
                attention_step(eng, name, L, b + 1, 0, before=(b, 3), ahead=(b + 1, 2),
                               tail=None if fold else b)
            b = NB - 1
            attention_step(eng, name, L, b, 1, before=(b, 0), ahead=(b, 3))
            attention_step(eng, name, L, b, 2, before=(b, 1))
            if name == "pool" and L == "L0x":
                ternary_pool(eng)
            early_norm(eng, name, L)
            attention_step(eng, name, L, b, 3, before=(b, 2))
            if name == "dve":
                mixed_dve(eng, L, b, 3)
                tail_dve(eng, L, b)
            elif not fold and name == "pe":
                tail_bias_pe(eng, L, b)
                tail_transposes_pe(eng, L, b)
                tail_project_pe(eng, L, b)
            elif not fold and name == "act":
                tail_act(eng, L, b)

        PAIR_OUT = (O, S[2])

        def pair_scores_pe(pe, b, i):
            L = "L2x"
            if i == 0:
                X.wait_drained(pe, L, 0, b)
            bk = S[i]
            bk.wait_empty(pe, L, 0, b)
            for u in range(2):
                t = 2 * i + u
                o = bk.t[:, u * 2 * CK:(u + 1) * 2 * CK]
                if t == 0:
                    pe.matmul(o, ident[:, :], spread(causal[:, :], 1, 2), start=True, stop=False)
                last = pe.matmul(o, xnT[:, t * P:(t + 1) * P], G2[:, b, :, :], start=t != 0, stop=True)
            last.then_inc(bk.full.sem, 1)

        def pair_shift_dve(dve, b, i):
            L = "L2x"
            S[i].wait_full(dve, L, 0, b)
            v = S[i].t[:, 0:4 * CK].rearrange("p (q k) -> p q k", k=CK)
            m = mx[:, i, 0:4]
            dve.tensor_reduce(m, v, AX.X, ALU.max).then_inc(max_ready.sem, 1)
            dve.wait_ge(max_ready.sem, max_ready.after(L, i, b))
            dve.tensor_tensor(prob[:, i, 0:4 * CK].rearrange("p (q k) -> p q k", k=CK), v, spread(m, 2, CK),
                              ALU.subtract).then_inc(S[i].drained.sem, 1)

        def pair_exp_act(act, b, i):
            S[i].wait_drained(act, "L2x", 0, b)
            act.activation(prob[:, i, 0:4 * CK], prob[:, i, 0:4 * CK], ACT.Exp, scale=ATT["L2x"]["scale"])\
                .then_inc(exp_ready.sem, 1)

        def pair_transposes_pe(pe, b, i):
            L = "L2x"
            pe.wait_ge(exp_ready.sem, exp_ready.after(L, i, b))
            TB[i].wait_empty(pe, L, 0, b)
            for q in range(4):
                last = pe.transpose(TB[i].t[0:CK, q * P:(q + 1) * P], prob[:, i, q * CK:(q + 1) * CK], ident[:, :])
            last.then_inc(TB[i].full.sem, 1)

        def pair_probT_act(act, b, i):
            TB[i].wait_full(act, "L2x", 0, b)
            act.activation(probT[0:CK, i * 512:(i + 1) * 512], TB[i].t[0:CK, :], ACT.Copy)\
                .then_inc(TB[i].drained.sem, 1)

        def pair_mix_pe(pe, b, i):
            L = "L2x"
            bk = PAIR_OUT[i]
            TB[i].wait_drained(pe, L, 0, b)
            bk.wait_empty(pe, L, 0, b)
            for q in range(4):
                last = pe.matmul(bk.t[:, q * 65:(q + 1) * 65], probT[0:CK, (4 * i + q) * P:(4 * i + q + 1) * P],
                                 V2[0:CK, b, q % 2, :], start=True, stop=True)
            last.then_inc(bk.full.sem, 1)

        def pair_mixed_dve(dve, b, i):
            L = "L2x"
            bk = PAIR_OUT[i]
            bk.wait_full(dve, L, 0, b)
            v = bk.t[:, 0:260].rearrange("p (q e) -> p q e", e=65)
            r = rden[:, i, 0:4]
            dve.reciprocal(r, v[:, :, 64]).then_inc(den_ready.sem, 1)
            dve.wait_ge(den_ready.sem, den_ready.after(L, i, b))
            dve.tensor_tensor(mix[:, 2 * i:2 * i + 2, :].rearrange("p t (h e) -> p (t h) e", e=64), v[:, :, 0:64],
                              spread(r, 2, 64), ALU.mult).then_inc(bk.drained.sem, 1)

        def run_attention2(eng, name):
            L = "L2x"

            def scores(b):
                for i in range(2):
                    if name == "pe":
                        pair_scores_pe(eng, b, i)
                    elif name == "dve":
                        pair_shift_dve(eng, b, i)
                    elif name == "act":
                        pair_exp_act(eng, b, i)

            def step(b, nxt=True, norm=True):
                if name == "pe":
                    for i in range(2):
                        pair_transposes_pe(eng, b, i)
                    if nxt:
                        scores(b + 1)
                    for i in range(2):
                        pair_mix_pe(eng, b, i)
                    S[2].wait_drained(eng, L, 0, b)
                    tail_transposes_pe(eng, L, b, 0)
                    tail_bias_pe(eng, L, b)
                    if norm:
                        front_pe(eng, L, b + 2)
                    tail_project_pe(eng, L, b, 1)
                elif name == "act":
                    for i in range(2):
                        pair_probT_act(eng, b, i)
                    if nxt:
                        scores(b + 1)
                    tail_act(eng, L, b, 1)
                    if norm:
                        front_act(eng, L, b + 2)
                elif name == "dve":
                    if nxt:
                        scores(b + 1)
                    if norm:
                        ln_stats_dve(eng, L, b + 2)
                    for i in range(2):
                        pair_mixed_dve(eng, b, i)
                    if norm:
                        ln_apply_dve(eng, L, b + 2)
                    if not nxt:
                        early_norm(eng, name, L)
                    tail_dve(eng, L, b)
                elif norm:
                    front_pool(eng, L, b + 2)
                elif not nxt:
                    early_norm(eng, name, L)

            if name in ("pe", "act"):
                fronts(eng, name, L, 0)
            if name in ("dve", "pool"):
                fronts(eng, name, L, 1)
            scores(0)
            if name in ("pe", "act"):
                fronts(eng, name, L, 1)
            with eng.Fori(0, NB - 2) as b:
                step(b)
            step(NB - 2, norm=False)
            step(NB - 1, nxt=False, norm=False)

        def run_attention(eng, name, L):
            if L == "L2x":
                run_attention2(eng, name)
            else:
                run_attention16(eng, name, L)

        WINDOW = lambda b, c, h, n: ctxT[:, b, PAD + P * c - CK * h:PAD + P * c - CK * h + n]

        PREP03_PARTS = 8
        values = probT[0:CK, 0:NB * P].rearrange("p (b d) -> p b d", b=NB)

        G_BANKS = {"L0x": [(S[0], 0), (S[1], 0), (S[2], 0)], "L3x": [(O, 0), (Y, 1), (TB[1], 0)]}

        KEYS_BY_HEAD = {"L0x": prob, "L3x": GB[:, :, :, :].rearrange("p b h k -> p b (h k)")}

        def plan_prep03(L):
            X.plan("prep" + L, 2)
            if L == "L0x":
                O.plan("prep" + L, 1)
                Y.plan("prep" + L, 1)
            else:
                Y.plan("prep" + L, 1 + NB)
            for bk, u in G_BANKS[L]:
                if bk is not Y:
                    bk.plan("prep" + L, NB)
            TB[0].plan("prep" + L, 2)
            dve_prep.plan("prep" + L, NB)

        def prep03_pe(pe, L, part):
            ph_ = "prep" + L
            first = L == "L0x"
            wk, wq, wv = (w0[:, 1, :], wT[:, 0, :], w0[:, 2, :]) if first else (wT[:, 1, :], w3[:, 0, :], wT[:, 2, :])
            if part == 0:
                X.wait_empty(pe, ph_, 0)
                if first:
                    pe.wait_ge(made.sem, MADE)
                    pe.wait_ge(loaded["ctx"].sem, 16)
                    for b in range(NB):
                        last = pe.transpose(X.t[:, b * CK:(b + 1) * CK], ctx_tok[:, b, :], ident[0:CK, 0:CK])
                else:
                    pe.wait_ge(loaded["attn3"].sem, LOADS["attn3"])
                    for i in range(3):
                        last = pe.transpose(X.t[:, i * P:(i + 1) * P], w3[:, 1 + i, :], ident[:, :])
                last.then_inc(X.full.sem, 1)
                if first:
                    pe.wait_ge(loaded["w0"].sem, LOADS["w0"])
                    O.wait_empty(pe, ph_, 0)
                    pe.transpose(O.t[:, 0:P], w0[:, 0, :], ident[:, :]).then_inc(O.full.sem, 1)
            elif part == 1:
                Y.wait_empty(pe, ph_, 0)
                X.wait_drained(pe, ph_, 0)
                pe.matmul(Y.t[:, 0:NB * CK], wk, keysT, start=True, stop=True).then_inc(Y.full.sem, 1)
                TB[0].wait_empty(pe, ph_, 0)
                for b in range(NB):
                    last = pe.matmul(TB[0].t[0:CK, b * P:(b + 1) * P], keysT[:, b, :], wv, start=True, stop=True)
                last.then_inc(TB[0].full.sem, 1)
            elif part in (2, 3):
                bk, u = (TB[0], 1) if part == 2 else (X, 1)
                TB[0].wait_drained(pe, ph_, 0)
                bk.wait_empty(pe, ph_, u)
                if part == 2:
                    pe.wait_ge(rep_made.sem, 1)
                for i in range(5):
                    c = 5 * (part - 2) + i
                    k0, h0 = CHUNKS16[c][0] % CK, CHUNK_HEAD[c]
                    last = pe.matmul(bk.t[:, i * 96:(i + 1) * 96], key_of_row[0:CK, k0:k0 + P],
                                     values[:, :, h0 * 8:(h0 + 3) * 8], start=True, stop=True)
                last.then_inc(bk.full.sem, 1)
            else:
                b = part - 4
                if b == 0 and first:
                    O.wait_drained(pe, ph_, 0)
                pe.wait_ge(dve_prep.sem, dve_prep.after(ph_, b))
                for (bk, u), (h0, h1) in zip(G_BANKS[L], BANK_HEADS):
                    bk.wait_empty(pe, ph_, u + b)
                    pe.matmul(bk.t[:, 0:(h1 - h0) * CK], wq, KEYS_BY_HEAD[L][:, b, h0 * CK:h1 * CK], start=True, stop=True)\
                        .then_inc(bk.full.sem, 1)

        def prep03_act(act, L, part):
            ph_ = "prep" + L
            if part == 0:
                if L == "L0x":
                    act.wait_ge(made.sem, MADE)
                    X.wait_full(act, ph_, 0)
                    act.activation(keysT, X.t[:, 0:NB * CK].rearrange("p (b k) -> p b k", b=NB), ACT.Copy)\
                        .then_inc(X.drained.sem, 1)
                    O.wait_full(act, ph_, 0)
                    act.activation(wT[:, 0, :], O.t[:, 0:P], ACT.Copy).then_inc(O.drained.sem, 1)
                else:
                    X.wait_full(act, ph_, 0)
                    act.activation(wT[:, 1:3, :], X.t[:, 0:2 * P].rearrange("p (i d) -> p i d", i=2), ACT.Copy)
                    act.activation(out_wT[:, 1, :], X.t[:, 2 * P:3 * P], ACT.Copy).then_inc(X.drained.sem, 1)
            elif part == 1:
                TB[0].wait_full(act, ph_, 0)
                act.activation(values, TB[0].t[0:CK, :].rearrange("p (b d) -> p b d", b=NB), ACT.Copy)\
                    .then_inc(TB[0].drained.sem, 1)
            elif part >= 4:
                b = part - 4
                for (bk, u), (h0, h1) in zip(G_BANKS[L], BANK_HEADS):
                    bk.wait_full(act, ph_, u + b)
                    act.activation(GA[:, b, h0:h1, :], bk.t[:, 0:(h1 - h0) * CK].rearrange("p (h k) -> p h k", k=CK),
                                   ACT.Copy).then_inc(bk.drained.sem, 1)

        def prep03_dve(dve, L, part):
            ph_ = "prep" + L
            if 1 <= part <= NB:
                b = part - 1
                Y.wait_full(dve, ph_, 0)
                dve.tensor_tensor(KEYS_BY_HEAD[L][:, b, :].rearrange("p (h k) -> p h k", k=CK),
                                  spread(Y.t[:, b * CK:(b + 1) * CK], 1, H16), spread(blk[:, :], 2, CK), ALU.mult)\
                    .then_inc(dve_prep.sem, 1)
                if b == NB - 1:
                    dve.wait_ge(dve_prep.sem, dve_prep.after(ph_, NB - 1))
                    dve.sem_inc(Y.drained.sem, 1)
            if part in (3, 4):
                bk, c0 = (TB[0], 0) if part == 3 else (X, 5)
                dve.wait_ge(grid_made.sem, 1)
                bk.wait_full(dve, ph_, 1)
                v = bk.t[:, 0:480].rearrange("p (c b m e) -> p c b m e", c=5, b=NB, m=3)
                for b in range(NB):
                    last = dve.tensor_tensor(V03[:, b, c0:c0 + 5, :, 0:8], v[:, :, b, :, :],
                                             spread(grid[:, c0:c0 + 5, :], 3, 8), ALU.mult)
                last.then_inc(bk.drained.sem, 1)

        def plan_prep1():
            L = "prepL1x"
            for bk in (S[1], S[2], TB[0]):
                bk.plan(L, 2)
            S[0].plan(L, 2)
            X.plan(L, 1 + 4)
            Y.plan(L, 1 + 4 + NB)
            TB[1].plan(L, 4 + NB)
            O.plan(L, 4 + NB)

        def head_bank(h):
            bk = (TB[1], O, X, Y)[h % 4]
            return bk, h // 4 + (1 if bk in (X, Y) else 0)

        def pair_banks(p):
            return (S[0], S[2]) if p < 4 else (S[1], TB[0])

        def prep1_pe(pe):
            L = "prepL1x"
            pe.wait_ge(loaded["attn1"].sem, LOADS["attn1"])

            def pairs(lhs, rhs, unit):
                for p in range(8):
                    for par, bk in enumerate(pair_banks(p)):
                        if p % 4 == 0:
                            bk.wait_empty(pe, L, unit)
                        r = slice(64 * par, 64 * par + 64)
                        last = pe.matmul(bk.t[:, (p % 4) * P:(p % 4 + 1) * P], lhs[r, p, :], rhs[r, p, :],
                                         start=True, stop=True)
                        if p % 4 == 3:
                            last.then_inc(bk.full.sem, 1)

            pairs(w1k, w1q, 0)
            for i, bk in enumerate((X, Y)):
                bk.wait_empty(pe, L, 0)
                for c in range(4):
                    last = pe.transpose(bk.t[:, c * P:(c + 1) * P], w1o[:, (4 * i + c) * P:(4 * i + c + 1) * P],
                                        ident[:, :])
                last.then_inc(bk.full.sem, 1)
            for bk in (S[0], S[1], S[2], TB[0]):
                bk.wait_drained(pe, L, 0)
            for h in range(H16):
                bk, u = head_bank(h)
                bk.wait_empty(pe, L, u)
                pe.matmul(bk.t[:, 0:NB * CK], head_mat[:, h % 2, h // 2, :], keysT, start=True, stop=True)\
                    .then_inc(bk.full.sem, 1)
            X.wait_drained(pe, L, 0)
            Y.wait_drained(pe, L, 0)
            pairs(w1v, w1oT, 1)

        def folded_values_pe(pe):
            L = "prepL1x"
            for bk in (S[0], S[1], S[2], TB[0]):
                bk.wait_drained(pe, L, 1)
            for b in range(NB):
                for bk, u, c0, c1 in ((O, 4 + b, 0, 4), (Y, 5 + b, 4, 8), (TB[1], 4 + b, 8, 10)):
                    bk.wait_empty(pe, L, u)
                    for c in range(c0, c1):
                        hs = [h for cc, h in PIECES16 if cc == c]
                        n = CHUNKS16[c][1]
                        for h in hs:
                            last = pe.matmul(bk.t[0:n, (c - c0) * P:(c - c0 + 1) * P], WINDOW(b, c, h, n),
                                             head_mat[:, h % 2, h // 2, :], start=h == hs[0], stop=h == hs[-1])
                    last.then_inc(bk.full.sem, 1)

        def prep1_act(act):
            L = "prepL1x"

            def halves(unit):
                for i in range(2):
                    S[i].wait_full(act, L, unit)
                    act.activation(head_mat[:, 0, 4 * i:4 * i + 4, :], S[i].t[:, :].rearrange("p (c d) -> p c d", c=4),
                                   ACT.Copy).then_inc(S[i].drained.sem, 1)

            halves(0)
            for i, bk in enumerate((X, Y)):
                bk.wait_full(act, L, 0)
                act.activation(w1oT[:, 4 * i:4 * i + 4, :], bk.t[:, :].rearrange("p (c d) -> p c d", c=4), ACT.Copy)\
                    .then_inc(bk.drained.sem, 1)
            for h in range(1, H16, 2):
                bk, u = head_bank(h)
                bk.wait_full(act, L, u)
                act.activation(GB[:, :, h, :], bk.t[:, 0:NB * CK].rearrange("p (b k) -> p b k", b=NB), ACT.Copy)\
                    .then_inc(bk.drained.sem, 1)
            halves(1)

        def folded_values_act(act):
            L = "prepL1x"
            r = CHUNKS16[9][1]
            for b in range(NB):
                O.wait_full(act, L, 4 + b)
                act.activation(V1[:, b, 0:4, :], O.t[:, :].rearrange("p (c d) -> p c d", c=4), ACT.Copy)\
                    .then_inc(O.drained.sem, 1)
                TB[1].wait_full(act, L, 4 + b)
                act.activation(V1[:, b, 8, :], TB[1].t[:, 0:P], ACT.Copy)
                act.activation(V1[0:r, b, 9, :], TB[1].t[0:r, P:2 * P], ACT.Copy).then_inc(TB[1].drained.sem, 1)

        def prep1_dve(dve):
            L = "prepL1x"
            dve.wait_ge(loaded["mask1"].sem, LOADS["mask1"])
            dve.tensor_scalar(mask1[:, :, :], mask_raw[:, :, :], 0.0, MASKED, ALU.is_equal, ALU.mult)\
                .then_inc(mask_made.sem, 1)
            dve.tensor_scalar(src_bias[:, :, :], src_raw[:, :, :], 0.0, MASKED, ALU.is_equal, ALU.mult)\
                .then_inc(mask_made.sem, 1)
            dve.wait_ge(mask_made.sem, 2)
            for b in range(NB):
                v = mask1[:, b * NT:(b + 1) * NT, :]
                dve.tensor_tensor(v, v, spread(src_bias[:, b, :], 1, NT), ALU.min).then_inc(mask_made.sem, 1)

            def halves(unit):
                for i, bk in enumerate((S[2], TB[0])):
                    bk.wait_full(dve, L, unit)
                    dve.tensor_copy(head_mat[:, 1, 4 * i:4 * i + 4, :], bk.t[:, :].rearrange("p (c d) -> p c d", c=4))\
                        .then_inc(bk.drained.sem, 1)

            halves(0)
            for h in range(0, H16, 2):
                bk, u = head_bank(h)
                bk.wait_full(dve, L, u)
                dve.tensor_copy(GB[:, :, h, :], bk.t[:, 0:NB * CK].rearrange("p (b k) -> p b k", b=NB))\
                    .then_inc(bk.drained.sem, 1)
            halves(1)

        def folded_values_dve(dve):
            L = "prepL1x"
            for b in range(NB):
                Y.wait_full(dve, L, 5 + b)
                dve.tensor_copy(V1[:, b, 4:8, :], Y.t[:, :].rearrange("p (c d) -> p c d", c=4))\
                    .then_inc(Y.drained.sem, 1)

        def plan_prep2():
            L = "prepL2x"
            for bk in (Y, O, X, S[0], S[1], TB[0]):
                bk.plan(L, 1)

        def prep2_pe(pe):
            L = "prepL2x"
            pe.wait_ge(loaded["attn2"].sem, LOADS["attn2"])
            for h, bk in enumerate((Y, O)):
                r = slice(64 * h, 64 * h + 64)
                bk.wait_empty(pe, L)
                pe.matmul(bk.t[:, 0:P], w2[r, 1, :], w2[r, 0, :], start=True, stop=True).then_inc(bk.full.sem, 1)
            X.wait_empty(pe, L)
            for i in range(2):
                last = pe.transpose(X.t[:, i * P:(i + 1) * P], w2[:, 2 + i, :], ident[:, :])
            last.then_inc(X.full.sem, 1)
            for h, (bk, src) in enumerate(((S[0], Y), (S[1], O))):
                src.wait_drained(pe, L)
                bk.wait_empty(pe, L)
                pe.matmul(bk.t[:, 0:NB * CK], a2[:, h, :], keysT, start=True, stop=True).then_inc(bk.full.sem, 1)
            X.wait_drained(pe, L)
            TB[0].wait_empty(pe, L)
            for b in range(NB):
                last = pe.matmul(TB[0].t[0:CK, b * P:(b + 1) * P], keysT[:, b, :], wT[:, 0, :], start=True, stop=True)
            last.then_inc(TB[0].full.sem, 1)

        def prep2_act(act):
            L = "prepL2x"
            for h, bk in enumerate((Y, O)):
                bk.wait_full(act, L)
                act.activation(a2[:, h, :], bk.t[:, 0:P], ACT.Copy).then_inc(bk.drained.sem, 1)
            X.wait_full(act, L)
            act.activation(wT[:, 0, :], X.t[:, 0:P], ACT.Copy)
            act.activation(out_wT[:, 0, :], X.t[:, P:2 * P], ACT.Copy).then_inc(X.drained.sem, 1)

        def prep2_dve(dve):
            L = "prepL2x"
            for h in range(2):
                S[h].wait_full(dve, L)
                dve.tensor_copy(G2[:, :, h, :], S[h].t[:, 0:NB * CK].rearrange("p (b k) -> p b k", b=NB))\
                    .then_inc(S[h].drained.sem, 1)
            TB[0].wait_full(dve, L)
            for b in range(NB):
                last = dve.tensor_copy(V2[0:CK, b, :, 0:64],
                                       TB[0].t[0:CK, b * P:(b + 1) * P].rearrange("p (h e) -> p h e", h=2))
            last.then_inc(TB[0].drained.sem, 1)

        FC_BANKS = [S[0], S[1], S[2], TB[0]]

        def plan_ffn0():
            for bk in (TB[0], TB[1], X, Y):
                bk.plan("prepL0f", 1)
            L = "L0f"
            plan_norm(L)
            X.plan(L, 1, NB)
            for bk in FC_BANKS:
                bk.plan(L, 1, NB)
            Y.plan(L, 1, NB)
            for e in square_ready:
                e.plan(L, 1, NB)
            x_done.plan(L, 1, NB)

        mean, scale, hi, lo = wsc[:, 0, 0:5], wsc[:, 0, 8:13], wsc[:, 1, 0:5], wsc[:, 1, 8:13]

        def ternary_scales_dve(dve):
            dve.wait_ge(loaded["ffn0"].sem, LOADS["ffn0"])
            n = 0

            def step(ins):
                nonlocal n
                n += 1
                ins.then_inc(tern_scale.sem, 1)
                dve.wait_ge(tern_scale.sem, n)

            dve.tensor_reduce(mean[:, 0:NC], wfc[:, :, :], AX.X, ALU.add, apply_absolute_value=True)
            step(dve.tensor_reduce(mean[:, NC:NC + 1], wpr[:, :], AX.X, ALU.add, apply_absolute_value=True))
            step(dve.tensor_scalar(scale[:, 0:NC], mean[:, 0:NC], 1.0 / P, 1e-5, ALU.mult, ALU.max))
            step(dve.tensor_scalar(scale[:, NC:NC + 1], mean[:, NC:NC + 1], 1.0 / FF, 1e-5, ALU.mult, ALU.max))
            step(dve.tensor_scalar(hi, scale, 0.5, None, ALU.mult))
            step(dve.tensor_scalar(lo, scale, -0.5, None, ALU.mult))
            assert n == TERN_SCALES

        def ternary_pool(pool):
            pool.wait_ge(tern_scale.sem, TERN_SCALES)
            n = 0

            def step(ins):
                nonlocal n
                n += 1
                ins.then_inc(tern.sem, 1)
                pool.wait_ge(tern.sem, n)

            wp = wpr[:, :].rearrange("p (c d) -> p c d", c=NC)
            for w, col in ((wfc, lambda c: c), (wp, lambda c: NC)):
                for c in range(NC):
                    k = col(c)
                    pool.tensor_scalar(wt1[:, c, :], w[:, c, :], hi[:, k:k + 1], None, ALU.is_gt)
                    last = pool.tensor_scalar(wt2[:, c, :], w[:, c, :], lo[:, k:k + 1], None, ALU.is_lt)
                step(last)
                step(pool.tensor_tensor(wt1[:, :, :], wt1[:, :, :], wt2[:, :, :], ALU.subtract))
                step(pool.tensor_tensor(wt1[:, :, :], wt1[:, :, :], w[:, :, :], ALU.subtract))
                step(pool.tensor_tensor(w[:, :, :], w[:, :, :], wt1[:, :, :], ALU.add))
                for c in range(NC):
                    last = pool.tensor_scalar(w[:, c, :], w[:, c, :], scale[:, col(c):col(c) + 1], None, ALU.mult)
                step(last)
            assert n == TERN_STEPS

        def prep_ffn0_dve(dve):
            TB[1].wait_full(dve, "prepL0f")
            dve.tensor_scalar(bv[:, :], TB[1].t[0:16, 0:P], gate[:, 0:1], None, ALU.mult).then_inc(TB[1].drained.sem, 1)

        TERN_SCALES = 5
        TERN_STEPS = 10

        def prep_ffn0_pe(pe):
            L = "prepL0f"
            pe.wait_ge(loaded["ffn0"].sem, LOADS["ffn0"])
            TB[0].wait_empty(pe, L)
            for c in range(NC):
                last = pe.transpose(TB[0].t[0:16, c * P:(c + 1) * P], lr[:, c, :], ident[:, :])
            last.then_inc(TB[0].full.sem, 1)
            TB[1].wait_empty(pe, L)
            pe.matmul(TB[1].t[0:16, 0:P], fbT[:, :], vlow[:, :], start=True, stop=True).then_inc(TB[1].full.sem, 1)
            TB[0].wait_drained(pe, L)
            TB[1].wait_drained(pe, L)
            pe.wait_ge(tern.sem, TERN_STEPS)
            X.wait_empty(pe, L)
            for c in range(NC):
                o = X.t[:, c * P:(c + 1) * P]
                pe.matmul(o, wfc[:, c, :], ident[:, :], start=True, stop=False)
                last = pe.matmul(o, bv[:, :], lrT[:, c * P:(c + 1) * P], start=False, stop=True)
            last.then_inc(X.full.sem, 1)
            Y.wait_empty(pe, L)
            for c in range(NC):
                last = pe.transpose(Y.t[:, c * P:(c + 1) * P], wpr[:, c * P:(c + 1) * P], ident[:, :])
            last.then_inc(Y.full.sem, 1)
            X.wait_drained(pe, L)
            Y.wait_drained(pe, L)

        def prep_ffn0_act(act):
            L = "prepL0f"
            TB[0].wait_full(act, L)
            act.activation(lrT[:, :], TB[0].t[0:16, :], ACT.Copy).then_inc(TB[0].drained.sem, 1)
            X.wait_full(act, L)
            act.activation(wfcT[:, :], X.t[:, :], ACT.Copy).then_inc(X.drained.sem, 1)
            Y.wait_full(act, L)
            act.activation(wprT[:, :, :], Y.t[:, :].rearrange("p (c d) -> p c d", c=NC), ACT.Copy)\
                .then_inc(Y.drained.sem, 1)

        def fc_pe(pe, L, b, w):
            X.wait_drained(pe, L, 0, b)
            for c, bk in enumerate(FC_BANKS):
                bk.wait_empty(pe, L, 0, b)
                pe.matmul(bk.t[:, :], w[:, c * P:(c + 1) * P], xnT[:, :], start=True, stop=True)\
                    .then_inc(bk.full.sem, 1)

        def proj_pe(pe, L, b, w, row, ready, halfway=None):
            Y.wait_empty(pe, L, 0, b)
            if row is not None:
                pe.matmul(Y.t[:, :], ones[0:1, :], spread(rows[0:1, row, :], 1, NT), start=True, stop=False,
                          skip_group_check=True)
            for c in range(NC):
                if c == NC // 2 and halfway is not None:
                    halfway()
                ready(pe, b, c)
                for t in range(NT):
                    last = pe.matmul(Y.t[:, t * P:(t + 1) * P], hT[:, c, t * P:(t + 1) * P], w[:, c, :],
                                     start=row is None and c == 0 and t == 0, stop=c == NC - 1,
                                     skip_group_check=True)
            last.then_inc(Y.full.sem, 1)

        def x_rows(b):
            return x[:, b * NT:(b + 1) * NT, :] if isinstance(b, int) else x[:, bass.ds(b * NT, NT), :]

        def add_result_dve(dve, L, b):
            Y.wait_full(dve, L, 0, b)
            dve.tensor_tensor(x_rows(b), x_rows(b), Y.t[:, :].rearrange("p (t d) -> p t d", t=NT), ALU.add)\
                .then_inc(Y.drained.sem, 1)
            Y.wait_drained(dve, L, 0, b)
            dve.sem_inc(x_done.sem, 1)

        def run_ffn0(eng, name):
            L = "L0f"

            def squares(b, chunks):
                for c in chunks:
                    FC_BANKS[c].wait_drained(eng, L, 0, b)
                    eng.tensor_tensor(hT[:, c, :], hT[:, c, :], hT[:, c, :], ALU.mult).then_inc(square_ready[c].sem, 1)

            if name == "act":
                eng.wait_ge(zeroed.sem, 16)

            def relus(b):
                for c, bk in enumerate(FC_BANKS):
                    bk.wait_full(eng, L, 0, b)
                    eng.activation(hT[:, c, :], bk.t[:, :], ACT.Relu).then_inc(bk.drained.sem, 1)

            def squared(pe, b, c):
                pe.wait_ge(square_ready[c].sem, square_ready[c].after(L, 0, b))

            def start(b, norm=True):
                if name == "pe":
                    fc_pe(eng, L, b, wfcT)
                elif name == "act":
                    relus(b)
                elif name == "dve":
                    if norm:
                        ln_stats_dve(eng, L, b + 1)
                    squares(b, (0, 1))
                    if norm:
                        ln_apply_dve(eng, L, b + 1)
                    squares(b, (2, 3))
                elif norm:
                    front_pool(eng, L, b + 1)

            def step(b, norm=True):
                if name == "act":
                    front_act(eng, L, b + 1)
                finish(b, lambda: front_pe(eng, L, b + 1))
                start(b + 1, norm)

            def finish(b, halfway=None):
                if name == "pe":
                    proj_pe(eng, L, b, wprT, None, squared, halfway)
                elif name == "dve":
                    add_result_dve(eng, L, b)

            if name in ("pe", "act"):
                fronts(eng, name, L, 0)
            start(0)
            with eng.Fori(0, NB - 2) as b:
                step(b)
            step(NB - 2, norm=False)
            early_norm(eng, name, L)
            finish(NB - 1)

        def fronts(eng, name, L, b):
            {"pe": front_pe, "dve": front_dve, "act": front_act, "pool": front_pool}[name](eng, L, b)

        GATE_STEPS = 13
        WHOLE = NB * NT
        flat = prob[:, :, :].rearrange("p t n -> p (t n)")
        f1 = {}
        at = 0
        for key, dims in (("xnT", (NB, 512)), ("weighted", (2, 4, P)), ("odd", (2, P)), ("sums", (NT, P)),
                          ("lg", (WHOLE, NE)), ("ex", (WHOLE, NE)), ("second", (WHOLE, NE)), ("top", (WHOLE, 8)),
                          ("index", (WHOLE, 8)), ("indexf", (WHOLE, 8)), ("gates", (WHOLE, NE)), ("gs", (4, WHOLE))):
            size = int(np.prod(dims))
            names = "abc"[:len(dims)]
            f1[key] = flat[:, at:at + size].rearrange(
                f"p ({' '.join(names)}) -> p {' '.join(names)}", **dict(zip(names[1:], dims[1:])))
            at += size
        assert at <= NT * ROWS16
        gates1 = f1["gates"]

        def plan_ffn1():
            L = "L1f"
            plan_norm(L)
            X.plan(L, 1, NB)
            O.plan(L, 1, NB)
            Y.plan(L, 1, NB)
            TB[0].plan(L, 1, NB)
            for bk in (S[0], S[1], S[2], TB[1]):
                bk.plan(L, 2, NB)
            gate_step.plan(L, GATE_STEPS)
            gate_exp.plan(L, 1)
            lhs_ready.plan(L, 2, NB)
            selected.plan(L, 1, NB)
            base_added.plan(L, 1, NB)
            chain.plan(L, 2 * NT, NB)
            pool_sum.plan(L, 3 * NT, NB)
            x_done.plan(L, 1, NB)

        def tile_banks(t):
            return (S[0], S[1]) if t % 2 == 0 else (S[2], TB[1])

        def run_ffn1(eng, name):
            L = "L1f"

            def logits_pe(b):
                X.wait_drained(eng, L, 0, b)
                O.wait_empty(eng, L, 0, b)
                for t in range(NT):
                    last = eng.matmul(O.t[:, t * NE:(t + 1) * NE], xnT[:, t * P:(t + 1) * P], wg1[:, :],
                                      start=True, stop=True)
                last.then_inc(O.full.sem, 1)

            def keep_xnT_act(b):
                X.wait_full(eng, L, 0, b)
                eng.activation(f1["xnT"][:, bass.ds(b, 1), :].squeeze(1), X.t[:, :], ACT.Copy)
                eng.activation(xnT[:, :], X.t[:, :], ACT.Copy).then_inc(X.drained.sem, 1)

            def logits_dve(b):
                O.wait_full(eng, L, 0, b)
                d = f1["lg"][:, b * NT:(b + 1) * NT, :] if isinstance(b, int) else f1["lg"][:, bass.ds(b * NT, NT), :]
                eng.tensor_tensor(d, O.t[:, 0:NT * NE].rearrange("p (t e) -> p t e", t=NT),
                                  spread(bg1[:, :], 1, NT), ALU.add).then_inc(O.drained.sem, 1)

            def gates_dve():
                n = 0

                def k(ins):
                    nonlocal n
                    ins.then_inc(gate_step.sem, 1)
                    eng.wait_ge(gate_step.sem, gate_step.after(L, n))
                    n += 1

                lg_, ex_, second, top, index, indexf, gs_ = (f1[i] for i in (
                    "lg", "ex", "second", "top", "index", "indexf", "gs"))
                O.wait_drained(eng, L, 0, NB - 1)
                k(eng.tensor_reduce(gs_[:, 0, :], lg_, AX.X, ALU.max))
                k(eng.tensor_tensor(lg_, lg_, spread(gs_[:, 0, :], 2, NE), ALU.subtract))
                eng.wait_ge(gate_exp.sem, gate_exp.after(L))
                for g in range(WHOLE):
                    last = eng.max(top[:, g, :], ex_[:, g, :])
                k(last)
                for g in range(WHOLE):
                    last = eng.max_index(index[:, g, :].bitcast(U32), top[:, g, :], ex_[:, g, :])
                k(last)
                k(eng.tensor_copy(indexf, index.bitcast(U32)))
                k(eng.tensor_tensor(gs_[:, 1, :], top[:, :, 0], top[:, :, 1], ALU.add))
                k(eng.reciprocal(gs_[:, 2, :], gs_[:, 1, :]))
                k(eng.tensor_tensor(gs_[:, 0, :], top[:, :, 0], gs_[:, 2, :], ALU.mult))
                k(eng.tensor_tensor(gs_[:, 3, :], top[:, :, 1], gs_[:, 2, :], ALU.mult))
                io = spread(iota8[:, :], 1, WHOLE)
                eng.tensor_tensor(gates1, io, spread(indexf[:, :, 0], 2, NE), ALU.is_equal)
                k(eng.tensor_tensor(second, io, spread(indexf[:, :, 1], 2, NE), ALU.is_equal))
                k(eng.tensor_tensor(gates1, gates1, spread(gs_[:, 0, :], 2, NE), ALU.mult))
                k(eng.tensor_tensor(second, second, spread(gs_[:, 3, :], 2, NE), ALU.mult))
                k(eng.tensor_tensor(gates1, gates1, second, ALU.add))
                assert n == GATE_STEPS, n

            def experts_pe(b, t):
                if t in (0, 2):
                    eng.wait_ge(lhs_ready.sem, lhs_ready.after(L, t // 2, b))
                for i, bk in enumerate(tile_banks(t)):
                    bk.wait_empty(eng, L, t // 2, b)
                    eng.matmul(bk.t[:, :], mixT[:, t * P:(t + 1) * P], we[:, 4 * i:4 * i + 4, :],
                               start=True, stop=True).then_inc(bk.full.sem, 1)

            def gates_transposed_pe(b):
                TB[0].wait_empty(eng, L, 0, b)
                for t in range(NT):
                    last = eng.transpose(TB[0].t[0:NE, t * P:(t + 1) * P], gsel[:, t, :], ident[:, :])
                last.then_inc(TB[0].full.sem, 1)

            def biases_pe(b):
                TB[0].wait_drained(eng, L, 0, b)
                Y.wait_empty(eng, L, 0, b)
                for t in range(NT):
                    last = eng.matmul(Y.t[:, t * P:(t + 1) * P], gT[:, t * P:(t + 1) * P], be[:, :],
                                      start=True, stop=True)
                last.then_inc(Y.full.sem, 1)

            def stage_act(b, half):
                src = f1["xnT"][:, b, :] if isinstance(b, int) else f1["xnT"][:, bass.ds(b, 1), :].squeeze(1)
                c = slice(256 * half, 256 * half + 256)
                eng.activation(mixT[:, c], src[:, c], ACT.Copy).then_inc(lhs_ready.sem, 1)

            def weigh_act(b, t):
                bk = tile_banks(t)[1]
                bk.wait_full(eng, L, t // 2, b)
                eng.wait_ge(pool_sum.sem, pool_sum.after(L, 3 * (t - 2) + 1, b))
                for e in range(4):
                    last = eng.activation(f1["weighted"][:, t % 2, e, :], bk.t[:, e * P:(e + 1) * P], ACT.Copy,
                                          scale=gsel[:, t, 4 + e:5 + e])
                last.then_inc(bk.drained.sem, 1)

            def sum_pool(b, t):
                w = f1["weighted"]
                step = lambda j: pool_sum.after(L, 3 * t + j, b)
                tile_banks(t)[1].wait_drained(eng, L, t // 2, b)
                eng.tensor_tensor(w[:, t % 2, 0:2, :], w[:, t % 2, 0:2, :], w[:, t % 2, 2:4, :], ALU.add)\
                    .then_inc(pool_sum.sem, 1)
                eng.wait_ge(pool_sum.sem, step(0))
                if t == 0:
                    eng.wait_ge(x_done.sem, x_done.after(L, 0, b - 1))
                eng.tensor_tensor(f1["sums"][:, t, :], w[:, t % 2, 0, :], w[:, t % 2, 1, :], ALU.add)\
                    .then_inc(pool_sum.sem, 1)
                eng.wait_ge(pool_sum.sem, step(1))
                tile_banks(t)[0].wait_drained(eng, L, t // 2, b)
                eng.tensor_tensor(f1["sums"][:, t, :], f1["sums"][:, t, :], f1["odd"][:, t % 2, :], ALU.add)\
                    .then_inc(pool_sum.sem, 1)

            def weigh_dve(b, t):
                xt = x[:, b * NT + t, :]
                bk = tile_banks(t)[0]
                odd = f1["odd"][:, t % 2, :]
                g = lambda e: gsel[:, t, e:e + 1]
                part = lambda e: bk.t[:, e * P:(e + 1) * P]
                bk.wait_full(eng, L, t // 2, b)
                eng.scalar_tensor_tensor(xt, part(0), g(0), xt, ALU.mult, ALU.add).then_inc(chain.sem, 1)
                eng.wait_ge(pool_sum.sem, pool_sum.after(L, 3 * (t - 2) + 2, b))
                eng.tensor_scalar(odd, part(1), g(1), None, ALU.mult).then_inc(chain.sem, 1)
                eng.wait_ge(chain.sem, chain.after(L, 2 * t, b))
                eng.scalar_tensor_tensor(xt, part(2), g(2), xt, ALU.mult, ALU.add)
                eng.wait_ge(chain.sem, chain.after(L, 2 * t + 1, b))
                eng.scalar_tensor_tensor(odd, part(3), g(3), odd, ALU.mult, ALU.add).then_inc(bk.drained.sem, 1)

            def select_dve(b):
                src = gates1[:, b * NT:(b + 1) * NT, :] if isinstance(b, int) else gates1[:, bass.ds(b * NT, NT), :]
                eng.tensor_copy(gsel[:, :, :], src).then_inc(selected.sem, 1)

            def finish_dve(b):
                eng.wait_ge(pool_sum.sem, pool_sum.after(L, 3 * NT - 1, b))
                eng.tensor_tensor(x_rows(b), x_rows(b), f1["sums"], ALU.add).then_inc(base_added.sem, 1)
                eng.wait_ge(base_added.sem, base_added.after(L, 0, b))
                add_result_dve(eng, L, b)

            def body(b, last):
                wait_selected = lambda: eng.wait_ge(selected.sem, selected.after(L, 0, b))
                if name == "pe":
                    experts_pe(b, 0)
                    experts_pe(b, 1)
                    wait_selected()
                    gates_transposed_pe(b)
                    experts_pe(b, 2)
                    experts_pe(b, 3)
                    biases_pe(b)
                elif name == "act":
                    wait_selected()
                    weigh_act(b, 0)
                    weigh_act(b, 1)
                    if not last:
                        stage_act(b + 1, 0)
                    TB[0].wait_full(eng, L, 0, b)
                    eng.activation(gT[:, :], TB[0].t[0:NE, :], ACT.Copy).then_inc(TB[0].drained.sem, 1)
                    weigh_act(b, 2)
                    weigh_act(b, 3)
                    if not last:
                        stage_act(b + 1, 1)
                elif name == "dve":
                    for t in range(1, NT):
                        weigh_dve(b, t)
                    if not last:
                        TB[1].wait_drained(eng, L, 1, b)
                        S[2].wait_drained(eng, L, 1, b)
                        TB[0].wait_full(eng, L, 0, b)
                        select_dve(b + 1)
                        eng.wait_ge(selected.sem, selected.after(L, 0, b + 1))
                        weigh_dve(b + 1, 0)
                    else:
                        early_norm(eng, name, L)
                    finish_dve(b)
                elif name == "pool":
                    for t in range(NT - 1):
                        sum_pool(b, t)
                    if last:
                        early_norm(eng, name, L)
                    sum_pool(b, NT - 1)

            norm_sets = ((stats, mv, ve, rstd), (stats_z, mv_z, ve_z, rstd_z))
            if name == "dve":
                ln_stats_dve(eng, L, 1, 0, *norm_sets[1][0:2])
                for b in range(1, NB):
                    if b + 1 < NB:
                        ln_stats_dve(eng, L, b + 1, 0, *norm_sets[(b + 1) % 2][0:2])
                    ln_apply_dve(eng, L, b, 0, norm_sets[b % 2][1], norm_sets[b % 2][3])
                    logits_dve(b - 1)
                logits_dve(NB - 1)
                gates_dve()
                select_dve(0)
                eng.wait_ge(selected.sem, selected.after(L, 0, 0))
                weigh_dve(0, 0)
            elif name == "pool":
                for b in range(1, NB):
                    ln_rstd_pool(eng, L, b, 0, *norm_sets[b % 2][1:])
            else:
                with eng.Fori(0, NB) as b:
                    if name == "pe":
                        front_pe(eng, L, b)
                        logits_pe(b)
                    else:
                        keep_xnT_act(b)
                if name == "act":
                    X.wait_drained(eng, L, 0, NB - 1)
                    stage_act(0, 0)
                    stage_act(0, 1)
                    eng.wait_ge(gate_step.sem, gate_step.after(L, 1))
                    eng.activation(f1["ex"], f1["lg"], ACT.Exp).then_inc(gate_exp.sem, 1)
            with eng.Fori(0, NB - 1) as b:
                body(b, False)
            body(NB - 1, True)

        def plan_ffn2():
            L = "L2f"
            plan_norm(L)
            X.plan(L, 1, NB)
            O.plan(L, 2, NB)
            Y.plan(L, 1, NB)
            for bk in (S[0], S[1], TB[0], TB[1]):
                bk.plan(L, 2, NB)
            xa_ready.plan(L, 1, NB)
            gelu_ready.plan(L, 1, NB)
            x_done.plan(L, 1, NB)

        w1e = big[:, 0, :].rearrange("p (e f) -> p e f", e=NE)
        w2e = big[:, 1, :].rearrange("p (e c d) -> p e c d", e=NE, c=NC)

        def run_ffn2(eng, name):
            L = "L2f"

            def front(b):
                if name == "pe":
                    front_pe(eng, L, b)
                    eng.wait_ge(z_ready.sem, z_ready.after(L, 0, b))
                    O.wait_empty(eng, L, 0, b)
                    for t in range(NT):
                        last = eng.transpose(O.t[:, t * P:(t + 1) * P], z[:, t, :], ident[:, :])
                    last.then_inc(O.full.sem, 1)
                elif name == "act":
                    front_act(eng, L, b)
                    O.wait_full(eng, L, 0, b)
                    eng.activation(mixT[:, :], O.t[:, :], ACT.Identity, scale=cols2[:, 0:1], bias=cols2[:, 1:2])\
                        .then_inc(O.drained.sem, 1)
                else:
                    fronts(eng, name, L, b)

            def attn_linear(b):
                if name == "pe":
                    O.wait_drained(eng, L, 0, b)
                    eng.matmul(O.t[:, :], attn_w[:, :], mixT[:, :], start=True, stop=True).then_inc(O.full.sem, 1)
                elif name == "dve":
                    O.wait_full(eng, L, 1, b)
                    X.wait_drained(eng, L, 0, b)
                    eng.scalar_tensor_tensor(xaT[:, :], O.t[:, :], cols2[:, 2:3], xnT[:, :], ALU.add, ALU.add)\
                        .then_inc(O.drained.sem, 1)

            def hidden(b, t):
                e = (b * NT + t) % NE
                bk = S[t % 2]
                if name == "pe":
                    if t == 0:
                        O.wait_drained(eng, L, 1, b)
                    bk.wait_empty(eng, L, t // 2, b)
                    for c in range(NC):
                        last = eng.matmul(bk.t[:, c * P:(c + 1) * P], w1e[:, e, c * P:(c + 1) * P],
                                          xaT[:, t * P:(t + 1) * P], start=True, stop=True)
                    last.then_inc(bk.full.sem, 1)
                elif name == "act":
                    bk.wait_full(eng, L, t // 2, b)
                    for c in range(NC):
                        last = eng.activation(hT[:, c, (t % 2) * P:(t % 2 + 1) * P], bk.t[:, c * P:(c + 1) * P],
                                              ACT.Gelu, bias=b1c[:, e, c:c + 1])
                    last.then_inc(bk.drained.sem, 1)

            def down(b, t):
                e = (b * NT + t) % NE
                bk = TB[t % 2]
                if name == "pe":
                    S[t % 2].wait_drained(eng, L, t // 2, b)
                    bk.wait_empty(eng, L, t // 2, b)
                    for c in range(NC):
                        last = eng.matmul(bk.t[:, 0:P], w2e[:, e, c, :], hT[:, c, (t % 2) * P:(t % 2 + 1) * P],
                                          start=c == 0, stop=c == NC - 1)
                    last.then_inc(bk.full.sem, 1)
                elif name == "act":
                    bk.wait_full(eng, L, t // 2, b)
                    eng.activation(mix[:, t, :], bk.t[:, 0:P], ACT.Identity, bias=b2c[:, e:e + 1])\
                        .then_inc(bk.drained.sem, 1)

            def last_linear(b):
                if name == "pe":
                    TB[0].wait_drained(eng, L, 1, b)
                    TB[1].wait_drained(eng, L, 1, b)
                    Y.wait_empty(eng, L, 0, b)
                    eng.matmul(Y.t[:, :], ones[0:1, :], spread(rows[0:1, 3, :], 1, NT), start=True, stop=False,
                               skip_group_check=True)
                    for t in range(NT):
                        last = eng.matmul(Y.t[:, t * P:(t + 1) * P], mix[:, t, :], next_w[:, :], start=False,
                                          stop=True, skip_group_check=True)
                    last.then_inc(Y.full.sem, 1)
                elif name == "act":
                    Y.wait_full(eng, L, 0, b)
                    if b:
                        eng.wait_ge(x_done.sem, x_done.after(L, 0, b - 1))
                    eng.activation(gout[:, :], Y.t[:, :], ACT.Gelu).then_inc(Y.drained.sem, 1)
                elif name == "dve":
                    Y.wait_drained(eng, L, 0, b)
                    eng.tensor_tensor(x_rows(b), x_rows(b), gout[:, :].rearrange("p (t d) -> p t d", t=NT), ALU.add)\
                        .then_inc(x_done.sem, 1)

            if name == "pe":
                eng.wait_ge(loaded["ffn2"].sem, LOADS["ffn2"])
            if name == "act":
                eng.wait_ge(loaded["ffn2"].sem, LOADS["ffn2"])
            if name == "dve":
                eng.wait_ge(loaded["ffn2"].sem, LOADS["ffn2"])
            if name in ("pe", "act"):
                front(0)
            attn_linear(0)
            hidden(0, 0)
            if name in ("dve", "pool"):
                front(1)
            for b in range(NB):
                for t in range(NT - 1):
                    hidden(b, t + 1)
                    if t == 2 and b < NB - 1 and name in ("pe", "act"):
                        front(b + 1)
                    down(b, t)
                if b < NB - 1:
                    attn_linear(b + 1)
                    hidden(b + 1, 0)
                if name in ("dve", "pool") and b < NB - 2:
                    front(b + 2)
                elif b == NB - 2:
                    early_norm(eng, name, L)
                down(b, NT - 1)
                last_linear(b)

        RES_STEPS = 16
        f3 = {}
        at = NTOK * P // P
        for key, dims in (("xnT", (NB, 512)), ("lg", (WHOLE, NE + 2)), ("ex", (WHOLE, NE + 2)), ("top", (WHOLE, 8)),
                          ("index", (WHOLE, 8)), ("gs", (4, WHOLE))):
            size = int(np.prod(dims))
            f3[key] = flat[:, at:at + size].rearrange("p (a b) -> p a b", b=dims[1])
            at += size
        assert at <= NT * ROWS16
        EARLY = NB - 1

        def plan_ffn3():
            L = "L3f"
            plan_norm(L)
            X.plan(L, 1, NB)
            O.plan(L, 1, NB)
            base_added.plan(L, 1, NB)
            normed_ready.plan(L, 2, NB)
            res_step.plan(L, RES_STEPS)
            res_exp.plan(L, 1)
            TB[1].plan("place", 1)
            for bk in FC_BANKS + [Y]:
                bk.plan(L, 1, EARLY)
            for bk in FC_BANKS:
                bk.plan("sent", 1)
                bk.plan("experts", NE // 2)
            O.plan("experts", NE // 2)
            Y.plan("experts", NE // 2)
            for bk in FC_BANKS + [Y]:
                bk.plan("L3f late", 1)
            x_done.plan(L, 1, NB)

        def ffn3_stats(dve, b, j):
            ln_stats_dve(dve, "L3f", b, j, *((stats, mv) if j == 0 else (stats_z, mv_z)))

        def ffn3_rstd(pool, b, j):
            ln_rstd_pool(pool, "L3f", b, j, *((mv, ve, rstd) if j == 0 else (mv_z, ve_z, rstd_z)))

        def ffn3_base(dve, b):
            L = "L3f"
            if not (isinstance(b, int) and b == 0):
                dve.wait_ge(z_ready.sem, z_ready.after(L, 0, b - 1))
                dve.wait_ge(base_added.sem, base_added.after(L, 0, b - 1))
            ln_apply_dve(dve, L, b, 0)
            dve.wait_ge(xn_ready.sem, xn_ready.after(L, 0, b))
            dve.tensor_tensor(x_rows(b), x_rows(b), xn[:, :, :], ALU.add).then_inc(base_added.sem, 1)

        def ffn3_z(dve, b):
            L = "L3f"
            if not (isinstance(b, int) and b == 0):
                X.wait_full(dve, L, 0, b - 1)
                dve.wait_ge(normed_ready.sem, normed_ready.after(L, 0, b - 1))
            ln_apply_dve(dve, L, b, 1, mv_z, rstd_z)

        def ffn3_normed(pool, b):
            L = "L3f"
            dst = normed[:, b * NT:(b + 1) * NT, :] if isinstance(b, int) else normed[:, bass.ds(b * NT, NT), :]
            pool.wait_ge(z_ready.sem, z_ready.after(L, 0, b))
            pool.sem_inc(pool_passed.sem, 1)
            pool.tensor_tensor(dst, z[:, :, :], spread(nw_all, 1, NT), ALU.mult).then_inc(normed_ready.sem, 1)
            pool.wait_ge(normed_ready.sem, normed_ready.after(L, 0, b))
            pool.sem_inc(pool_passed.sem, 1)
            pool.tensor_tensor(dst, dst, spread(nb_all, 1, NT), ALU.add).then_inc(normed_ready.sem, 1)

        def run_ffn3(eng, name):
            L = "L3f"
            eng.wait_ge(loaded["small3"].sem, LOADS["small3"])

            def logits_dve(b):
                O.wait_full(eng, L, 0, b)
                d = f3["lg"][:, b * NT:(b + 1) * NT, :] if isinstance(b, int) else f3["lg"][:, bass.ds(b * NT, NT), :]
                eng.tensor_copy(d, O.t[:, 0:NT * 10].rearrange("p (t e) -> p t e", t=NT)).then_inc(O.drained.sem, 1)

            if name == "pe":
                with eng.Fori(0, NB) as b:
                    eng.wait_ge(z_ready.sem, z_ready.after(L, 0, b))
                    X.wait_empty(eng, L, 0, b)
                    for t in range(NT):
                        last = eng.transpose(X.t[:, t * P:(t + 1) * P], z[:, t, :], ident[:, :])
                    last.then_inc(X.full.sem, 1)
                    X.wait_drained(eng, L, 0, b)
                    O.wait_empty(eng, L, 0, b)
                    for t in range(NT):
                        last = eng.matmul(O.t[:, t * 10:(t + 1) * 10], xnT[:, t * P:(t + 1) * P], wgc[:, :],
                                          start=True, stop=True)
                    last.then_inc(O.full.sem, 1)
            elif name == "act":
                with eng.Fori(0, NB) as b:
                    X.wait_full(eng, L, 0, b)
                    eng.activation(f3["xnT"][:, bass.ds(b, 1), :].squeeze(1), X.t[:, :], ACT.Identity,
                                   scale=cols3[:, 0:1], bias=cols3[:, 1:2])
                    eng.activation(xnT[:, :], X.t[:, :], ACT.Identity, scale=cols3[:, 0:1], bias=cols3[:, 1:2])\
                        .then_inc(X.drained.sem, 1)
            elif name == "dve":
                with eng.Fori(0, NB - 1) as b:
                    ffn3_stats(eng, b, 1)
                    ffn3_stats(eng, b + 1, 0)
                    ffn3_z(eng, b)
                    ffn3_base(eng, b + 1)
                    logits_dve(b)
                ffn3_stats(eng, NB - 1, 1)
                ffn3_z(eng, NB - 1)
                logits_dve(NB - 1)
            else:
                with eng.Fori(0, NB - 1) as b:
                    ffn3_rstd(eng, b, 1)
                    ffn3_rstd(eng, b + 1, 0)
                    ffn3_normed(eng, b)
                ffn3_rstd(eng, NB - 1, 1)
                ffn3_normed(eng, NB - 1)

            def mlp(b, ph, u):
                if name == "pe":
                    src = f3["xnT"][:, b, :] if isinstance(b, int) else f3["xnT"][:, bass.ds(b, 1), :].squeeze(1)
                    for c, bk in enumerate(FC_BANKS):
                        bk.wait_empty(eng, ph, 0, u)
                        eng.matmul(bk.t[:, :], res_w1[:, c * P:(c + 1) * P], src, start=True, stop=True)\
                            .then_inc(bk.full.sem, 1)
                    proj_pe(eng, ph, u, res_w2, 4, lambda pe, u_, c: FC_BANKS[c].wait_drained(pe, ph, 0, u_))
                elif name == "act":
                    for c, bk in enumerate(FC_BANKS):
                        bk.wait_full(eng, ph, 0, u)
                        eng.activation(hT[:, c, :], bk.t[:, :], ACT.Gelu_apprx_tanh, bias=cols3[:, 2 + c:3 + c])\
                            .then_inc(bk.drained.sem, 1)
                elif name == "dve":
                    Y.wait_full(eng, ph, 0, u)
                    for t in range(NT):
                        g = b * NT + t
                        xt = x[:, g, :]
                        ins = eng.scalar_tensor_tensor(xt, Y.t[:, t * P:(t + 1) * P],
                                                       coef0[:, g:g + 1] if isinstance(b, int)
                                                       else coef0[:, bass.ds(g, 1)], xt, ALU.mult, ALU.add)
                    ins.then_inc(Y.drained.sem, 1)

            tile_hidden = lambda e: (S[0], S[1]) if e % 2 == 0 else (S[2], TB[0])
            tile_out = lambda e: O if e % 2 == 0 else Y
            if name == "pe":
                eng.wait_ge(route_made.sem, 2)
                eng.wait_ge(res_step.sem, res_step.after(L, 7))
                TB[1].wait_empty(eng, "place")
                o = TB[1].t[:, 0:P].rearrange("p (g e) -> p g e", e=NE)
                eng.matmul(o, earlier, chosen, start=True, stop=False, skip_group_check=True)
                G = NB * NT
                for g in range(G - 1):
                    last = eng.matmul(o[:, g + 1:G, :], onesb, spread(chosen[:, g, :], 1, G - 1 - g),
                                      start=False, stop=g == G - 2, skip_group_check=True)
                last.then_inc(TB[1].full.sem, 1)
            elif name == "act":
                eng.wait_ge(res_step.sem, res_step.after(L, 3))
                eng.activation(f3["ex"], f3["lg"], ACT.Exp).then_inc(res_exp.sem, 1)
            elif name == "dve":
                n, m = 0, 0

                def k(ins):
                    nonlocal n
                    ins.then_inc(res_step.sem, 1)
                    eng.wait_ge(res_step.sem, res_step.after(L, n))
                    n += 1

                def step(ins):
                    nonlocal m
                    m += 1
                    ins.then_inc(route_step.sem, 1)
                    eng.wait_ge(route_step.sem, m)

                lg_, ex_, top, index, gs_ = (f3[i] for i in ("lg", "ex", "top", "index", "gs"))
                O.wait_drained(eng, L, 0, NB - 1)
                for i, (c0, c1) in enumerate(((0, NE), (NE, NE + 2))):
                    k(eng.tensor_reduce(gs_[:, i, :], lg_[:, :, c0:c1], AX.X, ALU.max))
                    k(eng.tensor_tensor(lg_[:, :, c0:c1], lg_[:, :, c0:c1], spread(gs_[:, i, :], 2, c1 - c0), ALU.subtract))
                for g in range(WHOLE):
                    last = eng.max(top[:, g, :], lg_[:, g, 0:NE])
                k(last)
                for g in range(WHOLE):
                    last = eng.max_index(index[:, g, :].bitcast(U32), top[:, g, :], lg_[:, g, 0:NE])
                k(last)
                k(eng.tensor_copy(expert_of, index[:, :, 0].bitcast(U32)))
                k(eng.tensor_tensor(chosen, spread(iota8[:, :], 1, WHOLE), spread(expert_of, 2, NE), ALU.is_equal))
                TB[1].wait_full(eng, "place")
                eng.tensor_tensor(counted, TB[1].t[:, 0:P].rearrange("p (g e) -> p g e", e=NE), chosen, ALU.mult)\
                    .then_inc(TB[1].drained.sem, 1)
                TB[1].wait_drained(eng, "place")
                step(eng.tensor_reduce(place, counted, AX.X, ALU.add))
                step(eng.tensor_scalar(kept, place, float(CAP), None, ALU.is_lt))
                step(eng.scalar_tensor_tensor(slot, expert_of, float(CAP), place, ALU.mult, ALU.add))
                step(eng.tensor_scalar(dropped, kept, -float(2 * NTOK), float(2 * NTOK), ALU.mult, ALU.add))
                step(eng.tensor_tensor(slot_put, slot, dropped, ALU.add))
                step(eng.tensor_tensor(slot_get, slot, kept, ALU.mult))
                eng.wait_ge(res_exp.sem, res_exp.after(L))
                k(eng.tensor_reduce(gs_[:, 0, :], ex_[:, :, 0:NE], AX.X, ALU.add))
                k(eng.reciprocal(gs_[:, 2, :], gs_[:, 0, :]))
                k(eng.tensor_reduce(gs_[:, 1, :], ex_[:, :, NE:NE + 2], AX.X, ALU.add))
                k(eng.reciprocal(gs_[:, 3, :], gs_[:, 1, :]))
                k(eng.tensor_tensor(coef0, ex_[:, :, NE], gs_[:, 3, :], ALU.mult))
                k(eng.tensor_tensor(gs_[:, 0, :], ex_[:, :, NE + 1], gs_[:, 3, :], ALU.mult))
                k(eng.tensor_tensor(gs_[:, 1, :], gs_[:, 0, :], gs_[:, 2, :], ALU.mult))
                k(eng.tensor_tensor(weight_of, gs_[:, 1, :], kept, ALU.mult))
                assert n == RES_STEPS, n
            else:
                eng.wait_ge(route_step.sem, 5)
                eng.wait_ge(zeroed.sem, 16)
                eng.wait_ge(normed_ready.sem, normed_ready.after(L, 1, NB - 1))
                for g in range(WHOLE):
                    eng.indirect_dma_start(out=dispatched_d, out_offset=bass.IndirectOffsetOnAxis(ap=slot_put[:, g:g + 1], axis=0),
                                           in_=normed[:, g, :], in_offset=None, bounds_check=NTOK - 1,
                                           oob_is_err=False).then_inc(scattered.sem, 16)

            if name != "pool":
                with eng.Fori(0, EARLY) as b:
                    mlp(b, L, b)

            if name != "pool":
                eng.wait_ge(loaded["ffn3"].sem, LOADS["ffn3"])
            if name == "pe":
                eng.wait_ge(sent_loaded.sem, 16)
                for i, bk in enumerate(FC_BANKS):
                    bk.wait_empty(eng, "sent")
                    for t in range(4):
                        last = eng.transpose(bk.t[:, t * P:(t + 1) * P], sent[:, 4 * i + t, :], ident[:, :])
                    last.then_inc(bk.full.sem, 1)
                for e in range(NE + 1):
                    if e < NE:
                        if e % 2 == 0:
                            FC_BANKS[e // 2].wait_drained(eng, "sent")
                        for i, bk in enumerate(tile_hidden(e)):
                            bk.wait_empty(eng, "experts", e // 2)
                            for c in range(2):
                                f = (2 * i + c) * P
                                last = eng.matmul(bk.t[:, c * 256:(c + 1) * 256], w1e[:, e, f:f + P],
                                                  sentT[:, e * CAP:(e + 1) * CAP], start=True, stop=True)
                            last.then_inc(bk.full.sem, 1)
                    if e > 0:
                        q = e - 1
                        bo = tile_out(q)
                        bo.wait_empty(eng, "experts", q // 2)
                        for bk in tile_hidden(q):
                            bk.wait_drained(eng, "experts", q // 2)
                        for c in range(NC):
                            for j in range(2):
                                col = (q % 2) * 256 + j * P
                                last = eng.matmul(bo.t[:, j * P:(j + 1) * P], hT[:, c, col:col + P], w2e[:, q, c, :],
                                                  start=c == 0 and j == 0, stop=c == NC - 1, skip_group_check=True)
                        last.then_inc(bo.full.sem, 1)
            elif name == "act":
                for i, bk in enumerate(FC_BANKS):
                    bk.wait_full(eng, "sent")
                    eng.activation(sentT[:, i * 512:(i + 1) * 512], bk.t[:, :], ACT.Copy).then_inc(bk.drained.sem, 1)
                for e in range(NE):
                    for i, bk in enumerate(tile_hidden(e)):
                        bk.wait_full(eng, "experts", e // 2)
                        for c in range(2):
                            col = (e % 2) * 256
                            last = eng.activation(hT[:, 2 * i + c, col:col + 256], bk.t[:, c * 256:(c + 1) * 256],
                                                  ACT.Gelu_apprx_tanh, bias=b1c[:, e, 2 * i + c:2 * i + c + 1])
                        last.then_inc(bk.drained.sem, 1)
            elif name == "dve":
                for e in range(NE):
                    bo = tile_out(e)
                    bo.wait_full(eng, "experts", e // 2)
                    eng.tensor_tensor(expert_out[:, 2 * e:2 * e + 2, :], bo.t[:, 0:256].rearrange("p (j d) -> p j d", j=2),
                                      spread(out_b_all[:, e, :], 1, 2), ALU.add).then_inc(bo.drained.sem, 1)
            else:
                eng.wait_ge(stored.sem, 16 * NE)
                for g in range(WHOLE):
                    eng.indirect_dma_start(out=got[:, g, :], out_offset=None, in_=expert_out_d,
                                           in_offset=bass.IndirectOffsetOnAxis(ap=slot_get[:, g:g + 1], axis=0))\
                        .then_inc(gathered[g // NT].sem, 16)

            if name != "pool":
                mlp(NB - 1, "L3f late", 0)
            if name == "dve":
                Y.wait_drained(eng, "L3f late")
                for b in range(NB):
                    eng.wait_ge(gathered[b].sem, 16 * NT)
                    for t in range(NT):
                        g = b * NT + t
                        last = eng.scalar_tensor_tensor(x[:, g, :], got[:, g, :], weight_of[:, g:g + 1], x[:, g, :],
                                                        ALU.mult, ALU.add)
                    last.then_inc(x_done.sem, 1)

        def route_constants_pool(pool):
            pool.wait_ge(x_done.sem, x_done.after("L2f", 0, NB - 1))
            pool.memset(earlier, 1.0).then_inc(pool_step.sem, 1)
            pool.wait_ge(pool_step.sem, POOL_STEPS + 1)
            pool.affine_select(out=earlier, in_=earlier, compare_op=ALU.is_gt, fill=0.0, base=0,
                               pattern=[[1, P]], channel_multiplier=-1).then_inc(route_made.sem, 1)
            pool.memset(onesb, 1.0).then_inc(route_made.sem, 1)

        POOL_STEPS = 7

        LOADS = {}
        MADE = 1

        PHB = TB[1]
        PHB.plan("phase", 11)
        plan_prep03("L0x")
        plan_attention("L0x")
        plan_ffn0()
        plan_prep1()
        plan_attention("L1x")
        plan_ffn1()
        plan_prep2()
        plan_attention("L2x")
        plan_ffn2()
        plan_prep03("L3x")
        plan_attention("L3x")
        plan_ffn3()

        WAVES = 10
        PHB = TB[1]
        phase_d = event("phase_dve")
        phase_a = event("phase_act")

        def start_pe(pe):
            for i in range(WAVES):
                if i == 0:
                    pe.wait_ge(loaded["const"].sem, LOADS["const"])
                    pe.wait_ge(phase_d.sem, 1)
                else:
                    pe.wait_ge(phase_a.sem, i)
                PHB.wait_empty(pe, "phase", i)
                pe.matmul(PHB.t[0:H16, 0:1], phw[:, 0:H16], ph[:, 0:1], start=True, stop=True)\
                    .then_inc(PHB.full.sem, 1)
                if i < PREP03_PARTS:
                    prep03_pe(pe, "L0x", i)
            pe.wait_ge(phase_d.sem, 1 + 5 * WAVES + 4)
            PHB.wait_empty(pe, "phase", WAVES)
            pe.matmul(PHB.t[:, 0:H16], ones16[:, :], dg[:, :], start=True, stop=True).then_inc(PHB.full.sem, 1)

        def start_dve(dve):
            dve.memset(ph[:, 0:1], 0.0).then_inc(phase_d.sem, 1)
            dve.memset(ones16[:, :], 1.0)
            dve.wait_ge(loaded["const"].sem, LOADS["const"])
            dve.wait_ge(made.sem, MADE)
            n = 1

            def step(ins):
                nonlocal n
                n += 1
                ins.then_inc(phase_d.sem, 1)
                dve.wait_ge(phase_d.sem, n)

            for i in range(WAVES):
                PHB.wait_full(dve, "phase", i)
                dve.tensor_scalar(ph[:, 1:2], PHB.t[0:H16, 0:1], ph[:, 7:8], phw[:, 16:17], ALU.mult, ALU.add)\
                    .then_inc(PHB.drained.sem, 1)
                PHB.wait_drained(dve, "phase", i)
                step(dve.tensor_scalar(ph[:, 2:3], ph[:, 1:2], 0.01, None, ALU.mult))
                step(dve.tensor_scalar(ph[:, 3:4], ph[:, 2:3], 1.0 / TWO_PI, None, ALU.mult))
                step(dve.tensor_scalar(ph[:, 4:5], ph[:, 3:4], ROUND, None, ALU.add))
                step(dve.tensor_scalar(ph[:, 5:6], ph[:, 4:5], ROUND, -TWO_PI, ALU.subtract, ALU.mult))
                if i:
                    dve.wait_ge(phase_a.sem, i)
                step(dve.tensor_tensor(ph[:, 6:7], ph[:, 5:6], ph[:, 2:3], ALU.add))
                if i < PREP03_PARTS:
                    prep03_dve(dve, "L0x", i)
                if i == 5:
                    front_dve(dve, "L0x", 0)
                if i == 6:
                    ternary_scales_dve(dve)
            step(dve.tensor_scalar(ph[:, 3:4], ph[:, 6:7], -1.0, None, ALU.mult))
            step(dve.tensor_tensor(ph[:, 1:2], ph[:, 6:7], ph[:, 3:4], ALU.min))
            step(dve.tensor_scalar(ph[:, 2:3], ph[:, 1:2], math.pi / 2, None, ALU.add))
            dve.wait_ge(phase_a.sem, WAVES + 1)
            step(dve.tensor_scalar(dg[:, :], ident[0:H16, 0:H16], ph[:, 8:9], 0.1, ALU.mult, ALU.mult))
            PHB.wait_full(dve, "phase", WAVES)
            dve.tensor_copy(head_bias[:, :], PHB.t[:, 0:H16]).then_inc(PHB.drained.sem, 1)
            PHB.wait_drained(dve, "phase", WAVES)

        def start_act(act):
            for i in range(WAVES):
                act.wait_ge(phase_d.sem, 1 + 5 * (i + 1))
                act.activation(ph[:, 0:1], ph[:, 6:7], ACT.Sin).then_inc(phase_a.sem, 1)
                if i < PREP03_PARTS:
                    prep03_act(act, "L0x", i)
            act.wait_ge(phase_d.sem, 1 + 5 * WAVES + 3)
            act.activation(ph[:, 8:9], ph[:, 2:3], ACT.Sin).then_inc(phase_a.sem, 1)

        LOADS.update({"const": 48, "w0": 80, "ctx": 16, "ffn0": 96, "attn1": 80, "mask1": 32, "ffn1": 64,
                      "attn2": 80, "attn3": 64, "ffn2": 160, "mask3": 16, "small3": 10 * 16, "ffn3": 4 * 16})

        block = ctx.enter_context(nc.Block())

        @block.sync
        def _(sp):
            load(sp, "ctx", ctx_tok[:, :, :], a["ctx_1024"].rearrange("b k d -> k b d"))
            for i, n in enumerate(("Wq", "Wk", "Wv")):
                load(sp, "w0", w0[:, i, :].rearrange("d (h k) -> d h k", h=H16),
                     a["L0_xattn_" + n].rearrange("h d k -> d h k"))
            load(sp, "x", x[:, :, :], a["x"].rearrange("b (t p) d -> p (b t) d", p=P))
            load(sp, "w0", w0[:, 3, :], a["L0_xattn_out_w"])
            load(sp, "w0", rows[0:1, 0, :], a["L0_xattn_out_b"].rearrange("(a n) -> a n", a=1))
            sp.wait_ge(zeros_made.sem, 1)
            sp.dma_start(dispatched_d.rearrange("(p r) d -> p (r d)", p=P), hT[:, :, :].rearrange("p c n -> p (c n)"))\
                .then_inc(zeroed.sem, 16)
            load(sp, "ffn0", wfc[:, :, :], a["L0_ffn_w_fc"].rearrange("(c p) d -> p c d", p=P))
            load(sp, "ffn0", wpr[:, :], a["L0_ffn_w_proj"])
            load(sp, "ffn0", lr[:, :, :], a["L0_ffn_u"].rearrange("(c p) r -> p c r", p=P))
            with nc.allow_non_contiguous_dma(reason="a 16x16 transpose"):
                load(sp, "ffn0", fbT[:, :], a["L0_ffn_fast_b"].rearrange("i j -> j i"))
            load(sp, "ffn0", vlow[:, :], a["L0_ffn_v"])
            load(sp, "ffn0", gate[:, :], a["L0_ffn_gate"].rearrange("(a n) -> a n", a=1).broadcast_to([16, 1]))
            for n, dst in (("Wq", w1q), ("Wk", w1k), ("Wv", w1v)):
                load(sp, "attn1", dst, a["L1_xattn_" + n].rearrange("(c p) d -> p c d", p=P))
            load(sp, "attn1", w1o, a["L1_xattn_Wo"])
            load(sp, "attn1", rows[0:1, 1, :], a["L1_xattn_bo"].rearrange("(a n) -> a n", a=1))
            load(sp, "mask1", mask_raw[:, :, :], a["mask_Bx1xSxS2_ik0"].rearrange("b o (t p) k -> p (b o t) k", p=P))
            load(sp, "mask1", src_raw[:, :, :].rearrange("p b k -> p (b k)"),
                 a["mask_Bx1xS2_bk0"].bitcast(U8).rearrange("(a n) -> a n", a=1).broadcast_to([P, NB * CK]))
            load(sp, "ffn1", we[:, :, :], a["L1_ffn_We"].rearrange("e d o -> d e o"))
            load(sp, "ffn1", be[:, :], a["L1_ffn_be"])
            load(sp, "ffn1", wg1[:, :], a["L1_ffn_Wg"])
            load(sp, "ffn1", bg1[:, :], a["L1_ffn_bg"].rearrange("(a n) -> a n", a=1).broadcast_to([P, NE]))
            for i, n in enumerate(("Wq", "Wk", "Wv", "Wp")):
                load(sp, "attn2", w2[:, i, :], a["L2_xattn_" + n])
            load(sp, "attn2", rows[0:1, 2, :], a["L2_xattn_bp"].rearrange("(a n) -> a n", a=1))
            for i, n in enumerate(("wq", "wk", "wv", "w_out")):
                load(sp, "attn3", w3[:, i, :], a["L3_xattn_" + n])
            load(sp, "ffn2", attn_w[:, :], a["L2_ffn_attn_w"])
            load(sp, "ffn2", next_w[:, :], a["L2_ffn_next_w"])
            load(sp, "ffn2", rows[0:1, 3, :], a["L2_ffn_next_b"].rearrange("(a n) -> a n", a=1))
            with nc.allow_non_contiguous_dma(reason="biases as columns"):
                for i, n in enumerate(("ln_g", "ln_b", "attn_b")):
                    load(sp, "ffn2", cols2[:, i:i + 1], a["L2_ffn_" + n].rearrange("(n a) -> n a", a=1))
                load(sp, "ffn2", b1c[:, :, :], a["L2_ffn_b1"].rearrange("e (c p) -> p e c", p=P))
                load(sp, "ffn2", b2c[:, :], a["L2_ffn_b2"].rearrange("e d -> d e"))
            if len(LAYERS) > 2:
                sp.wait_ge(mask_made.sem, 2 + NB)
            load(sp, "mask3", mask_raw[:, :, :], a["mask_BxSxS2_ik1"].rearrange("b (t p) k -> p (b t) k", p=P))
            if len(LAYERS) > 2:
                TB[1].wait_full(sp, "prepL1x", 3 + NB)
                load(sp, "ffn2", w1e, a["L2_ffn_w1"].rearrange("e d f -> d e f"))
                load(sp, "ffn2", w2e, a["L2_ffn_w2"].rearrange("e (c p) d -> p e c d", p=P))
            if len(LAYERS) > 7:
                sp.wait_ge(x_done.sem, x_done.after("L2f", 0, NB - 1))
                load(sp, "small3", nw_all, a["L3_ffn_attn_nw"].rearrange("(a n) -> a n", a=1).broadcast_to([P, P]))
                load(sp, "small3", nb_all, a["L3_ffn_attn_nb"].rearrange("(a n) -> a n", a=1).broadcast_to([P, P]))
                load(sp, "small3", wgc[:, 0:NE], a["L3_ffn_wg"])
                load(sp, "small3", wgc[:, NE:NE + 2], a["L3_ffn_res_coef"])
                load(sp, "small3", res_w1, a["L3_ffn_res_inter_w"])
                load(sp, "small3", res_w2[:, :, :], a["L3_ffn_res_output_w"].rearrange("(c p) d -> p c d", p=P))
                load(sp, "small3", rows[0:1, 4, :], a["L3_ffn_res_output_b"].rearrange("(a n) -> a n", a=1))
                with nc.allow_non_contiguous_dma(reason="biases as columns"):
                    load(sp, "ffn3", b1c[:, :, :], a["L3_ffn_inter_b"].rearrange("e (c p) -> p e c", p=P))
                    load(sp, "small3", cols3[:, 0:1], a["L3_ffn_attn_nw"].rearrange("(n a) -> n a", a=1))
                    load(sp, "small3", cols3[:, 1:2], a["L3_ffn_attn_nb"].rearrange("(n a) -> n a", a=1))
                    load(sp, "small3", cols3[:, 2:2 + NC], a["L3_ffn_res_inter_b"].rearrange("(c p) -> p c", p=P))
                load(sp, "ffn3", w1e, a["L3_ffn_inter_w"].rearrange("e d f -> d e f"))
                load(sp, "ffn3", w2e, a["L3_ffn_output_w"].rearrange("e (c p) d -> p e c d", p=P))
                sp.wait_ge(x_done.sem, x_done.after("L3x", 0, NB - 1))
                load(sp, "ffn3", out_b_all.rearrange("p e d -> p (e d)"),
                     a["L3_ffn_output_b"].rearrange("(a e) d -> a (e d)", a=1).broadcast_to([P, NE * P]))
            assert len(LAYERS) < 8 or all(loads[k] == v for k, v in LOADS.items() if k != "const"), loads
            if len(LAYERS) > 7:
                sp.wait_ge(scattered.sem, 16 * NB * NT)
                sp.dma_start(sent, dispatched_d.rearrange("(g p) d -> p g d", p=P)).then_inc(sent_loaded.sem, 16)
                for e in range(NE):
                    bo = O if e % 2 == 0 else Y
                    bo.wait_drained(sp, "experts", e // 2)
                    sp.dma_start(expert_out_d[e * CAP:(e + 1) * CAP, :].rearrange("(j p) d -> p j d", p=P),
                                 expert_out[:, 2 * e:2 * e + 2, :]).then_inc(stored.sem, 16)
            for b in range(NB):
                sp.wait_ge(x_done.sem, x_done.after(LAYERS[-1], 0, b))
                sp.dma_start(out[b].rearrange("(t p) d -> p t d", p=P), x[:, b * NT:(b + 1) * NT, :])\
                    .then_inc(out_done.sem, 16)
            sp.wait_ge(out_done.sem, 16 * NB)
            if len(LAYERS) < 8:
                sp.wait_ge(zeroed.sem, 16)
            for n in loaded:
                if loads[n] and n != "const":
                    sp.wait_ge(loaded[n].sem, loads[n])

        @block.gpsimd
        def _(pool):
            for bk in BANKS:
                pool.sem_inc(bk.drained.sem, 1)
            pool.sem_inc(pool_sum.sem, pool_sum.credit)
            pool.sem_inc(normed_ready.sem, normed_ready.credit)
            k = [0]

            def step(ins):
                k[0] += 1
                ins.then_inc(pool_step.sem, 1)
                pool.wait_ge(pool_step.sem, k[0])

            pool.memset(ident[:, :], 0.0)
            pool.memset(blk[:, :], 1.0)
            step(pool.memset(ctxT[:, :, :], 0.0))
            pool.affine_select(out=ident[:, :], in_=ident[:, :], compare_op=ALU.not_equal, fill=1.0, base=0,
                               pattern=[[-1, P]], channel_multiplier=1)
            step(pool.affine_select(out=blk[:, :], in_=blk[:, :], compare_op=ALU.is_ge, fill=0.0, base=0,
                                    pattern=[[-8, H16]], channel_multiplier=1))
            pool.affine_select(out=blk[:, :], in_=blk[:, :], compare_op=ALU.is_ge, fill=0.0, base=7,
                               pattern=[[8, H16]], channel_multiplier=-1).then_inc(made.sem, 1)
            for r in range(3):
                last = pool.tensor_copy(key_of_row[:, r * CK:(r + 1) * CK], ident[:, 0:CK])
            last.then_inc(rep_made.sem, 1)
            pool.memset(grid[:, :, :], 1.0)
            pool.memset(minus_half[:, :], -0.5)
            pool.memset(eps5[:, :], EPS)
            pool.memset(eps12[:, :], EPS3)
            pool.memset(ones[:, :], 1.0)
            pool.tensor_copy(identb[:, :], ident[:, :])
            pool.memset(V2[:, :, :, 64], 1.0)
            step(pool.memset(causal[:, :], 0.0))
            step(pool.affine_select(out=causal[:, :], in_=causal[:, :], compare_op=ALU.is_ge, fill=-1e13, base=0,
                                    pattern=[[-1, CK]], channel_multiplier=1))
            step(pool.iota(iota8[:, :], pattern=[[1, NE]], base=0, channel_multiplier=0,
                           allow_small_or_imprecise_dtypes=True))
            for c, h0 in enumerate(CHUNK_HEAD):
                last = pool.affine_select(out=grid[:, c, :], in_=grid[:, c, :], compare_op=ALU.is_ge, fill=0.0,
                                          base=P * c - CK * h0, pattern=[[-CK, 3]], channel_multiplier=1)
            step(last)
            for c, h0 in enumerate(CHUNK_HEAD):
                last = pool.affine_select(out=grid[:, c, :], in_=grid[:, c, :], compare_op=ALU.is_ge, fill=0.0,
                                          base=CK - 1 - P * c + CK * h0, pattern=[[CK, 3]], channel_multiplier=-1)
            step(last)
            pool.tensor_copy(V03[:, :, :, :, 8], spread(grid[:, :, :], 1, NB)).then_inc(grid_made.sem, 1)
            assert k[0] == POOL_STEPS, k
            pool.memset(hT[:, :, :], 0.0).then_inc(zeros_made.sem, 1)
            for L in LAYERS:
                if L in ATT:
                    run_attention(pool, "pool", L)
                if L == "L0f":
                    run_ffn0(pool, "pool")
                if L == "L1f":
                    run_ffn1(pool, "pool")
                if L == "L2f":
                    run_ffn2(pool, "pool")
                if L == "L3f":
                    route_constants_pool(pool)
                    run_ffn3(pool, "pool")

        @block.scalar
        def _(act):
            load(act, "const", phw[:, 0:H16], a["phase_weights"])
            load(act, "const", phw[:, 16:17], a["phase_intrinsic"])
            load(act, "const", ph[:, 7:8], a["L0_xattn_coupling"].rearrange("(n a) -> n a", a=1))
            start_act(act)
            for L in LAYERS:
                if L == "L3x":
                    for part in range(5):
                        prep03_act(act, L, part)
                if L == "L1x":
                    prep1_act(act)
                if L == "L2x":
                    prep2_act(act)
                if L == "L0f":
                    prep_ffn0_act(act)
                if L in ATT:
                    run_attention(act, "act", L)
                if L == "L0f":
                    run_ffn0(act, "act")
                if L == "L1f":
                    run_ffn1(act, "act")
                if L == "L2f":
                    run_ffn2(act, "act")
                if L == "L3f":
                    run_ffn3(act, "act")

        @block.vector
        def _(dve):
            start_dve(dve)
            for L in LAYERS:
                if L == "L3x":
                    for part in range(5):
                        prep03_dve(dve, L, part)
                if L == "L1x":
                    prep1_dve(dve)
                if L == "L2x":
                    prep2_dve(dve)
                if L == "L0f":
                    prep_ffn0_dve(dve)
                if L == "L3x":
                    dve.wait_ge(loaded["mask3"].sem, LOADS["mask3"])
                    dve.tensor_scalar(mask3[:, :, :], mask_raw[:, :, :], 1.0, MASKED, ALU.is_equal, ALU.mult)\
                        .then_inc(mask_made.sem, 1)
                if L == "L1f":
                    dve.wait_ge(loaded["ffn1"].sem, LOADS["ffn1"])
                if L in ATT:
                    run_attention(dve, "dve", L)
                if L == "L0f":
                    run_ffn0(dve, "dve")
                if L == "L1f":
                    run_ffn1(dve, "dve")
                if L == "L2f":
                    run_ffn2(dve, "dve")
                if L == "L3f":
                    run_ffn3(dve, "dve")

        @block.tensor
        def _(pe):
            start_pe(pe)
            for L in LAYERS:
                if L == "L3x":
                    for part in range(5):
                        prep03_pe(pe, L, part)
                if L == "L1x":
                    prep1_pe(pe)
                if L == "L2x":
                    prep2_pe(pe)
                if L == "L0f":
                    prep_ffn0_pe(pe)
                if L == "L1x":
                    pe.wait_ge(mask_made.sem, 2 + NB)
                if L == "L3x":
                    pe.wait_ge(mask_made.sem, 3 + NB)
                if L == "L1f":
                    pe.wait_ge(loaded["ffn1"].sem, LOADS["ffn1"])
                if L in ATT:
                    if L == "L2x":
                        prepared_pe(pe, L)
                    elif L == "L1x":
                        for h in range(H16 - 4, H16):
                            bk, u = head_bank(h)
                            bk.wait_drained(pe, "prepL1x", u)
                    elif L == "L3x":
                        for bk, u in G_BANKS[L]:
                            bk.wait_drained(pe, "prepL3x", u)
                    run_attention(pe, "pe", L)
                if L == "L0f":
                    run_ffn0(pe, "pe")
                if L == "L1f":
                    run_ffn1(pe, "pe")
                if L == "L2f":
                    run_ffn2(pe, "pe")
                if L == "L3f":
                    run_ffn3(pe, "pe")


def phase_tables():
    side = 4
    w = np.zeros((H16, H16), np.float32)
    for i in range(H16):
        for j in range(i):
            dr, dc = j // side - i // side, j % side - i % side
            if abs(dr) <= 1 and abs(dc) <= 1:
                w[j, i] = math.exp(-math.hypot(dr, dc))
    f = np.asarray([[1.0 + 0.1 * h] for h in range(H16)], np.float32)
    return w, f


_INS = ['x', 'ctx_1024', 'mask_Bx1xSxS2_ik0', 'mask_Bx1xS2_bk0', 'mask_BxSxS2_ik1', 'L0_xattn_Wq', 'L0_xattn_Wk', 'L0_xattn_Wv', 'L0_xattn_out_w', 'L0_xattn_out_b', 'L0_xattn_coupling', 'L0_ffn_fast_b', 'L0_ffn_w_fc', 'L0_ffn_w_proj', 'L0_ffn_u', 'L0_ffn_v', 'L0_ffn_gate', 'L1_xattn_Wq', 'L1_xattn_Wk', 'L1_xattn_Wv', 'L1_xattn_Wo', 'L1_xattn_bo', 'L1_ffn_We', 'L1_ffn_be', 'L1_ffn_Wg', 'L1_ffn_bg', 'L2_xattn_Wq', 'L2_xattn_Wk', 'L2_xattn_Wv', 'L2_xattn_Wp', 'L2_xattn_bp', 'L2_ffn_ln_g', 'L2_ffn_ln_b', 'L2_ffn_attn_w', 'L2_ffn_attn_b', 'L2_ffn_w1', 'L2_ffn_b1', 'L2_ffn_w2', 'L2_ffn_b2', 'L2_ffn_next_w', 'L2_ffn_next_b', 'L3_xattn_wq', 'L3_xattn_wk', 'L3_xattn_wv', 'L3_xattn_w_out', 'L3_ffn_attn_nw', 'L3_ffn_attn_nb', 'L3_ffn_wg', 'L3_ffn_inter_w', 'L3_ffn_inter_b', 'L3_ffn_output_w', 'L3_ffn_output_b', 'L3_ffn_res_inter_w', 'L3_ffn_res_inter_b', 'L3_ffn_res_output_w', 'L3_ffn_res_output_b', 'L3_ffn_res_coef']


def kernel(**inputs):
    import numpy as _np
    import concourse.bacc as _bacc
    from concourse import mybir as _mybir
    from concourse.bass_utils import run_bass_kernel_spmd as _run

    nc = _bacc.Bacc("TRN2", target_bir_lowering=False, num_devices=1)
    arrays, args = {}, {}

    def give(name, a):
        arrays[f"in_{name}_dram"] = a
        args[name] = nc.dram_tensor(f"in_{name}_dram", a.shape, _mybir.dt.from_np(a.dtype), kind="ExternalInput").ap()

    for name in _INS:
        a = _np.ascontiguousarray(inputs[name])
        if a.dtype == _np.bool_:
            a = a.reshape(-1).view(_np.int32)
        if a.shape == ():
            a = a.reshape(1)
        give(name, a)
    w, f = phase_tables()
    give("phase_weights", w)
    give("phase_intrinsic", f)
    o = nc.dram_tensor("out_0_dram", (NB, NT * P, P), _mybir.dt.float32, kind="ExternalOutput").ap()
    four_layers(nc, args, o)
    r = _run(nc, [arrays], core_ids=[0])
    return r.results[0]["out_0_dram"]
```

```python
import math
from contextlib import ExitStack

import numpy as np

import concourse.bass as bass
from concourse import mybir

F32 = mybir.dt.float32
BF16 = mybir.dt.bfloat16
I32 = mybir.dt.int32
U32 = mybir.dt.uint32
U8 = mybir.dt.uint8
ALU = mybir.AluOpType
ACT = mybir.ActivationFunctionType
AX = mybir.AxisListType

P = 128
NB = 4
NT = 4
NTOK = NB * NT * P
CK = 77
NE = 8
FF = 512
NC = FF // P
CAP = NTOK // NE
EPS = 1e-5
EPS3 = 1e-12
MASKED = -float(2.0 ** 100)
TWO_PI = 2.0 * math.pi
ROUND = 1.5 * 2.0 ** 23

H16 = 16
BANK_HEADS = [(0, 6), (6, 12), (12, 16)]
ROWS16 = H16 * CK
CHUNKS16 = [(s, min(P, ROWS16 - s)) for s in range(0, ROWS16, P)]
CHUNK_HEAD = [min(s // CK, H16 - 3) for s, _ in CHUNKS16]


class Event:

    def __init__(self, nc, ctx, name, credit=0):
        self.sem = ctx.enter_context(nc.semaphore(name))
        self.credit = credit
        self.total = credit
        self.base = {}

    def plan(self, phase, per, reps=1):
        self.base[phase] = (self.total, per)
        self.total += per * reps

    def after(self, phase, j=0, b=0):
        base, per = self.base[phase]
        return b * per + (base + j + 1)


class Bank:
    def __init__(self, nc, ctx, name):
        self.t = ctx.enter_context(nc.psum_tensor(name, [P, 512], F32))
        self.full = Event(nc, ctx, name + "_full")
        self.drained = Event(nc, ctx, name + "_drained", credit=1)

    def plan(self, phase, per, reps=1):
        self.full.plan(phase, per, reps)
        self.drained.plan(phase, per, reps)

    def wait_empty(self, pe, phase, j=0, b=0):
        pe.wait_ge(self.drained.sem, self.drained.after(phase, j - 1, b))

    def wait_full(self, eng, phase, j=0, b=0):
        eng.wait_ge(self.full.sem, self.full.after(phase, j, b))

    def wait_drained(self, eng, phase, j=0, b=0):
        eng.wait_ge(self.drained.sem, self.drained.after(phase, j, b))


def spread(ap, axis, n):
    v = ap.unsqueeze(axis)
    shape = list(v.shape)
    shape[axis] = n
    return v.broadcast_to(shape)


def four_layers(nc, a, out):
    ctx = ExitStack()
    with ctx:
        def sb(name, shape, dt=F32):
            return ctx.enter_context(nc.sbuf_tensor(name, shape, dt))

        def event(name, credit=0):
            return Event(nc, ctx, name, credit)

        S = [Bank(nc, ctx, f"scores{i}") for i in range(3)]
        TB = [Bank(nc, ctx, f"probsT{i}") for i in range(2)]
        O = Bank(nc, ctx, "mixed")
        X = Bank(nc, ctx, "transposed")
        Y = Bank(nc, ctx, "result")
        BANKS = S + TB + [O, X, Y]

        x = sb("x", [P, NB * NT, P])
        xn = sb("xn", [P, NT, P])
        z = sb("z", [P, NT, P])
        xnT = sb("xnT", [P, NT * P])
        stats = sb("stats", [P, NT, 6])
        mv = sb("mv", [P, NT, 2])
        ve = sb("ve", [P, NT])
        rstd = sb("rstd", [P, NT])
        stats_z = sb("stats_z", [P, NT, 6])
        mv_z = sb("mv_z", [P, NT, 2])
        ve_z = sb("ve_z", [P, NT])
        rstd_z = sb("rstd_z", [P, NT])
        minus_half = sb("minus_half", [P, NT])
        eps5 = sb("eps5", [P, NT])
        eps12 = sb("eps12", [P, NT])
        prob = sb("prob", [P, NT, ROWS16])
        probT = sb("probT", [P, 10 * P])
        mx = sb("mx", [P, 2, H16])
        rden = sb("rden", [P, 2, H16])
        mix = sb("mix", [P, NT, P])
        mixT = sb("mixT", [P, NT * P])
        hT = sb("hT", [P, NC, 512])
        ident = sb("ident", [P, P])
        identb = sb("identb", [P, P], BF16)
        ones = sb("ones", [1, P])
        blk = sb("blk", [P, H16])
        grid = sb("grid", [P, 10, 3])
        key_of_row = sb("key_of_row", [P, 3 * CK])
        ctx_all = sb("ctx_tok", [P, NB, P])
        ctx_tok = ctx_all[0:CK, :, :]
        keysT = sb("keysT", [P, NB, CK])[:, :, :]
        GA = sb("GA", [P, NB, H16, CK])
        GB = sb("GB", [P, NB, H16, CK])
        G2 = sb("G2", [P, NB, 2, CK])
        V03 = sb("V03", [P, NB, 10, 3, 9])
        V1 = sb("V1", [P, NB, 10, P])
        V2 = sb("V2", [P, NB, 2, 65])
        mask1 = sb("mask1", [P, NB * NT, CK], BF16)
        mask3 = sb("mask3", [P, NB * NT, CK], BF16)
        mask_raw = sb("mask_raw", [P, NB * NT, CK], I32)
        src_raw = sb("src_raw", [P, NB, CK], U8)
        src_bias = sb("src_bias", [P, NB, CK], BF16)
        causal = sb("causal", [P, CK])
        w0 = sb("w0", [P, 4, P])
        w3 = sb("w3", [P, 4, P])
        w2 = sb("w2", [P, 4, P])
        wT = sb("wT", [P, 3, P])
        out_wT = sb("out_wT", [P, 2, P])
        rows = sb("rows", [1, 6, P])
        head_bias = sb("head_bias", [P, H16])
        wfc = sb("wfc", [P, NC, P])
        wpr = sb("wpr", [P, NC * P])
        wt1 = sb("wt1", [P, NC, P])
        wt2 = sb("wt2", [P, NC, P])
        wfcT = sb("wfcT", [P, NC * P])
        wprT = sb("wprT", [P, NC, P])
        lr = sb("lr", [P, NC, 16])
        lrT = sb("lrT", [16, FF])
        fbT = sb("fbT", [16, 16])
        vlow = sb("vlow", [16, P])
        gate = sb("gate", [16, 1])
        bv = sb("bv", [16, P])
        wsc = sb("wsc", [P, 2, 16])
        we = sb("we", [P, NE, P])
        be = sb("be", [NE, P])
        wg1 = sb("wg1", [P, NE])
        bg1 = sb("bg1", [P, NE])
        attn_w = sb("attn_w", [P, P])
        next_w = sb("next_w", [P, P])
        cols2 = sb("cols2", [P, 3])
        b1c = sb("b1c", [P, NE, NC])
        b2c = sb("b2c", [P, NE])
        big = sb("big", [P, 2, NE * FF])
        iota8 = sb("iota8", [P, NE])
        ph = sb("ph", [H16, 24])
        phw = sb("phw", [H16, H16 + 2])
        dg = sb("dg", [H16, H16])
        ones16 = sb("ones16", [H16, P])
        gsel = sb("gsel", [P, NT, NE])
        gT = sb("gT", [NE, NT * P])
        a2 = sb("a2", [P, 2, P])
        xaT = wt1[:, :, :].rearrange("p c d -> p (c d)")
        gout = wt2[:, :, :].rearrange("p c d -> p (c d)")

        wgc = sb("wgc", [P, NE + 2])
        cols3 = sb("cols3", [P, 2 + NC])
        route = ctx_all[:, :, :].rearrange("p b d -> p (b d)")
        earlier = route[:, 0:64].bitcast(BF16)
        onesb = route[:, 64:128].bitcast(BF16)
        chosen = route[:, 128:192].bitcast(BF16).rearrange("p (g e) -> p g e", e=NE)
        expert_of, weight_of, coef0, place, kept, slot = (route[:, 192 + 16 * i:208 + 16 * i] for i in range(6))
        slot_put = route[:, 288:304].bitcast(U32)
        token_of_slot = route[:, 304:320].bitcast(U32)
        dropped = route[:, 448:464]
        token_number = route[:, 464:480].bitcast(I32)
        counted = route[:, 320:448].rearrange("p (g e) -> p g e", e=NE)
        v1f = V1[:, :, :, :].rearrange("p b c d -> p (b c d)")
        gbf = GB[:, :, :, :].rearrange("p b h k -> p (b h k)")
        SENT = P + 1
        ROWS_SENT = NTOK // P * SENT
        normed = v1f[:, 0:ROWS_SENT].rearrange("p (g d) -> p g d", d=SENT)
        expert_out = v1f[:, ROWS_SENT:ROWS_SENT + NTOK].rearrange("p (g d) -> p g d", d=P)
        nw_all, nb_all = (v1f[:, ROWS_SENT + NTOK + i * P:ROWS_SENT + NTOK + (i + 1) * P] for i in range(2))
        sent = gbf[:, 0:ROWS_SENT].rearrange("p (g d) -> p g d", d=SENT)
        sentT = gbf[:, ROWS_SENT:ROWS_SENT + NTOK]
        got = prob[:, :, :].rearrange("p t n -> p (t n)")[:, 0:2048].rearrange("p (g d) -> p g d", d=P)
        res_w1 = w0[:, :, :].rearrange("p c d -> p (c d)")
        res_w2 = w2
        out_b_all = GA[:, :, :, :].rearrange("p b h k -> p (b h k)")[:, 0:NE * P].rearrange("p (e d) -> p e d", d=P)
        dispatched_d = nc.dram_tensor("dispatched", [NTOK, SENT], F32, kind="Internal").ap()
        returned_d = nc.dram_tensor("returned", [NTOK, P], F32, kind="Internal").ap()

        w1q = big[:, 0, 0:1024].rearrange("p (c d) -> p c d", c=8)
        w1k = big[:, 0, 1024:2048].rearrange("p (c d) -> p c d", c=8)
        w1v = big[:, 0, 2048:3072].rearrange("p (c d) -> p c d", c=8)
        w1o = big[:, 0, 3072:4096]
        w1oT = big[:, 1, 0:1024].rearrange("p (c d) -> p c d", c=8)
        head_mat = big[:, 1, 1024:3072].rearrange("p (q c d) -> p q c d", q=2, c=8)

        loaded = {}
        for n in ("x", "const", "w0", "ctx", "mask1", "mask3", "ffn0", "attn1", "ffn1", "attn2", "ffn2", "attn3", "small3", "ffn3"):
            loaded[n] = event("loaded_" + n)
        made = event("constants_made")
        rep_made = event("key_of_row_made")
        grid_made = event("grid_made")
        lhs_ready = event("tiles_staged")
        selected = event("gates_selected")
        pool_sum = event("pool_sum", credit=6)
        pool_step = event("pool_step")
        stats_ready = event("stats_ready")
        passed = event("passed")
        pool_passed = event("pool_passed")
        mv_ready = event("mv_ready")
        ve_ready = event("ve_ready")
        rstd_ready = event("rstd_ready")
        xn_ready = event("xn_ready")
        stats3_ready = event("stats3_ready")
        mv3_ready = event("mv3_ready")
        ve3_ready = event("ve3_ready")
        rstd3_ready = event("rstd3_ready")
        xn3_ready = event("xn3_ready")
        z_ready = event("z_ready")
        max_ready = event("max_ready")
        exp_ready = event("exp_ready")
        den_ready = event("den_ready")
        scaled_ready = event("scaled_ready")
        square_ready = [event(f"square_ready{c}") for c in range(NC)]
        dve_prep = event("dve_prep")
        out_done = event("out_done")
        x_done = event("x_done")
        gate_step = event("gate_step")
        gate_exp = event("gate_exp")
        chain = event("chain")
        mask_made = event("mask_made")
        zeroed = event("dram_zeroed")
        ZEROED = 3 * 16
        token_known = event("token_of_slot_known")
        zeros_made = event("zeros_made")
        base_added = event("base_added")
        normed_ready = event("normed_ready", credit=2)
        res_step = event("res_step")
        res_exp = event("res_exp")
        route_made = event("route_made")
        route_step = event("route_step")
        scattered = event("scattered")
        sent_loaded = event("sent_loaded")
        returned = event("returned")
        gathered = [event(f"gathered{b}") for b in range(NB)]
        tern_scale = event("ternary_scale")
        tern = event("ternary_step")

        loads = {n: 0 for n in loaded}

        def load(eng, group, dst, src, **kw):
            loads[group] += 16
            eng.dma_start(dst, src, **kw).then_inc(loaded[group].sem, 16)

        ATT = {
            "L0x": dict(H=16, G=GA, V=V03, dv=8, scale=8 ** -0.5, mask=None, row=0, wout=w0[:, 3, :], fold=False, bias=True),
            "L1x": dict(H=16, G=GB, V=V1, dv=P, scale=64 ** -0.5, mask=mask1, row=1, wout=None, fold=True, bias=False),
            "L2x": dict(H=2, G=G2, V=V2, dv=64, scale=64 ** -0.5, mask="causal", row=2, wout=out_wT[:, 0, :], fold=False, bias=False),
            "L3x": dict(H=16, G=GA, V=V03, dv=8, scale=8 ** -0.5, mask=mask3, row=None, wout=out_wT[:, 1, :], fold=False, bias=False),
        }
        LAYERS = ["L0x", "L0f", "L1x", "L1f", "L2x", "L2f", "L3x", "L3f"]

        def plan_norm(L):
            for e in (stats_ready, mv_ready, ve_ready, rstd_ready):
                e.plan(L, 2 if L in ("L2f", "L3f") else 1, NB)
            xn_ready.plan(L, 1, NB)
            if L in ("L2f", "L3f"):
                z_ready.plan(L, 1, NB)

        def plan_attention(L):
            c = ATT[L]
            plan_norm(L)
            if c["H"] == 2:
                for bk in (S[0], S[1], S[2], TB[0], TB[1], X, Y):
                    bk.plan(L, 1, NB)
                O.plan(L, 2, NB)
                for e in (max_ready, exp_ready, den_ready):
                    e.plan(L, 2, NB)
                x_done.plan(L, 1, NB)
                return
            for bk in S:
                bk.plan(L, NT, NB)
            TB[0].plan(L, 2 * NT, NB)
            TB[1].plan(L, NT, NB)
            max_ready.plan(L, 3 if c["bias"] else 1, NB * NT)
            exp_ready.plan(L, NT, NB)
            den_ready.plan(L, 2 if c["fold"] else 1, NB * NT)
            if c["fold"]:
                scaled_ready.plan(L, NT, NB)
                O.plan(L, 2, NB); Y.plan(L, 2, NB); X.plan(L, 1, NB)
            else:
                O.plan(L, NT + 1, NB); X.plan(L, 1, NB)
                if L == "L3x":
                    Y.plan(L, 1)
                    Y.plan("L3x with norm", 3, NB - 1)
                else:
                    Y.plan(L, 1, NB)
            x_done.plan(L, 1, NB)

        def prev_of(L, b):
            i = LAYERS.index(L)
            return None if i == 0 else LAYERS[i - 1]

        INNER = {"L2f", "L3f"}

        def ln_stats_dve(dve, L, b, j=0, stats=stats, mv=mv):
            if j == 0:
                p = prev_of(L, b)
                if p is None:
                    dve.wait_ge(loaded["x"].sem, 16)
                else:
                    dve.wait_ge(x_done.sem, x_done.after(p, 0, b))
            else:
                dve.wait_ge(xn_ready.sem, xn_ready.after(L, 0, b))
            for t in range(NT):
                last = dve.bn_stats(stats[:, t, :], x[:, b * NT + t, :] if j == 0 else xn[:, t, :])
            last.then_inc(stats_ready.sem, 1)
            dve.wait_ge(stats_ready.sem, stats_ready.after(L, j, b))
            dve.sem_inc(passed.sem, 1)
            for t in range(NT):
                last = dve.bn_aggr(mv[:, t, :], stats[:, t, :])
            last.then_inc(mv_ready.sem, 1)

        def ln_rstd_pool(pool, L, b, j=0, mv=mv, ve=ve, rstd=rstd):
            eps = eps12 if (L == "L3f" and j == 1) else eps5
            pool.wait_ge(mv_ready.sem, mv_ready.after(L, j, b))
            pool.tensor_tensor(ve[:, :], mv[:, :, 1], eps[:, :], ALU.add).then_inc(ve_ready.sem, 1)
            pool.wait_ge(ve_ready.sem, ve_ready.after(L, j, b))
            pool.tensor_tensor(rstd[:, :], ve[:, :], minus_half[:, :], ALU.pow).then_inc(rstd_ready.sem, 1)

        def ln_apply_dve(dve, L, b, j=0, mv=mv, rstd=rstd):
            dve.wait_ge(rstd_ready.sem, rstd_ready.after(L, j, b))
            if j == 0:
                wait_xn_free(dve, L, b)
            src = (lambda t: x[:, b * NT + t, :]) if j == 0 else (lambda t: xn[:, t, :])
            dst, ev = (xn, xn_ready) if j == 0 else (z, z_ready)
            for t in range(NT):
                last = dve.tensor_scalar(dst[:, t, :], src(t), mv[:, t, 0:1], rstd[:, t:t + 1],
                                         ALU.subtract, ALU.mult)
            last.then_inc(ev.sem, 1)

        def wait_xn_free(dve, L, b):
            xt = XT_UNIT[L]
            if isinstance(b, int) and b == 0:
                i = LAYERS.index(L)
                if i:
                    q = LAYERS[i - 1]
                    X.wait_full(dve, q, XT_UNIT[q], NB - 1)
            else:
                X.wait_full(dve, L, xt, b - 1)

        XT_UNIT = {L: 0 for L in LAYERS}

        def front_dve(dve, L, b):
            for j in range(2 if L in INNER else 1):
                ln_stats_dve(dve, L, b, j)
                ln_apply_dve(dve, L, b, j)

        def front_pool(pool, L, b):
            for j in range(2 if L in INNER else 1):
                ln_rstd_pool(pool, L, b, j)

        def early_norm(eng, name, L):
            i = LAYERS.index(L) + 1
            if name not in ("dve", "pool"):
                return
            if LAYERS[i] != "L3f":
                (front_dve if name == "dve" else front_pool)(eng, LAYERS[i], 0)

        def front_pe(pe, L, b):
            pe.wait_ge(xn_ready.sem, xn_ready.after(L, 0, b))
            X.wait_empty(pe, L, XT_UNIT[L], b)
            for t in range(NT):
                last = pe.transpose(X.t[:, t * P:(t + 1) * P], xn[:, t, :], ident[:, :])
            last.then_inc(X.full.sem, 1)

        def front_act(act, L, b, free=None):
            X.wait_full(act, L, XT_UNIT[L], b)
            if free is not None:
                free(act)
            act.activation(xnT[:, :], X.t[:, :], ACT.Copy).then_inc(X.drained.sem, 1)

        def scores_pe(pe, L, b, t, banks=(0, 1, 2)):
            c = ATT[L]
            if t == 0 and 0 in banks:
                X.wait_drained(pe, L, 0, b)
            lhs = xnT[:, t * P:(t + 1) * P]
            for j in banks:
                h0, h1 = BANK_HEADS[j]
                n = (h1 - h0) * CK
                S[j].wait_empty(pe, L, t, b)
                o = S[j].t[:, 0:n]
                if c["mask"] is not None:
                    pe.matmul(o, identb[:, :], spread(c["mask"][:, b * NT + t, :], 1, h1 - h0),
                              start=True, stop=False)
                pe.matmul(o, lhs, c["G"][:, b, h0:h1, :], start=c["mask"] is None, stop=True)\
                    .then_inc(S[j].full.sem, 1)

        def shift_dve(dve, L, b, t):
            c = ATT[L]
            k = 3 if c["bias"] else 1
            m = mx[:, t % 2, :]
            parts = [(S[j], h0, h1) for j, (h0, h1) in enumerate(BANK_HEADS)]
            for bk, h0, h1 in parts:
                bk.wait_full(dve, L, t, b)
                last = dve.tensor_reduce(m[:, h0:h1], bk.t[:, 0:(h1 - h0) * CK].rearrange("p (h k) -> p h k", k=CK),
                                         AX.X, ALU.max)
            last.then_inc(max_ready.sem, 1)
            dve.wait_ge(max_ready.sem, max_ready.after(L, k * t, 0) + b * (k * NT))
            if c["bias"]:
                dve.tensor_tensor(m, m, head_bias[:, :], ALU.add).then_inc(max_ready.sem, 1)
                dve.wait_ge(max_ready.sem, max_ready.after(L, k * t + 1, 0) + b * (k * NT))
                dve.tensor_tensor(m, m, head_bias[:, :], ALU.subtract).then_inc(max_ready.sem, 1)
                dve.wait_ge(max_ready.sem, max_ready.after(L, k * t + 2, 0) + b * (k * NT))
            for bk, h0, h1 in parts:
                dve.tensor_tensor(prob[:, t, h0 * CK:h1 * CK].rearrange("p (h k) -> p h k", k=CK),
                                  bk.t[:, 0:(h1 - h0) * CK].rearrange("p (h k) -> p h k", k=CK),
                                  spread(m[:, h0:h1], 2, CK), ALU.subtract).then_inc(bk.drained.sem, 1)

        def exp_act(act, L, b, t):
            c = ATT[L]
            S[2].wait_drained(act, L, t, b)
            act.activation(prob[:, t, :], prob[:, t, :], ACT.Exp, scale=c["scale"]).then_inc(exp_ready.sem, 1)

        def normalise_dve(dve, L, b, t):
            dve.wait_ge(exp_ready.sem, exp_ready.after(L, t, b))
            r = rden[:, t % 2, :]
            dve.tensor_reduce(r, prob[:, t, :].rearrange("p (h k) -> p h k", k=CK), AX.X, ALU.add)\
                .then_inc(den_ready.sem, 1)
            dve.wait_ge(den_ready.sem, den_ready.after(L, 2 * t, 0) + b * (2 * NT))
            dve.reciprocal(r, r).then_inc(den_ready.sem, 1)

        def normalise_pool(pool, L, b, t):
            pool.wait_ge(den_ready.sem, den_ready.after(L, 2 * t + 1, 0) + b * (2 * NT))
            v = prob[:, t, :].rearrange("p (h k) -> p h k", k=CK)
            pool.tensor_tensor(v, v, spread(rden[:, t % 2, :], 2, CK), ALU.mult).then_inc(scaled_ready.sem, 1)

        def t_units(L, t):
            return [(TB[0], 2 * t, 0, 4), (TB[1], t, 4, 8), (TB[0], 2 * t + 1, 8, 10)]

        def transposes_pe(pe, L, b, t, units):
            c = ATT[L]
            chunks = CHUNKS16
            if 0 not in units:
                pass
            elif c["fold"]:
                pe.wait_ge(scaled_ready.sem, scaled_ready.after(L, t, b))
            else:
                pe.wait_ge(exp_ready.sem, exp_ready.after(L, t, b))
            for k in units:
                bk, u, c0, c1 = t_units(L, t)[k]
                bk.wait_empty(pe, L, u, b)
                for i in range(c0, c1):
                    s, n = chunks[i]
                    last = pe.transpose(bk.t[0:n, (i - c0) * P:(i - c0 + 1) * P], prob[:, t, s:s + n], ident[:, :])
                last.then_inc(bk.full.sem, 1)

        def mix_pe(pe, L, b, t):
            c = ATT[L]
            chunks = CHUNKS16
            first = True
            if c["fold"]:
                dst, u = (O, Y)[t % 2], t // 2
                dst.wait_empty(pe, L, u, b)
                pe.matmul(dst.t[:, 0:P], ones[0:1, :], rows[0:1, c["row"], :], start=True, stop=False)
                for bk, tu, c0, c1 in t_units(L, t):
                    bk.wait_drained(pe, L, tu, b)
                    for i in range(c0, c1):
                        n = chunks[i][1]
                        last = pe.matmul(dst.t[:, 0:P], probT[0:n, i * P:(i + 1) * P], c["V"][0:n, b, i, :],
                                         start=False, stop=i == len(chunks) - 1)
                last.then_inc(dst.full.sem, 1)
            else:
                w = c["dv"] + 1
                O.wait_empty(pe, L, t, b)
                for bk, tu, c0, c1 in t_units(L, t):
                    bk.wait_drained(pe, L, tu, b)
                    for i in range(c0, c1):
                        n = chunks[i][1]
                        h0 = CHUNK_HEAD[i]
                        last = pe.matmul(O.t[:, h0 * w:(h0 + 3) * w], probT[0:n, i * P:(i + 1) * P],
                                         c["V"][0:n, b, i, :, :],
                                         start=first, stop=i == len(chunks) - 1, skip_group_check=True)
                        first = False
                last.then_inc(O.full.sem, 1)

        def probT_act(act, L, b, t, units=(0,)):
            c = ATT[L]
            for k in units:
                bk, u, c0, c1 = t_units(L, t)[k]
                bk.wait_full(act, L, u, b)
                if c1 == 10:
                    r = CHUNKS16[9][1]
                    act.activation(probT[:, c0 * P:(c0 + 1) * P], bk.t[:, 0:P], ACT.Copy)
                    act.activation(probT[0:r, (c0 + 1) * P:c1 * P], bk.t[0:r, P:2 * P], ACT.Copy)\
                        .then_inc(bk.drained.sem, 1)
                else:
                    act.activation(probT[:, c0 * P:c1 * P], bk.t[:, 0:(c1 - c0) * P], ACT.Copy)\
                        .then_inc(bk.drained.sem, 1)

        def mixed_dve(dve, L, b, t):
            c = ATT[L]
            if c["fold"]:
                bk, u = (O, Y)[t % 2], t // 2
                bk.wait_full(dve, L, u, b)
                ins = dve.tensor_tensor(x[:, b * NT + t, :], x[:, b * NT + t, :], bk.t[:, 0:P], ALU.add)
                ins.then_inc(bk.drained.sem, 1)
                return
            H, dv = c["H"], c["dv"]
            O.wait_full(dve, L, t, b)
            v = O.t[:, 0:H * (dv + 1)].rearrange("p (h e) -> p h e", e=dv + 1)
            r = rden[:, t % 2, 0:H]
            dve.reciprocal(r, v[:, :, dv]).then_inc(den_ready.sem, 1)
            dve.wait_ge(den_ready.sem, den_ready.after(L, t, 0) + b * NT)
            dve.tensor_tensor(mix[:, t, :].rearrange("p (h e) -> p h e", e=dv), v[:, :, 0:dv],
                              spread(r, 2, dv), ALU.mult).then_inc(O.drained.sem, 1)

        def tail_transposes_pe(pe, L, b, done=NT - 1):
            O.wait_drained(pe, L, done, b)
            for t in range(NT):
                last = pe.transpose(O.t[:, t * P:(t + 1) * P], mix[:, t, :], ident[:, :])
            last.then_inc(O.full.sem, 1)

        def projection_unit(L, b):
            if L != "L3x":
                return L, 0, b
            return ("L3x", 0, 0) if isinstance(b, int) and b == 0 else ("L3x with norm", 2, b - 1)

        def tail_bias_pe(pe, L, b):
            c = ATT[L]
            Y.wait_empty(pe, *projection_unit(L, b))
            if c["row"] is not None:
                pe.matmul(Y.t[:, :], ones[0:1, :], spread(rows[0:1, c["row"], :], 1, NT), start=True, stop=False,
                          skip_group_check=True)

        def tail_project_pe(pe, L, b, unit=NT):
            c = ATT[L]
            O.wait_drained(pe, L, unit, b)
            for t in range(NT):
                last = pe.matmul(Y.t[:, t * P:(t + 1) * P], mixT[:, t * P:(t + 1) * P], c["wout"],
                                 start=c["row"] is None and t == 0, stop=t == NT - 1, skip_group_check=True)
            last.then_inc(Y.full.sem, 1)

        def tail_act(act, L, b, unit=NT):
            O.wait_full(act, L, unit, b)
            act.activation(mixT[:, :], O.t[:, :], ACT.Copy).then_inc(O.drained.sem, 1)

        def tail_dve(dve, L, b):
            if ATT[L]["fold"]:
                dve.wait_ge(Y.drained.sem, Y.drained.after(L, 1, b))
                dve.wait_ge(O.drained.sem, O.drained.after(L, 1, b))
                dve.sem_inc(x_done.sem, 1)
                return
            Y.wait_full(dve, *projection_unit(L, b))
            xb = x[:, bass.ds(b * NT, NT), :] if not isinstance(b, int) else x[:, b * NT:(b + 1) * NT, :]
            dve.tensor_tensor(xb, xb, Y.t[:, :].rearrange("p (t d) -> p t d", t=NT), ALU.add)\
                .then_inc(Y.drained.sem, 1)
            Y.wait_drained(dve, *projection_unit(L, b))
            dve.sem_inc(x_done.sem, 1)

        def attention_step(eng, name, L, b, t, before=None, ahead=None, front=None, stats=None, tail=None,
                           ffn=None):
            fold = ATT[L]["fold"]
            if name == "pe":
                transposes_pe(eng, L, b, t, (0, 1))
                if front is not None:
                    front_pe(eng, L, front)
                if ahead is not None:
                    scores_pe(eng, L, *ahead, (0,))
                if tail is not None:
                    tail_transposes_pe(eng, L, tail)
                if ffn is not None and t == 0:
                    ffn3_transposes_pe(eng, ffn)
                if ahead is not None:
                    scores_pe(eng, L, *ahead, (1, 2))
                transposes_pe(eng, L, b, t, (2,))
                if ffn is not None and t == 0:
                    ffn3_logits_pe(eng, ffn)
                if tail is not None:
                    tail_bias_pe(eng, L, tail)
                    tail_project_pe(eng, L, tail)
                mix_pe(eng, L, b, t)
            elif name == "act":
                probT_act(eng, L, b, t, (0, 1))
                if front is not None:
                    front_act(eng, L, front)
                if tail is not None:
                    tail_act(eng, L, tail)
                if ffn is not None and t == 0:
                    ffn3_keep_act(eng, ffn)
                probT_act(eng, L, b, t, (2,))
                if ahead is not None:
                    exp_act(eng, L, *ahead)
            elif name == "dve":
                if before is not None:
                    mixed_dve(eng, L, *before)
                    if fold and before[1] == NT - 1:
                        tail_dve(eng, L, before[0])
                if ffn is not None and t == 2:
                    ffn3_xn(eng, ffn)
                if ffn is not None and t == 3:
                    ffn3_stats(eng, ffn, 1)
                if stats is not None:
                    ln_stats_dve(eng, L, stats)
                if fold:
                    if t < NT - 1:
                        normalise_dve(eng, L, b, t + 1)
                    elif ahead is not None:
                        normalise_dve(eng, L, b + 1, 0)
                if ahead is not None:
                    shift_dve(eng, L, *ahead)
                if stats is not None:
                    ln_apply_dve(eng, L, stats)
                if ffn is not None and t == 0:
                    ffn3_logits_dve(eng, ffn)
                if tail is not None and not fold:
                    tail_dve(eng, L, tail)
                if L == "L3x" and tail is not None:
                    ffn3_stats(eng, tail, 0)
                if ffn is not None and t == 2:
                    ffn3_base(eng, ffn)
                if ffn is not None and t == 3:
                    ffn3_z(eng, ffn)
            elif name == "pool":
                if ffn is not None and t == 1:
                    ffn3_rstd(eng, ffn, 0)
                if stats is not None:
                    ln_rstd_pool(eng, L, stats)
                if ffn is not None and t == 3:
                    ffn3_rstd(eng, ffn, 1)
                if ffn is not None and t == 0:
                    ffn3_normed(eng, ffn)
                if fold:
                    if t < NT - 1:
                        normalise_pool(eng, L, b, t + 1)
                    elif ahead is not None:
                        normalise_pool(eng, L, b + 1, 0)

        def prepared_pe(pe, L):
            for bk in BANKS:
                if "prep" + L in bk.drained.base:
                    bk.wait_drained(pe, "prep" + L, bk.drained.base["prep" + L][1] - 1)

        def run_attention16(eng, name, L):
            fold = ATT[L]["fold"]
            head = {"pe": scores_pe, "dve": shift_dve, "act": exp_act}.get(name)
            if name in ("pe", "act") or (name == "pool" and L == LAYERS[0]):
                fronts(eng, name, L, 0)
            for t in range(2):
                if head and name == "act" and L == "L1x":
                    turned_values_act(eng, t)
                if head:
                    head(eng, L, 0, t)
                if name == "pe" and L == "L1x":
                    turned_values_pe(eng, t)
            if fold and name in ("dve", "pool"):
                (normalise_dve if name == "dve" else normalise_pool)(eng, L, 0, 0)
            if L == "L1x" and name != "pool":
                {"pe": folded_values_pe, "act": folded_values_act, "dve": folded_values_dve}[name](eng)
            if L == "L3x" and name in ("pe", "act"):
                for part in range(5, PREP03_PARTS):
                    {"pe": prep03_pe, "act": prep03_act}[name](eng, L, part)
            if L != "L0x" and name == "pe":
                prepared_pe(eng, L)
            attention_step(eng, name, L, 0, 0, ahead=(0, 2))

            def batch(b, ffn=None):
                attention_step(eng, name, L, b, 1, before=(b, 0), ahead=(b, 3), stats=b + 1, ffn=ffn)
                attention_step(eng, name, L, b, 2, before=(b, 1), ahead=(b + 1, 0), front=b + 1, ffn=ffn)
                attention_step(eng, name, L, b, 3, before=(b, 2), ahead=(b + 1, 1), ffn=ffn)
                attention_step(eng, name, L, b + 1, 0, before=(b, 3), ahead=(b + 1, 2),
                               tail=None if fold else b, ffn=ffn)

            with_ffn = L == "L3x"
            if with_ffn:
                eng.wait_ge(loaded["small3"].sem, LOADS["small3"])
                batch(0)
                with eng.Fori(1, NB - 1) as b:
                    batch(b, ffn=b - 1)
            else:
                with eng.Fori(0, NB - 1) as b:
                    batch(b)
            b = NB - 1
            ffn = b - 1 if with_ffn else None
            attention_step(eng, name, L, b, 1, before=(b, 0), ahead=(b, 3), ffn=ffn)
            attention_step(eng, name, L, b, 2, before=(b, 1), ffn=ffn)
            if name == "pool" and L == "L0x":
                ternary_pool(eng)
            early_norm(eng, name, L)
            attention_step(eng, name, L, b, 3, before=(b, 2), ffn=ffn)
            with_ffn0 = L == "L0x"
            if name == "dve":
                mixed_dve(eng, L, b, 3)
                if with_ffn:
                    ffn3_logits_dve(eng, ffn)
                tail_dve(eng, L, b)
                if with_ffn0:
                    prep_ffn0_dve(eng)
            elif not fold and name == "pe":
                tail_transposes_pe(eng, L, b)
                if with_ffn:
                    ffn3_transposes_pe(eng, ffn)
                    ffn3_logits_pe(eng, ffn)
                tail_bias_pe(eng, L, b)
                tail_project_pe(eng, L, b)
                if with_ffn0:
                    prep_ffn0_pe(eng)
                    prep_ffn0_first_pe(eng)
                    prep_ffn0_second_pe(eng)
            elif not fold and name == "act":
                tail_act(eng, L, b)
                if with_ffn0:
                    prep_ffn0_act(eng)
                    prep_ffn0_weights_act(eng)
                if with_ffn:
                    ffn3_keep_act(eng, ffn)
            elif with_ffn:
                ffn3_normed(eng, ffn)

        PAIR_OUT = (O, S[2])

        def pair_scores_pe(pe, b, i):
            L = "L2x"
            if i == 0:
                X.wait_drained(pe, L, 0, b)
            bk = S[i]
            bk.wait_empty(pe, L, 0, b)
            for u in range(2):
                t = 2 * i + u
                o = bk.t[:, u * 2 * CK:(u + 1) * 2 * CK]
                if t == 0:
                    pe.matmul(o, ident[:, :], spread(causal[:, :], 1, 2), start=True, stop=False)
                last = pe.matmul(o, xnT[:, t * P:(t + 1) * P], G2[:, b, :, :], start=t != 0, stop=True)
            last.then_inc(bk.full.sem, 1)

        def pair_shift_dve(dve, b, i):
            L = "L2x"
            S[i].wait_full(dve, L, 0, b)
            v = S[i].t[:, 0:4 * CK].rearrange("p (q k) -> p q k", k=CK)
            m = mx[:, i, 0:4]
            dve.tensor_reduce(m, v, AX.X, ALU.max).then_inc(max_ready.sem, 1)
            dve.wait_ge(max_ready.sem, max_ready.after(L, i, b))
            dve.tensor_tensor(prob[:, i, 0:4 * CK].rearrange("p (q k) -> p q k", k=CK), v, spread(m, 2, CK),
                              ALU.subtract).then_inc(S[i].drained.sem, 1)

        def pair_exp_act(act, b, i):
            S[i].wait_drained(act, "L2x", 0, b)
            act.activation(prob[:, i, 0:4 * CK], prob[:, i, 0:4 * CK], ACT.Exp, scale=ATT["L2x"]["scale"])\
                .then_inc(exp_ready.sem, 1)

        def pair_transposes_pe(pe, b, i):
            L = "L2x"
            pe.wait_ge(exp_ready.sem, exp_ready.after(L, i, b))
            TB[i].wait_empty(pe, L, 0, b)
            for q in range(4):
                last = pe.transpose(TB[i].t[0:CK, q * P:(q + 1) * P], prob[:, i, q * CK:(q + 1) * CK], ident[:, :])
            last.then_inc(TB[i].full.sem, 1)

        def pair_probT_act(act, b, i):
            TB[i].wait_full(act, "L2x", 0, b)
            act.activation(probT[0:CK, i * 512:(i + 1) * 512], TB[i].t[0:CK, :], ACT.Copy)\
                .then_inc(TB[i].drained.sem, 1)

        def pair_mix_pe(pe, b, i):
            L = "L2x"
            bk = PAIR_OUT[i]
            TB[i].wait_drained(pe, L, 0, b)
            bk.wait_empty(pe, L, 0, b)
            for q in range(4):
                last = pe.matmul(bk.t[:, q * 65:(q + 1) * 65], probT[0:CK, (4 * i + q) * P:(4 * i + q + 1) * P],
                                 V2[0:CK, b, q % 2, :], start=True, stop=True)
            last.then_inc(bk.full.sem, 1)

        def pair_mixed_dve(dve, b, i):
            L = "L2x"
            bk = PAIR_OUT[i]
            bk.wait_full(dve, L, 0, b)
            v = bk.t[:, 0:260].rearrange("p (q e) -> p q e", e=65)
            r = rden[:, i, 0:4]
            dve.reciprocal(r, v[:, :, 64]).then_inc(den_ready.sem, 1)
            dve.wait_ge(den_ready.sem, den_ready.after(L, i, b))
            dve.tensor_tensor(mix[:, 2 * i:2 * i + 2, :].rearrange("p t (h e) -> p (t h) e", e=64), v[:, :, 0:64],
                              spread(r, 2, 64), ALU.mult).then_inc(bk.drained.sem, 1)

        def run_attention2(eng, name):
            L = "L2x"

            def scores(b):
                for i in range(2):
                    if name == "pe":
                        pair_scores_pe(eng, b, i)
                    elif name == "dve":
                        pair_shift_dve(eng, b, i)
                    elif name == "act":
                        pair_exp_act(eng, b, i)

            def step(b, nxt=True, norm=True):
                if name == "pe":
                    for i in range(2):
                        pair_transposes_pe(eng, b, i)
                    if nxt:
                        scores(b + 1)
                    for i in range(2):
                        pair_mix_pe(eng, b, i)
                    tail_bias_pe(eng, L, b)
                    S[2].wait_drained(eng, L, 0, b)
                    tail_transposes_pe(eng, L, b, 0)
                    if norm:
                        front_pe(eng, L, b + 2)
                    tail_project_pe(eng, L, b, 1)
                elif name == "act":
                    for i in range(2):
                        pair_probT_act(eng, b, i)
                    if nxt:
                        scores(b + 1)
                    tail_act(eng, L, b, 1)
                    if norm:
                        front_act(eng, L, b + 2)
                elif name == "dve":
                    if nxt:
                        scores(b + 1)
                    if norm:
                        ln_stats_dve(eng, L, b + 2)
                    if not nxt:
                        ln_apply_dve(eng, "L2f", 0)
                        ln_stats_dve(eng, "L2f", 0, 1)
                    for i in range(2):
                        pair_mixed_dve(eng, b, i)
                    if norm:
                        ln_apply_dve(eng, L, b + 2)
                    elif nxt:
                        ln_stats_dve(eng, "L2f", 0)
                    else:
                        ln_apply_dve(eng, "L2f", 0, 1)
                    tail_dve(eng, L, b)
                elif norm:
                    front_pool(eng, L, b + 2)
                elif not nxt:
                    front_pool(eng, "L2f", 0)

            if name in ("pe", "act"):
                fronts(eng, name, L, 0)
            if name == "pool":
                front_pool(eng, L, 1)
            if name == "dve":
                ln_stats_dve(eng, L, 1)
            scores(0)
            if name == "dve":
                ln_apply_dve(eng, L, 1)
            if name in ("pe", "act"):
                fronts(eng, name, L, 1)
            with eng.Fori(0, NB - 2) as b:
                step(b)
            step(NB - 2, norm=False)
            step(NB - 1, nxt=False, norm=False)

        PREP03_PARTS = 8
        values = probT[0:CK, 0:NB * P].rearrange("p (b d) -> p b d", b=NB)

        G_BANKS = {"L0x": [(S[0], 0), (S[1], 0), (S[2], 0)], "L3x": [(O, 0), (Y, 0), (TB[1], 0)]}

        KEYS_BY_HEAD = {"L0x": prob, "L3x": GB[:, :, :, :].rearrange("p b h k -> p b (h k)")}

        def plan_prep03(L):
            X.plan("prep" + L, 2)
            if L == "L0x":
                O.plan("prep" + L, 1)
                Y.plan("prep" + L, 1)
            else:
                S[2].plan("prep" + L, 1)
            for bk, u in G_BANKS[L]:
                bk.plan("prep" + L, NB)
            TB[0].plan("prep" + L, 2)
            dve_prep.plan("prep" + L, NB)

        KEY_BANK = {"L0x": Y, "L3x": S[2]}

        def keys_pe(pe, L):
            ph_ = "prep" + L
            wk = w0[:, 1, :] if L == "L0x" else wT[:, 1, :]
            bk = KEY_BANK[L]
            bk.wait_empty(pe, ph_, 0)
            X.wait_drained(pe, ph_, 0)
            pe.matmul(bk.t[:, 0:NB * CK], wk, keysT, start=True, stop=True).then_inc(bk.full.sem, 1)

        def keys_dve(dve, L, b):
            ph_ = "prep" + L
            bk = KEY_BANK[L]
            bk.wait_full(dve, ph_, 0)
            dve.tensor_tensor(KEYS_BY_HEAD[L][:, b, :].rearrange("p (h k) -> p h k", k=CK),
                              spread(bk.t[:, b * CK:(b + 1) * CK], 1, H16), spread(blk[:, :], 2, CK), ALU.mult)\
                .then_inc(dve_prep.sem, 1)
            if b == NB - 1:
                dve.wait_ge(dve_prep.sem, dve_prep.after(ph_, NB - 1))
                dve.sem_inc(bk.drained.sem, 1)

        def prep03_pe(pe, L, part):
            ph_ = "prep" + L
            first = L == "L0x"
            wq, wv = (wT[:, 0, :], w0[:, 2, :]) if first else (w3[:, 0, :], wT[:, 2, :])
            if part == 0:
                X.wait_empty(pe, ph_, 0)
                if first:
                    pe.wait_ge(made.sem, MADE)
                    pe.wait_ge(loaded["ctx"].sem, 16)
                    for b in range(NB):
                        last = pe.transpose(X.t[:, b * CK:(b + 1) * CK], ctx_tok[:, b, :], ident[0:CK, 0:CK])
                else:
                    pe.wait_ge(loaded["attn3"].sem, LOADS["attn3"])
                    for i in range(3):
                        last = pe.transpose(X.t[:, i * P:(i + 1) * P], w3[:, 1 + i, :], ident[:, :])
                last.then_inc(X.full.sem, 1)
                if first:
                    pe.wait_ge(loaded["w0"].sem, LOADS["w0"])
                    O.wait_empty(pe, ph_, 0)
                    pe.transpose(O.t[:, 0:P], w0[:, 0, :], ident[:, :]).then_inc(O.full.sem, 1)
            elif part == 1:
                if first:
                    keys_pe(pe, L)
                TB[0].wait_empty(pe, ph_, 0)
                for b in range(NB):
                    last = pe.matmul(TB[0].t[0:CK, b * P:(b + 1) * P], keysT[:, b, :], wv, start=True, stop=True)
                last.then_inc(TB[0].full.sem, 1)
            elif part in (2, 3):
                bk, u = (TB[0], 1) if part == 2 else (X, 1)
                TB[0].wait_drained(pe, ph_, 0)
                bk.wait_empty(pe, ph_, u)
                if part == 2:
                    pe.wait_ge(rep_made.sem, 1)
                for i in range(5):
                    c = 5 * (part - 2) + i
                    k0, h0 = CHUNKS16[c][0] % CK, CHUNK_HEAD[c]
                    last = pe.matmul(bk.t[:, i * 96:(i + 1) * 96], key_of_row[0:CK, k0:k0 + P],
                                     values[:, :, h0 * 8:(h0 + 3) * 8], start=True, stop=True)
                last.then_inc(bk.full.sem, 1)
            else:
                b = part - 4
                if b == 0 and first:
                    O.wait_drained(pe, ph_, 0)
                pe.wait_ge(dve_prep.sem, dve_prep.after(ph_, b))
                for (bk, u), (h0, h1) in zip(G_BANKS[L], BANK_HEADS):
                    bk.wait_empty(pe, ph_, u + b)
                    pe.matmul(bk.t[:, 0:(h1 - h0) * CK], wq, KEYS_BY_HEAD[L][:, b, h0 * CK:h1 * CK], start=True, stop=True)\
                        .then_inc(bk.full.sem, 1)

        def prep03_act(act, L, part):
            ph_ = "prep" + L
            if part == 0:
                if L == "L0x":
                    act.wait_ge(made.sem, MADE)
                    X.wait_full(act, ph_, 0)
                    act.activation(keysT, X.t[:, 0:NB * CK].rearrange("p (b k) -> p b k", b=NB), ACT.Copy)\
                        .then_inc(X.drained.sem, 1)
                    O.wait_full(act, ph_, 0)
                    act.activation(wT[:, 0, :], O.t[:, 0:P], ACT.Copy).then_inc(O.drained.sem, 1)
                else:
                    X.wait_full(act, ph_, 0)
                    act.activation(wT[:, 1:3, :], X.t[:, 0:2 * P].rearrange("p (i d) -> p i d", i=2), ACT.Copy)
                    act.activation(out_wT[:, 1, :], X.t[:, 2 * P:3 * P], ACT.Copy).then_inc(X.drained.sem, 1)
            elif part == 1:
                TB[0].wait_full(act, ph_, 0)
                act.activation(values, TB[0].t[0:CK, :].rearrange("p (b d) -> p b d", b=NB), ACT.Copy)\
                    .then_inc(TB[0].drained.sem, 1)
            elif part >= 4:
                b = part - 4
                for (bk, u), (h0, h1) in zip(G_BANKS[L], BANK_HEADS):
                    bk.wait_full(act, ph_, u + b)
                    act.activation(GA[:, b, h0:h1, :], bk.t[:, 0:(h1 - h0) * CK].rearrange("p (h k) -> p h k", k=CK),
                                   ACT.Copy).then_inc(bk.drained.sem, 1)

        def prep03_dve(dve, L, part):
            ph_ = "prep" + L
            if L == "L0x" and 1 <= part <= NB:
                keys_dve(dve, L, part - 1)
            if part in (3, 4):
                bk, c0 = (TB[0], 0) if part == 3 else (X, 5)
                dve.wait_ge(grid_made.sem, 1)
                bk.wait_full(dve, ph_, 1)
                v = bk.t[:, 0:480].rearrange("p (c b m e) -> p c b m e", c=5, b=NB, m=3)
                for b in range(NB):
                    last = dve.tensor_tensor(V03[:, b, c0:c0 + 5, :, 0:8], v[:, :, b, :, :],
                                             spread(grid[:, c0:c0 + 5, :], 3, 8), ALU.mult)
                last.then_inc(bk.drained.sem, 1)

        def plan_prep1():
            L = "prepL1x"
            for bk in (S[1], S[2], TB[0]):
                bk.plan(L, 2)
            S[0].plan(L, 2)
            X.plan(L, 1 + 4)
            Y.plan(L, 1 + 4 + 5 + NB)
            TB[1].plan(L, 4 + 6 + NB)
            O.plan(L, 4 + 5 + NB)

        def head_bank(h):
            bk = (TB[1], O, X, Y)[h % 4]
            return bk, h // 4 + (1 if bk in (X, Y) else 0)

        def pair_banks(p):
            return (S[0], S[2]) if p < 4 else (S[1], TB[0])

        def prep1_pe(pe):
            L = "prepL1x"
            pe.wait_ge(loaded["attn1"].sem, LOADS["attn1"])

            def pairs(lhs, rhs, unit):
                for p in range(8):
                    for par, bk in enumerate(pair_banks(p)):
                        if p % 4 == 0:
                            bk.wait_empty(pe, L, unit)
                        r = slice(64 * par, 64 * par + 64)
                        last = pe.matmul(bk.t[:, (p % 4) * P:(p % 4 + 1) * P], lhs[r, p, :], rhs[r, p, :],
                                         start=True, stop=True)
                        if p % 4 == 3:
                            last.then_inc(bk.full.sem, 1)

            pairs(w1k, w1q, 0)
            for i, bk in enumerate((X, Y)):
                bk.wait_empty(pe, L, 0)
                for c in range(4):
                    last = pe.transpose(bk.t[:, c * P:(c + 1) * P], w1o[:, (4 * i + c) * P:(4 * i + c + 1) * P],
                                        ident[:, :])
                last.then_inc(bk.full.sem, 1)
            for bk in (S[0], S[1], S[2], TB[0]):
                bk.wait_drained(pe, L, 0)
            for h in range(H16):
                bk, u = head_bank(h)
                bk.wait_empty(pe, L, u)
                pe.matmul(bk.t[:, 0:NB * CK], head_mat[:, h % 2, h // 2, :], keysT, start=True, stop=True)\
                    .then_inc(bk.full.sem, 1)
            X.wait_drained(pe, L, 0)
            Y.wait_drained(pe, L, 0)
            pairs(w1v, w1oT, 1)

        def turned_bank(h):
            bk = (TB[1], O, Y)[h % 3]
            return bk, h // 3 + (5 if bk is Y else 4)

        turned = GA
        TURNED_HALVES = (range(0, H16 // 2), range(H16 // 2, H16))

        def turned_values_pe(pe, half):
            L = "prepL1x"
            for bk in (S[0], S[1], S[2], TB[0]):
                bk.wait_drained(pe, L, 1)
            for h in TURNED_HALVES[half]:
                bk, u = turned_bank(h)
                bk.wait_empty(pe, L, u)
                pe.matmul(bk.t[:, 0:NB * CK], head_mat[:, h % 2, h // 2, :], keysT, start=True, stop=True)\
                    .then_inc(bk.full.sem, 1)

        def turned_values_act(act, half):
            L = "prepL1x"
            for h in TURNED_HALVES[half]:
                bk, u = turned_bank(h)
                bk.wait_full(act, L, u)
                act.activation(turned[:, :, h, :], bk.t[:, 0:NB * CK].rearrange("p (b k) -> p b k", b=NB), ACT.Copy)\
                    .then_inc(bk.drained.sem, 1)

        FOLDED_BANKS = ((O, 9, 0, 4), (Y, 10, 4, 8), (TB[1], 10, 8, 10))

        def folded_values_pe(pe):
            L = "prepL1x"
            for h in range(H16 - 3, H16):
                bk, u = turned_bank(h)
                bk.wait_drained(pe, L, u)
            for b in range(NB):
                rows_of_b = turned[:, b, :, :].rearrange("p h k -> p (h k)")
                for bk, u, c0, c1 in FOLDED_BANKS:
                    bk.wait_empty(pe, L, u + b)
                    for c in range(c0, c1):
                        r, n = CHUNKS16[c]
                        last = pe.transpose(bk.t[0:n, (c - c0) * P:(c - c0 + 1) * P], rows_of_b[:, r:r + n],
                                            ident[:, :])
                    last.then_inc(bk.full.sem, 1)

        def prep1_act(act):
            L = "prepL1x"

            def halves(unit):
                for i in range(2):
                    S[i].wait_full(act, L, unit)
                    act.activation(head_mat[:, 0, 4 * i:4 * i + 4, :], S[i].t[:, :].rearrange("p (c d) -> p c d", c=4),
                                   ACT.Copy).then_inc(S[i].drained.sem, 1)

            halves(0)
            for i, bk in enumerate((X, Y)):
                bk.wait_full(act, L, 0)
                act.activation(w1oT[:, 4 * i:4 * i + 4, :], bk.t[:, :].rearrange("p (c d) -> p c d", c=4), ACT.Copy)\
                    .then_inc(bk.drained.sem, 1)
            for h in range(1, H16, 2):
                bk, u = head_bank(h)
                bk.wait_full(act, L, u)
                act.activation(GB[:, :, h, :], bk.t[:, 0:NB * CK].rearrange("p (b k) -> p b k", b=NB), ACT.Copy)\
                    .then_inc(bk.drained.sem, 1)
            halves(1)

        def folded_values_act(act):
            L = "prepL1x"
            r = CHUNKS16[9][1]
            for b in range(NB):
                O.wait_full(act, L, 9 + b)
                act.activation(V1[:, b, 0:4, :], O.t[:, :].rearrange("p (c d) -> p c d", c=4), ACT.Copy)\
                    .then_inc(O.drained.sem, 1)
                TB[1].wait_full(act, L, 10 + b)
                act.activation(V1[:, b, 8, :], TB[1].t[:, 0:P], ACT.Copy)
                act.activation(V1[0:r, b, 9, :], TB[1].t[0:r, P:2 * P], ACT.Copy).then_inc(TB[1].drained.sem, 1)

        def prep1_dve(dve):
            L = "prepL1x"
            dve.wait_ge(loaded["mask1"].sem, LOADS["mask1"])
            dve.tensor_scalar(mask1[:, :, :], mask_raw[:, :, :], 0.0, MASKED, ALU.is_equal, ALU.mult)\
                .then_inc(mask_made.sem, 1)
            dve.tensor_scalar(src_bias[:, :, :], src_raw[:, :, :], 0.0, MASKED, ALU.is_equal, ALU.mult)\
                .then_inc(mask_made.sem, 1)
            dve.wait_ge(mask_made.sem, 2)
            for b in range(NB):
                v = mask1[:, b * NT:(b + 1) * NT, :]
                dve.tensor_tensor(v, v, spread(src_bias[:, b, :], 1, NT), ALU.min).then_inc(mask_made.sem, 1)

            def halves(unit):
                for i, bk in enumerate((S[2], TB[0])):
                    bk.wait_full(dve, L, unit)
                    dve.tensor_copy(head_mat[:, 1, 4 * i:4 * i + 4, :], bk.t[:, :].rearrange("p (c d) -> p c d", c=4))\
                        .then_inc(bk.drained.sem, 1)

            halves(0)
            for h in range(0, H16, 2):
                bk, u = head_bank(h)
                bk.wait_full(dve, L, u)
                dve.tensor_copy(GB[:, :, h, :], bk.t[:, 0:NB * CK].rearrange("p (b k) -> p b k", b=NB))\
                    .then_inc(bk.drained.sem, 1)
            halves(1)

        def folded_values_dve(dve):
            L = "prepL1x"
            for b in range(NB):
                Y.wait_full(dve, L, 10 + b)
                dve.tensor_copy(V1[:, b, 4:8, :], Y.t[:, :].rearrange("p (c d) -> p c d", c=4))\
                    .then_inc(Y.drained.sem, 1)

        def plan_prep2(before_ffn1):
            L = "prepL2x"
            for bk in (Y, S[0], S[1], TB[0]) if before_ffn1 else (O, X):
                bk.plan(L, 1)

        def prep2_pe(pe):
            L = "prepL2x"
            pe.wait_ge(loaded["attn2"].sem, LOADS["attn2"])
            for h, bk in enumerate((Y, O)):
                r = slice(64 * h, 64 * h + 64)
                bk.wait_empty(pe, L)
                pe.matmul(bk.t[:, 0:P], w2[r, 1, :], w2[r, 0, :], start=True, stop=True).then_inc(bk.full.sem, 1)
            X.wait_empty(pe, L)
            for i in range(2):
                last = pe.transpose(X.t[:, i * P:(i + 1) * P], w2[:, 2 + i, :], ident[:, :])
            last.then_inc(X.full.sem, 1)
            for h, (bk, src) in enumerate(((S[0], Y), (S[1], O))):
                src.wait_drained(pe, L)
                bk.wait_empty(pe, L)
                pe.matmul(bk.t[:, 0:NB * CK], a2[:, h, :], keysT, start=True, stop=True).then_inc(bk.full.sem, 1)
            X.wait_drained(pe, L)
            TB[0].wait_empty(pe, L)
            for b in range(NB):
                last = pe.matmul(TB[0].t[0:CK, b * P:(b + 1) * P], keysT[:, b, :], wT[:, 0, :], start=True, stop=True)
            last.then_inc(TB[0].full.sem, 1)

        def prep2_act(act):
            L = "prepL2x"
            for h, bk in enumerate((Y, O)):
                bk.wait_full(act, L)
                act.activation(a2[:, h, :], bk.t[:, 0:P], ACT.Copy).then_inc(bk.drained.sem, 1)
            X.wait_full(act, L)
            act.activation(wT[:, 0, :], X.t[:, 0:P], ACT.Copy)
            act.activation(out_wT[:, 0, :], X.t[:, P:2 * P], ACT.Copy).then_inc(X.drained.sem, 1)
            for h in range(2):
                S[h].wait_full(act, L)
                act.activation(G2[:, :, h, :], S[h].t[:, 0:NB * CK].rearrange("p (b k) -> p b k", b=NB), ACT.Copy)\
                    .then_inc(S[h].drained.sem, 1)
            TB[0].wait_full(act, L)
            for b in range(NB):
                last = act.activation(V2[0:CK, b, :, 0:64],
                                      TB[0].t[0:CK, b * P:(b + 1) * P].rearrange("p (h e) -> p h e", h=2), ACT.Copy)
            last.then_inc(TB[0].drained.sem, 1)

        FC_BANKS = [S[0], S[1], S[2], TB[0]]

        def plan_ffn0():
            for bk in (TB[0], TB[1], X, Y):
                bk.plan("prepL0f", 1)
            L = "L0f"
            plan_norm(L)
            X.plan(L, 1, NB)
            for bk in FC_BANKS:
                bk.plan(L, 1, NB)
            Y.plan(L, 1, NB)
            for e in square_ready:
                e.plan(L, 1, NB)
            x_done.plan(L, 1, NB)

        mean, scale, hi, lo = wsc[:, 0, 0:5], wsc[:, 0, 8:13], wsc[:, 1, 0:5], wsc[:, 1, 8:13]

        def ternary_scales_dve(dve):
            dve.wait_ge(loaded["ffn0"].sem, LOADS["ffn0"])
            n = 0

            def step(ins):
                nonlocal n
                n += 1
                ins.then_inc(tern_scale.sem, 1)
                dve.wait_ge(tern_scale.sem, n)

            dve.tensor_reduce(mean[:, 0:NC], wfc[:, :, :], AX.X, ALU.add, apply_absolute_value=True)
            step(dve.tensor_reduce(mean[:, NC:NC + 1], wpr[:, :], AX.X, ALU.add, apply_absolute_value=True))
            step(dve.tensor_scalar(scale[:, 0:NC], mean[:, 0:NC], 1.0 / P, 1e-5, ALU.mult, ALU.max))
            step(dve.tensor_scalar(scale[:, NC:NC + 1], mean[:, NC:NC + 1], 1.0 / FF, 1e-5, ALU.mult, ALU.max))
            step(dve.tensor_scalar(hi, scale, 0.5, None, ALU.mult))
            step(dve.tensor_scalar(lo, scale, -0.5, None, ALU.mult))
            assert n == TERN_SCALES

        def ternary_pool(pool):
            pool.wait_ge(tern_scale.sem, TERN_SCALES)
            n = 0

            def step(ins):
                nonlocal n
                n += 1
                ins.then_inc(tern.sem, 1)
                pool.wait_ge(tern.sem, n)

            wp = wpr[:, :].rearrange("p (c d) -> p c d", c=NC)
            for w, col in ((wfc, lambda c: c), (wp, lambda c: NC)):
                for c in range(NC):
                    k = col(c)
                    pool.tensor_scalar(wt1[:, c, :], w[:, c, :], hi[:, k:k + 1], None, ALU.is_gt)
                    last = pool.tensor_scalar(wt2[:, c, :], w[:, c, :], lo[:, k:k + 1], None, ALU.is_lt)
                step(last)
                step(pool.tensor_tensor(wt1[:, :, :], wt1[:, :, :], wt2[:, :, :], ALU.subtract))
                step(pool.tensor_tensor(wt1[:, :, :], wt1[:, :, :], w[:, :, :], ALU.subtract))
                step(pool.tensor_tensor(w[:, :, :], w[:, :, :], wt1[:, :, :], ALU.add))
                for c in range(NC):
                    last = pool.tensor_scalar(w[:, c, :], w[:, c, :], scale[:, col(c):col(c) + 1], None, ALU.mult)
                step(last)
            assert n == TERN_STEPS

        def prep_ffn0_dve(dve):
            TB[1].wait_full(dve, "prepL0f")
            dve.tensor_scalar(bv[:, :], TB[1].t[0:16, 0:P], gate[:, 0:1], None, ALU.mult).then_inc(TB[1].drained.sem, 1)

        TERN_SCALES = 5
        TERN_STEPS = 10

        def prep_ffn0_pe(pe):
            L = "prepL0f"
            pe.wait_ge(loaded["ffn0"].sem, LOADS["ffn0"])
            TB[0].wait_empty(pe, L)
            for c in range(NC):
                last = pe.transpose(TB[0].t[0:16, c * P:(c + 1) * P], lr[:, c, :], ident[:, :])
            last.then_inc(TB[0].full.sem, 1)
            TB[1].wait_empty(pe, L)
            pe.matmul(TB[1].t[0:16, 0:P], fbT[:, :], vlow[:, :], start=True, stop=True).then_inc(TB[1].full.sem, 1)

        def prep_ffn0_first_pe(pe):
            L = "prepL0f"
            TB[0].wait_drained(pe, L)
            TB[1].wait_drained(pe, L)
            pe.wait_ge(tern.sem, TERN_STEPS)
            X.wait_empty(pe, L)
            for c in range(NC):
                o = X.t[:, c * P:(c + 1) * P]
                pe.matmul(o, wfc[:, c, :], ident[:, :], start=True, stop=False)
                last = pe.matmul(o, bv[:, :], lrT[:, c * P:(c + 1) * P], start=False, stop=True)
            last.then_inc(X.full.sem, 1)

        def prep_ffn0_second_pe(pe):
            L = "prepL0f"
            Y.wait_empty(pe, L)
            for c in range(NC):
                last = pe.transpose(Y.t[:, c * P:(c + 1) * P], wpr[:, c * P:(c + 1) * P], ident[:, :])
            last.then_inc(Y.full.sem, 1)
            X.wait_drained(pe, L)
            Y.wait_drained(pe, L)

        def prep_ffn0_act(act):
            L = "prepL0f"
            TB[0].wait_full(act, L)
            act.activation(lrT[:, :], TB[0].t[0:16, :], ACT.Copy).then_inc(TB[0].drained.sem, 1)

        def prep_ffn0_weights_act(act):
            L = "prepL0f"
            X.wait_full(act, L)
            act.activation(wfcT[:, :], X.t[:, :], ACT.Copy).then_inc(X.drained.sem, 1)
            Y.wait_full(act, L)
            act.activation(wprT[:, :, :], Y.t[:, :].rearrange("p (c d) -> p c d", c=NC), ACT.Copy)\
                .then_inc(Y.drained.sem, 1)

        def fc_pe(pe, L, b, w):
            X.wait_drained(pe, L, 0, b)
            for c, bk in enumerate(FC_BANKS):
                bk.wait_empty(pe, L, 0, b)
                pe.matmul(bk.t[:, :], w[:, c * P:(c + 1) * P], xnT[:, :], start=True, stop=True)\
                    .then_inc(bk.full.sem, 1)

        def proj_pe(pe, L, b, w, row, ready, halfway=None):
            Y.wait_empty(pe, L, 0, b)
            if row is not None:
                pe.matmul(Y.t[:, :], ones[0:1, :], spread(rows[0:1, row, :], 1, NT), start=True, stop=False,
                          skip_group_check=True)
            for c in range(NC):
                if c == NC // 2 and halfway is not None:
                    halfway()
                ready(pe, b, c)
                for t in range(NT):
                    last = pe.matmul(Y.t[:, t * P:(t + 1) * P], hT[:, c, t * P:(t + 1) * P], w[:, c, :],
                                     start=row is None and c == 0 and t == 0, stop=c == NC - 1,
                                     skip_group_check=True)
            last.then_inc(Y.full.sem, 1)

        def x_rows(b):
            return x[:, b * NT:(b + 1) * NT, :] if isinstance(b, int) else x[:, bass.ds(b * NT, NT), :]

        def add_result_dve(dve, L, b):
            Y.wait_full(dve, L, 0, b)
            dve.tensor_tensor(x_rows(b), x_rows(b), Y.t[:, :].rearrange("p (t d) -> p t d", t=NT), ALU.add)\
                .then_inc(Y.drained.sem, 1)
            Y.wait_drained(dve, L, 0, b)
            dve.sem_inc(x_done.sem, 1)

        def run_ffn0(eng, name):
            L = "L0f"

            def squares(b, chunks):
                for c in chunks:
                    FC_BANKS[c].wait_drained(eng, L, 0, b)
                    eng.tensor_tensor(hT[:, c, :], hT[:, c, :], hT[:, c, :], ALU.mult).then_inc(square_ready[c].sem, 1)

            if name == "act":
                eng.wait_ge(zeroed.sem, ZEROED)

            def relus(b):
                for c, bk in enumerate(FC_BANKS):
                    bk.wait_full(eng, L, 0, b)
                    eng.activation(hT[:, c, :], bk.t[:, :], ACT.Relu).then_inc(bk.drained.sem, 1)

            def squared(pe, b, c):
                pe.wait_ge(square_ready[c].sem, square_ready[c].after(L, 0, b))

            def start(b, norm=True):
                if name == "pe":
                    fc_pe(eng, L, b, wfcT)
                elif name == "act":
                    relus(b)
                elif name == "dve":
                    if norm:
                        ln_stats_dve(eng, L, b + 1)
                    squares(b, (0, 1))
                    if norm:
                        ln_apply_dve(eng, L, b + 1)
                    squares(b, (2, 3))
                elif norm:
                    front_pool(eng, L, b + 1)

            def step(b, norm=True):
                if name == "act":
                    front_act(eng, L, b + 1)
                finish(b, lambda: front_pe(eng, L, b + 1))
                start(b + 1, norm)

            def finish(b, halfway=None):
                if name == "pe":
                    proj_pe(eng, L, b, wprT, None, squared, halfway)
                elif name == "dve":
                    add_result_dve(eng, L, b)

            if name in ("pe", "act"):
                fronts(eng, name, L, 0)
            start(0)
            with eng.Fori(0, NB - 2) as b:
                step(b)
            step(NB - 2, norm=False)
            early_norm(eng, name, L)
            finish(NB - 1)

        def fronts(eng, name, L, b):
            {"pe": front_pe, "dve": front_dve, "act": front_act, "pool": front_pool}[name](eng, L, b)

        GATE_STEPS = 13
        WHOLE = NB * NT
        flat = prob[:, :, :].rearrange("p t n -> p (t n)")
        f1 = {}
        at = 0
        for key, dims in (("xnT", (NB, 512)), ("weighted", (2, 4, P)), ("odd", (2, P)), ("sums", (NT, P)),
                          ("lg", (WHOLE, NE)), ("ex", (WHOLE, NE)), ("second", (WHOLE, NE)), ("top", (WHOLE, 8)),
                          ("index", (WHOLE, 8)), ("indexf", (WHOLE, 8)), ("gates", (WHOLE, NE)), ("gs", (4, WHOLE))):
            size = int(np.prod(dims))
            names = "abc"[:len(dims)]
            f1[key] = flat[:, at:at + size].rearrange(
                f"p ({' '.join(names)}) -> p {' '.join(names)}", **dict(zip(names[1:], dims[1:])))
            at += size
        assert at <= NT * ROWS16
        gates1 = f1["gates"]

        def plan_ffn1():
            L = "L1f"
            plan_norm(L)
            X.plan(L, 1, NB)
            O.plan(L, 1, NB)
            Y.plan(L, 1, NB)
            TB[0].plan(L, 1, NB)
            for bk in (S[0], S[1], S[2], TB[1]):
                bk.plan(L, 2, NB)
            gate_step.plan(L, GATE_STEPS)
            gate_exp.plan(L, 1)
            lhs_ready.plan(L, 2, NB)
            selected.plan(L, 1, NB)
            base_added.plan(L, 1, NB)
            chain.plan(L, 2 * NT, NB)
            pool_sum.plan(L, 3 * NT, NB)
            x_done.plan(L, 1, NB)

        def tile_banks(t):
            return (S[0], S[1]) if t % 2 == 0 else (S[2], TB[1])

        def run_ffn1(eng, name):
            L = "L1f"

            def logits_pe(b):
                X.wait_drained(eng, L, 0, b)
                O.wait_empty(eng, L, 0, b)
                for t in range(NT):
                    last = eng.matmul(O.t[:, t * NE:(t + 1) * NE], f1["xnT"][:, b, t * P:(t + 1) * P], wg1[:, :],
                                      start=True, stop=True)
                last.then_inc(O.full.sem, 1)

            def keep_xnT_act(b):
                X.wait_full(eng, L, 0, b)
                eng.activation(f1["xnT"][:, b, :], X.t[:, :], ACT.Copy).then_inc(X.drained.sem, 1)

            def logits_dve(b):
                O.wait_full(eng, L, 0, b)
                d = f1["lg"][:, b * NT:(b + 1) * NT, :] if isinstance(b, int) else f1["lg"][:, bass.ds(b * NT, NT), :]
                eng.tensor_tensor(d, O.t[:, 0:NT * NE].rearrange("p (t e) -> p t e", t=NT),
                                  spread(bg1[:, :], 1, NT), ALU.add).then_inc(O.drained.sem, 1)

            def gates_dve():
                n = 0

                def k(ins):
                    nonlocal n
                    ins.then_inc(gate_step.sem, 1)
                    eng.wait_ge(gate_step.sem, gate_step.after(L, n))
                    n += 1

                lg_, ex_, second, top, index, indexf, gs_ = (f1[i] for i in (
                    "lg", "ex", "second", "top", "index", "indexf", "gs"))
                O.wait_drained(eng, L, 0, NB - 1)
                k(eng.tensor_reduce(gs_[:, 0, :], lg_, AX.X, ALU.max))
                k(eng.tensor_tensor(lg_, lg_, spread(gs_[:, 0, :], 2, NE), ALU.subtract))
                eng.wait_ge(gate_exp.sem, gate_exp.after(L))
                for g in range(WHOLE):
                    last = eng.max(top[:, g, :], ex_[:, g, :])
                k(last)
                for g in range(WHOLE):
                    last = eng.max_index(index[:, g, :].bitcast(U32), top[:, g, :], ex_[:, g, :])
                k(last)
                k(eng.tensor_copy(indexf, index.bitcast(U32)))
                k(eng.tensor_tensor(gs_[:, 1, :], top[:, :, 0], top[:, :, 1], ALU.add))
                k(eng.reciprocal(gs_[:, 2, :], gs_[:, 1, :]))
                k(eng.tensor_tensor(gs_[:, 0, :], top[:, :, 0], gs_[:, 2, :], ALU.mult))
                k(eng.tensor_tensor(gs_[:, 3, :], top[:, :, 1], gs_[:, 2, :], ALU.mult))
                io = spread(iota8[:, :], 1, WHOLE)
                eng.tensor_tensor(gates1, io, spread(indexf[:, :, 0], 2, NE), ALU.is_equal)
                k(eng.tensor_tensor(second, io, spread(indexf[:, :, 1], 2, NE), ALU.is_equal))
                k(eng.tensor_tensor(gates1, gates1, spread(gs_[:, 0, :], 2, NE), ALU.mult))
                k(eng.tensor_tensor(second, second, spread(gs_[:, 3, :], 2, NE), ALU.mult))
                k(eng.tensor_tensor(gates1, gates1, second, ALU.add))
                assert n == GATE_STEPS, n

            def experts_pe(b, t):
                if t in (0, 2):
                    eng.wait_ge(lhs_ready.sem, lhs_ready.after(L, t // 2, b))
                for i, bk in enumerate(tile_banks(t)):
                    bk.wait_empty(eng, L, t // 2, b)
                    eng.matmul(bk.t[:, :], mixT[:, t * P:(t + 1) * P], we[:, 4 * i:4 * i + 4, :],
                               start=True, stop=True).then_inc(bk.full.sem, 1)

            def gates_transposed_pe(b):
                TB[0].wait_empty(eng, L, 0, b)
                for t in range(NT):
                    last = eng.transpose(TB[0].t[0:NE, t * P:(t + 1) * P], gsel[:, t, :], ident[:, :])
                last.then_inc(TB[0].full.sem, 1)

            def biases_pe(b):
                TB[0].wait_drained(eng, L, 0, b)
                Y.wait_empty(eng, L, 0, b)
                for t in range(NT):
                    last = eng.matmul(Y.t[:, t * P:(t + 1) * P], gT[:, t * P:(t + 1) * P], be[:, :],
                                      start=True, stop=True)
                last.then_inc(Y.full.sem, 1)

            def stage_act(b, half):
                src = f1["xnT"][:, b, :] if isinstance(b, int) else f1["xnT"][:, bass.ds(b, 1), :].squeeze(1)
                c = slice(256 * half, 256 * half + 256)
                eng.activation(mixT[:, c], src[:, c], ACT.Copy).then_inc(lhs_ready.sem, 1)

            def weigh_act(b, t):
                bk = tile_banks(t)[1]
                bk.wait_full(eng, L, t // 2, b)
                eng.wait_ge(pool_sum.sem, pool_sum.after(L, 3 * (t - 2) + 1, b))
                for e in range(4):
                    last = eng.activation(f1["weighted"][:, t % 2, e, :], bk.t[:, e * P:(e + 1) * P], ACT.Copy,
                                          scale=gsel[:, t, 4 + e:5 + e])
                last.then_inc(bk.drained.sem, 1)

            def sum_pool(b, t):
                w = f1["weighted"]
                step = lambda j: pool_sum.after(L, 3 * t + j, b)
                tile_banks(t)[1].wait_drained(eng, L, t // 2, b)
                eng.tensor_tensor(w[:, t % 2, 0:2, :], w[:, t % 2, 0:2, :], w[:, t % 2, 2:4, :], ALU.add)\
                    .then_inc(pool_sum.sem, 1)
                eng.wait_ge(pool_sum.sem, step(0))
                if t == 0:
                    eng.wait_ge(x_done.sem, x_done.after(L, 0, b - 1))
                eng.tensor_tensor(f1["sums"][:, t, :], w[:, t % 2, 0, :], w[:, t % 2, 1, :], ALU.add)\
                    .then_inc(pool_sum.sem, 1)
                eng.wait_ge(pool_sum.sem, step(1))
                tile_banks(t)[0].wait_drained(eng, L, t // 2, b)
                eng.tensor_tensor(f1["sums"][:, t, :], f1["sums"][:, t, :], f1["odd"][:, t % 2, :], ALU.add)\
                    .then_inc(pool_sum.sem, 1)

            def weigh_dve(b, t):
                xt = x[:, b * NT + t, :]
                bk = tile_banks(t)[0]
                odd = f1["odd"][:, t % 2, :]
                g = lambda e: gsel[:, t, e:e + 1]
                part = lambda e: bk.t[:, e * P:(e + 1) * P]
                bk.wait_full(eng, L, t // 2, b)
                eng.scalar_tensor_tensor(xt, part(0), g(0), xt, ALU.mult, ALU.add).then_inc(chain.sem, 1)
                eng.wait_ge(pool_sum.sem, pool_sum.after(L, 3 * (t - 2) + 2, b))
                eng.tensor_scalar(odd, part(1), g(1), None, ALU.mult).then_inc(chain.sem, 1)
                eng.wait_ge(chain.sem, chain.after(L, 2 * t, b))
                eng.scalar_tensor_tensor(xt, part(2), g(2), xt, ALU.mult, ALU.add)
                eng.wait_ge(chain.sem, chain.after(L, 2 * t + 1, b))
                eng.scalar_tensor_tensor(odd, part(3), g(3), odd, ALU.mult, ALU.add).then_inc(bk.drained.sem, 1)

            def select_dve(b):
                src = gates1[:, b * NT:(b + 1) * NT, :] if isinstance(b, int) else gates1[:, bass.ds(b * NT, NT), :]
                eng.tensor_copy(gsel[:, :, :], src).then_inc(selected.sem, 1)

            def finish_dve(b):
                eng.wait_ge(pool_sum.sem, pool_sum.after(L, 3 * NT - 1, b))
                eng.tensor_tensor(x_rows(b), x_rows(b), f1["sums"], ALU.add).then_inc(base_added.sem, 1)
                eng.wait_ge(base_added.sem, base_added.after(L, 0, b))
                add_result_dve(eng, L, b)

            def body(b, last):
                wait_selected = lambda: eng.wait_ge(selected.sem, selected.after(L, 0, b))
                if name == "pe":
                    experts_pe(b, 0)
                    experts_pe(b, 1)
                    wait_selected()
                    gates_transposed_pe(b)
                    experts_pe(b, 2)
                    experts_pe(b, 3)
                    biases_pe(b)
                elif name == "act":
                    wait_selected()
                    weigh_act(b, 0)
                    weigh_act(b, 1)
                    if not last:
                        stage_act(b + 1, 0)
                    TB[0].wait_full(eng, L, 0, b)
                    eng.activation(gT[:, :], TB[0].t[0:NE, :], ACT.Copy).then_inc(TB[0].drained.sem, 1)
                    weigh_act(b, 2)
                    weigh_act(b, 3)
                    if not last:
                        stage_act(b + 1, 1)
                elif name == "dve":
                    for t in range(1, NT):
                        weigh_dve(b, t)
                    if not last:
                        TB[1].wait_drained(eng, L, 1, b)
                        S[2].wait_drained(eng, L, 1, b)
                        TB[0].wait_full(eng, L, 0, b)
                        select_dve(b + 1)
                        eng.wait_ge(selected.sem, selected.after(L, 0, b + 1))
                        weigh_dve(b + 1, 0)
                    else:
                        early_norm(eng, name, L)
                    finish_dve(b)
                elif name == "pool":
                    for t in range(NT - 1):
                        sum_pool(b, t)
                    if last:
                        early_norm(eng, name, L)
                    sum_pool(b, NT - 1)

            norm_sets = ((stats, mv, ve, rstd), (stats_z, mv_z, ve_z, rstd_z))
            if name == "dve":
                ln_stats_dve(eng, L, 1, 0, *norm_sets[1][0:2])
                for b in range(1, NB):
                    if b + 1 < NB:
                        ln_stats_dve(eng, L, b + 1, 0, *norm_sets[(b + 1) % 2][0:2])
                    ln_apply_dve(eng, L, b, 0, norm_sets[b % 2][1], norm_sets[b % 2][3])
                    if b >= 2:
                        logits_dve(b - 2)
                logits_dve(NB - 2)
                logits_dve(NB - 1)
                gates_dve()
                select_dve(0)
                eng.wait_ge(selected.sem, selected.after(L, 0, 0))
                weigh_dve(0, 0)
            elif name == "pool":
                for b in range(1, NB):
                    ln_rstd_pool(eng, L, b, 0, *norm_sets[b % 2][1:])
            else:
                for b in range(NB):
                    if name == "pe":
                        front_pe(eng, L, b)
                        if b:
                            logits_pe(b - 1)
                    else:
                        keep_xnT_act(b)
                if name == "pe":
                    logits_pe(NB - 1)
                if name == "act":
                    X.wait_drained(eng, L, 0, NB - 1)
                    stage_act(0, 0)
                    stage_act(0, 1)
                    eng.wait_ge(gate_step.sem, gate_step.after(L, 1))
                    eng.activation(f1["ex"], f1["lg"], ACT.Exp).then_inc(gate_exp.sem, 1)
                    prep2_act(eng)
                else:
                    prep2_pe(eng)
            with eng.Fori(0, NB - 1) as b:
                body(b, False)
            body(NB - 1, True)

        def plan_ffn2():
            L = "L2f"
            plan_norm(L)
            X.plan(L, 1, NB)
            O.plan(L, 2, NB)
            Y.plan(L, 1, NB)
            for bk in (S[0], S[1], TB[0], TB[1]):
                bk.plan(L, 2, NB)
            x_done.plan(L, 1, NB)

        w1e = big[:, 0, :].rearrange("p (e f) -> p e f", e=NE)
        w2e = big[:, 1, :].rearrange("p (e c d) -> p e c d", e=NE, c=NC)

        def run_ffn2(eng, name):
            L = "L2f"

            def front(b):
                if name == "pe":
                    front_pe(eng, L, b)
                    eng.wait_ge(z_ready.sem, z_ready.after(L, 0, b))
                    O.wait_empty(eng, L, 0, b)
                    for t in range(NT):
                        last = eng.transpose(O.t[:, t * P:(t + 1) * P], z[:, t, :], ident[:, :])
                    last.then_inc(O.full.sem, 1)
                elif name == "act":
                    front_act(eng, L, b)
                    O.wait_full(eng, L, 0, b)
                    eng.activation(mixT[:, :], O.t[:, :], ACT.Identity, scale=cols2[:, 0:1], bias=cols2[:, 1:2])\
                        .then_inc(O.drained.sem, 1)
                else:
                    fronts(eng, name, L, b)

            def attn_linear(b):
                if name == "pe":
                    O.wait_drained(eng, L, 0, b)
                    eng.matmul(O.t[:, :], attn_w[:, :], mixT[:, :], start=True, stop=True).then_inc(O.full.sem, 1)
                elif name == "dve":
                    O.wait_full(eng, L, 1, b)
                    X.wait_drained(eng, L, 0, b)
                    eng.scalar_tensor_tensor(xaT[:, :], O.t[:, :], cols2[:, 2:3], xnT[:, :], ALU.add, ALU.add)\
                        .then_inc(O.drained.sem, 1)

            def hidden(b, t):
                e = (b * NT + t) % NE
                bk = S[t % 2]
                if name == "pe":
                    if t == 0:
                        O.wait_drained(eng, L, 1, b)
                    bk.wait_empty(eng, L, t // 2, b)
                    for c in range(NC):
                        last = eng.matmul(bk.t[:, c * P:(c + 1) * P], w1e[:, e, c * P:(c + 1) * P],
                                          xaT[:, t * P:(t + 1) * P], start=True, stop=True)
                    last.then_inc(bk.full.sem, 1)
                elif name == "act":
                    bk.wait_full(eng, L, t // 2, b)
                    for c in range(NC):
                        last = eng.activation(hT[:, c, (t % 2) * P:(t % 2 + 1) * P], bk.t[:, c * P:(c + 1) * P],
                                              ACT.Gelu, bias=b1c[:, e, c:c + 1])
                    last.then_inc(bk.drained.sem, 1)

            def down(b, t):
                e = (b * NT + t) % NE
                bk = TB[t % 2]
                if name == "pe":
                    S[t % 2].wait_drained(eng, L, t // 2, b)
                    bk.wait_empty(eng, L, t // 2, b)
                    for c in range(NC):
                        last = eng.matmul(bk.t[:, 0:P], w2e[:, e, c, :], hT[:, c, (t % 2) * P:(t % 2 + 1) * P],
                                          start=c == 0, stop=c == NC - 1)
                    last.then_inc(bk.full.sem, 1)
                elif name == "act":
                    bk.wait_full(eng, L, t // 2, b)
                    eng.activation(mix[:, t, :], bk.t[:, 0:P], ACT.Identity, bias=b2c[:, e:e + 1])\
                        .then_inc(bk.drained.sem, 1)

            def last_linear(b):
                if name == "pe":
                    TB[0].wait_drained(eng, L, 1, b)
                    TB[1].wait_drained(eng, L, 1, b)
                    Y.wait_empty(eng, L, 0, b)
                    eng.matmul(Y.t[:, :], ones[0:1, :], spread(rows[0:1, 3, :], 1, NT), start=True, stop=False,
                               skip_group_check=True)
                    for t in range(NT):
                        last = eng.matmul(Y.t[:, t * P:(t + 1) * P], mix[:, t, :], next_w[:, :], start=False,
                                          stop=True, skip_group_check=True)
                    last.then_inc(Y.full.sem, 1)
                elif name == "act":
                    Y.wait_full(eng, L, 0, b)
                    if b:
                        eng.wait_ge(x_done.sem, x_done.after(L, 0, b - 1))
                    eng.activation(gout[:, :], Y.t[:, :], ACT.Gelu).then_inc(Y.drained.sem, 1)
                elif name == "dve":
                    Y.wait_drained(eng, L, 0, b)
                    eng.tensor_tensor(x_rows(b), x_rows(b), gout[:, :].rearrange("p (t d) -> p t d", t=NT), ALU.add)\
                        .then_inc(x_done.sem, 1)

            if name != "pool":
                eng.wait_ge(loaded["ffn2"].sem, LOADS["ffn2"])
            if name in ("pe", "act"):
                front(0)
            if name == "dve":
                ln_stats_dve(eng, L, 1)
            attn_linear(0)
            hidden(0, 0)
            hidden(0, 1)
            if name == "dve":
                ln_apply_dve(eng, L, 1)
                ln_stats_dve(eng, L, 1, 1)
                ln_apply_dve(eng, L, 1, 1)
            elif name == "pool":
                front(1)
            for b in range(NB):
                down(b, 0)
                hidden(b, 2)
                if b == NB - 1 and name in ("pe", "act"):
                    (prep03_pe if name == "pe" else prep03_act)(eng, "L3x", 0)
                if b < NB - 1 and name in ("pe", "act"):
                    front(b + 1)
                down(b, 1)
                hidden(b, 3)
                if b == NB - 1 and name == "pe":
                    keys_pe(eng, "L3x")
                if b == NB - 1 and name == "dve":
                    for i in range(NB):
                        keys_dve(eng, "L3x", i)
                if b < NB - 2 and name == "dve":
                    ln_stats_dve(eng, L, b + 2)
                if b < NB - 1:
                    attn_linear(b + 1)
                if b < NB - 2 and name == "dve":
                    ln_apply_dve(eng, L, b + 2)
                    ln_stats_dve(eng, L, b + 2, 1)
                    ln_apply_dve(eng, L, b + 2, 1)
                elif b < NB - 2 and name == "pool":
                    front(b + 2)
                elif b == NB - 2:
                    early_norm(eng, name, L)
                down(b, 2)
                if b < NB - 1:
                    hidden(b + 1, 0)
                down(b, 3)
                if b < NB - 1:
                    hidden(b + 1, 1)
                last_linear(b)

        RES_STEPS = 16
        f3 = {}
        at = NTOK * P // P
        for key, dims in (("ex", (WHOLE, NE + 2)), ("top", (WHOLE, 8)),
                          ("index", (WHOLE, 8)), ("gs", (4, WHOLE))):
            size = int(np.prod(dims))
            f3[key] = flat[:, at:at + size].rearrange("p (a b) -> p a b", b=dims[1])
            at += size
        assert at <= NT * ROWS16
        f3["lg"] = gbf[:, ROWS_SENT + NTOK:ROWS_SENT + NTOK + WHOLE * (NE + 2)].rearrange("p (a b) -> p a b", b=NE + 2)
        xn3 = hT[:, 0, :].rearrange("p (t d) -> p t d", t=NT)
        xnT3 = hT[:, 1, :]

        def kept_xnT(b):
            if isinstance(b, int):
                return xnT[:, :] if b == NB - 1 else sentT[:, 512 * b:512 * b + 512]
            return sentT.rearrange("p (b n) -> p b n", b=NB)[:, bass.ds(b, 1), :].squeeze(1)

        def norm_unit(b, j):
            return ("L3f norm", j, 0) if isinstance(b, int) and b == NB - 1 else ("L3x with norm", j, b)

        EARLY = NB - 1

        def plan_ffn3():
            L = "L3f"
            for e in (stats3_ready, mv3_ready, ve3_ready, rstd3_ready):
                e.plan(L, 2, NB)
            xn3_ready.plan(L, 1, NB)
            z_ready.plan(L, 1, NB)
            Y.plan("L3f norm", 2)
            base_added.plan(L, 1, NB)
            normed_ready.plan(L, 2, NB)
            res_step.plan(L, RES_STEPS)
            res_exp.plan(L, 1)
            TB[1].plan("place", 1)
            for bk in FC_BANKS + [Y]:
                bk.plan(L, 1, EARLY)
            for bk in FC_BANKS:
                bk.plan("sent", 1)
                bk.plan("experts", NE // 2)
            O.plan("experts", NE // 2)
            Y.plan("experts", NE // 2)
            for bk in FC_BANKS + [Y]:
                bk.plan("L3f late", 1)
            x_done.plan(L, 1, NB)

        def ffn3_stats(dve, b, j):
            L = "L3f"
            if j == 0:
                dve.wait_ge(x_done.sem, x_done.after("L3x", 0, b))
                if not (isinstance(b, int) and b == 0):
                    dve.wait_ge(z_ready.sem, z_ready.after(L, 0, b - 1))
            else:
                dve.wait_ge(xn3_ready.sem, xn3_ready.after(L, 0, b))
            dve.sem_inc(passed.sem, 1)
            for t in range(NT):
                last = dve.bn_stats(stats_z[:, t, :], x[:, b * NT + t, :] if j == 0 else xn3[:, t, :])
            last.then_inc(stats3_ready.sem, 1)
            dve.wait_ge(stats3_ready.sem, stats3_ready.after(L, j, b))
            dve.sem_inc(passed.sem, 1)
            for t in range(NT):
                last = dve.bn_aggr(mv_z[:, t, :], stats_z[:, t, :])
            last.then_inc(mv3_ready.sem, 1)

        def ffn3_rstd(pool, b, j):
            L = "L3f"
            pool.wait_ge(mv3_ready.sem, mv3_ready.after(L, j, b))
            pool.tensor_tensor(ve_z[:, :], mv_z[:, :, 1], (eps5, eps12)[j][:, :], ALU.add).then_inc(ve3_ready.sem, 1)
            pool.wait_ge(ve3_ready.sem, ve3_ready.after(L, j, b))
            pool.tensor_tensor(rstd_z[:, :], ve_z[:, :], minus_half[:, :], ALU.pow).then_inc(rstd3_ready.sem, 1)

        def ffn3_xn(dve, b):
            L = "L3f"
            dve.wait_ge(rstd3_ready.sem, rstd3_ready.after(L, 0, b))
            if not (isinstance(b, int) and b == 0):
                dve.wait_ge(z_ready.sem, z_ready.after(L, 0, b - 1))
                dve.wait_ge(base_added.sem, base_added.after(L, 0, b - 1))
            for t in range(NT):
                last = dve.tensor_scalar(xn3[:, t, :], x[:, b * NT + t, :], mv_z[:, t, 0:1], rstd_z[:, t:t + 1],
                                         ALU.subtract, ALU.mult)
            last.then_inc(xn3_ready.sem, 1)

        def ffn3_base(dve, b):
            L = "L3f"
            dve.wait_ge(xn3_ready.sem, xn3_ready.after(L, 0, b))
            dve.tensor_tensor(x_rows(b), x_rows(b), xn3, ALU.add).then_inc(base_added.sem, 1)

        def ffn3_z(dve, b):
            L = "L3f"
            dve.wait_ge(rstd3_ready.sem, rstd3_ready.after(L, 1, b))
            if not (isinstance(b, int) and b == 0):
                Y.wait_full(dve, *norm_unit(b - 1, 0))
                dve.wait_ge(normed_ready.sem, normed_ready.after(L, 0, b - 1))
            for t in range(NT):
                last = dve.tensor_scalar(z[:, t, :], xn3[:, t, :], mv_z[:, t, 0:1], rstd_z[:, t:t + 1],
                                         ALU.subtract, ALU.mult)
            last.then_inc(z_ready.sem, 1)

        def ffn3_transposes_pe(pe, b):
            pe.wait_ge(z_ready.sem, z_ready.after("L3f", 0, b))
            Y.wait_empty(pe, *norm_unit(b, 0))
            for t in range(NT):
                last = pe.transpose(Y.t[:, t * P:(t + 1) * P], z[:, t, :], ident[:, :])
            last.then_inc(Y.full.sem, 1)

        def ffn3_keep_act(act, b):
            Y.wait_full(act, *norm_unit(b, 0))
            if isinstance(b, int) and b == NB - 1:
                act.activation(xnT[:, :], Y.t[:, :], ACT.Identity, scale=cols3[:, 0:1], bias=cols3[:, 1:2])\
                    .then_inc(Y.drained.sem, 1)
                return
            act.activation(kept_xnT(b), Y.t[:, :], ACT.Identity, scale=cols3[:, 0:1], bias=cols3[:, 1:2])
            act.activation(xnT3, Y.t[:, :], ACT.Identity, scale=cols3[:, 0:1], bias=cols3[:, 1:2])\
                .then_inc(Y.drained.sem, 1)

        def ffn3_logits_pe(pe, b):
            src = xnT if isinstance(b, int) and b == NB - 1 else xnT3
            Y.wait_empty(pe, *norm_unit(b, 1))
            for t in range(NT):
                last = pe.matmul(Y.t[:, t * 10:(t + 1) * 10], src[:, t * P:(t + 1) * P], wgc[:, :],
                                 start=True, stop=True)
            last.then_inc(Y.full.sem, 1)

        def ffn3_logits_dve(dve, b):
            Y.wait_full(dve, *norm_unit(b, 1))
            d = f3["lg"][:, b * NT:(b + 1) * NT, :] if isinstance(b, int) else f3["lg"][:, bass.ds(b * NT, NT), :]
            dve.tensor_copy(d, Y.t[:, 0:NT * 10].rearrange("p (t e) -> p t e", t=NT)).then_inc(Y.drained.sem, 1)

        def ffn3_normed(pool, b):
            L = "L3f"
            dst = normed[:, b * NT:(b + 1) * NT, 0:P] if isinstance(b, int) else normed[:, bass.ds(b * NT, NT), 0:P]
            pool.wait_ge(z_ready.sem, z_ready.after(L, 0, b))
            pool.sem_inc(pool_passed.sem, 1)
            pool.tensor_tensor(dst, z[:, :, :], spread(nw_all, 1, NT), ALU.mult).then_inc(normed_ready.sem, 1)
            pool.wait_ge(normed_ready.sem, normed_ready.after(L, 0, b))
            pool.sem_inc(pool_passed.sem, 1)
            pool.tensor_tensor(dst, dst, spread(nb_all, 1, NT), ALU.add).then_inc(normed_ready.sem, 1)

        def run_ffn3(eng, name):
            L = "L3f"
            last = NB - 1
            if name == "pe":
                ffn3_transposes_pe(eng, last)
                ffn3_logits_pe(eng, last)
            elif name == "act":
                ffn3_keep_act(eng, last)
            elif name == "dve":
                ffn3_stats(eng, last, 0)
                ffn3_xn(eng, last)
                ffn3_stats(eng, last, 1)
                ffn3_base(eng, last)
                ffn3_z(eng, last)
                ffn3_logits_dve(eng, last)
            else:
                ffn3_rstd(eng, last, 0)
                ffn3_rstd(eng, last, 1)
                ffn3_normed(eng, last)

            def mlp(b, ph, u):
                if name == "pe":
                    src = kept_xnT(b)
                    for c, bk in enumerate(FC_BANKS):
                        bk.wait_empty(eng, ph, 0, u)
                        eng.matmul(bk.t[:, :], res_w1[:, c * P:(c + 1) * P], src, start=True, stop=True)\
                            .then_inc(bk.full.sem, 1)
                    proj_pe(eng, ph, u, res_w2, 4, lambda pe, u_, c: FC_BANKS[c].wait_drained(pe, ph, 0, u_))
                elif name == "act":
                    for c, bk in enumerate(FC_BANKS):
                        bk.wait_full(eng, ph, 0, u)
                        eng.activation(hT[:, c, :], bk.t[:, :], ACT.Gelu_apprx_tanh, bias=cols3[:, 2 + c:3 + c])\
                            .then_inc(bk.drained.sem, 1)
                elif name == "dve":
                    Y.wait_full(eng, ph, 0, u)
                    for t in range(NT):
                        g = b * NT + t
                        xt = x[:, g, :]
                        ins = eng.scalar_tensor_tensor(xt, Y.t[:, t * P:(t + 1) * P],
                                                       coef0[:, g:g + 1] if isinstance(b, int)
                                                       else coef0[:, bass.ds(g, 1)], xt, ALU.mult, ALU.add)
                    ins.then_inc(Y.drained.sem, 1)

            tile_hidden = lambda e: (S[0], S[1]) if e % 2 == 0 else (S[2], TB[0])
            tile_out = lambda e: O if e % 2 == 0 else Y
            if name == "pe":
                eng.wait_ge(route_made.sem, 2)
                eng.wait_ge(res_step.sem, res_step.after(L, 7))
                TB[1].wait_empty(eng, "place")
                o = TB[1].t[:, 0:P].rearrange("p (g e) -> p g e", e=NE)
                eng.matmul(o, earlier, chosen, start=True, stop=False, skip_group_check=True)
                G = NB * NT
                for g in range(G - 1):
                    last = eng.matmul(o[:, g + 1:G, :], onesb, spread(chosen[:, g, :], 1, G - 1 - g),
                                      start=False, stop=g == G - 2, skip_group_check=True)
                last.then_inc(TB[1].full.sem, 1)
            elif name == "act":
                eng.wait_ge(res_step.sem, res_step.after(L, 3))
                eng.activation(f3["ex"], f3["lg"], ACT.Exp).then_inc(res_exp.sem, 1)
            elif name == "dve":
                n, m = 0, 0

                def k(ins):
                    nonlocal n
                    ins.then_inc(res_step.sem, 1)
                    eng.wait_ge(res_step.sem, res_step.after(L, n))
                    n += 1

                def step(ins):
                    nonlocal m
                    m += 1
                    ins.then_inc(route_step.sem, 1)
                    eng.wait_ge(route_step.sem, m)

                lg_, ex_, top, index, gs_ = (f3[i] for i in ("lg", "ex", "top", "index", "gs"))
                Y.wait_drained(eng, *norm_unit(NB - 1, 1))
                for i, (c0, c1) in enumerate(((0, NE), (NE, NE + 2))):
                    k(eng.tensor_reduce(gs_[:, i, :], lg_[:, :, c0:c1], AX.X, ALU.max))
                    k(eng.tensor_tensor(lg_[:, :, c0:c1], lg_[:, :, c0:c1], spread(gs_[:, i, :], 2, c1 - c0), ALU.subtract))
                for g in range(WHOLE):
                    last = eng.max(top[:, g, :], lg_[:, g, 0:NE])
                k(last)
                for g in range(WHOLE):
                    last = eng.max_index(index[:, g, :].bitcast(U32), top[:, g, :], lg_[:, g, 0:NE])
                k(last)
                k(eng.tensor_copy(expert_of, index[:, :, 0].bitcast(U32)))
                k(eng.tensor_tensor(chosen, spread(iota8[:, :], 1, WHOLE), spread(expert_of, 2, NE), ALU.is_equal))
                TB[1].wait_full(eng, "place")
                eng.tensor_tensor(counted, TB[1].t[:, 0:P].rearrange("p (g e) -> p g e", e=NE), chosen, ALU.mult)\
                    .then_inc(TB[1].drained.sem, 1)
                TB[1].wait_drained(eng, "place")
                step(eng.tensor_reduce(place, counted, AX.X, ALU.add))
                step(eng.tensor_scalar(kept, place, float(CAP), None, ALU.is_lt))
                step(eng.scalar_tensor_tensor(slot, expert_of, float(CAP), place, ALU.mult, ALU.add))
                step(eng.tensor_scalar(dropped, kept, -float(2 * NTOK), float(2 * NTOK), ALU.mult, ALU.add))
                step(eng.tensor_tensor(slot_put, slot, dropped, ALU.add))
                eng.wait_ge(res_exp.sem, res_exp.after(L))
                k(eng.tensor_reduce(gs_[:, 0, :], ex_[:, :, 0:NE], AX.X, ALU.add))
                k(eng.reciprocal(gs_[:, 2, :], gs_[:, 0, :]))
                k(eng.tensor_reduce(gs_[:, 1, :], ex_[:, :, NE:NE + 2], AX.X, ALU.add))
                k(eng.reciprocal(gs_[:, 3, :], gs_[:, 1, :]))
                k(eng.tensor_tensor(coef0, ex_[:, :, NE], gs_[:, 3, :], ALU.mult))
                k(eng.tensor_tensor(gs_[:, 0, :], ex_[:, :, NE + 1], gs_[:, 3, :], ALU.mult))
                k(eng.tensor_tensor(gs_[:, 1, :], gs_[:, 0, :], gs_[:, 2, :], ALU.mult))
                k(eng.tensor_tensor(weight_of, gs_[:, 1, :], kept, ALU.mult))
                assert n == RES_STEPS, n
            else:
                eng.wait_ge(route_step.sem, 5)
                eng.wait_ge(zeroed.sem, ZEROED)
                eng.wait_ge(normed_ready.sem, normed_ready.after(L, 1, NB - 1))
                for g in range(WHOLE):
                    eng.indirect_dma_start(out=dispatched_d, out_offset=bass.IndirectOffsetOnAxis(ap=slot_put[:, g:g + 1], axis=0),
                                           in_=normed[:, g, :], in_offset=None, bounds_check=NTOK - 1,
                                           oob_is_err=False).then_inc(scattered.sem, 16)

            if name != "pool":
                with eng.Fori(0, EARLY) as b:
                    mlp(b, L, b)

            if name != "pool":
                eng.wait_ge(loaded["ffn3"].sem, LOADS["ffn3"])
            if name == "pe":
                eng.wait_ge(sent_loaded.sem, 16)
                for i, bk in enumerate(FC_BANKS):
                    bk.wait_empty(eng, "sent")
                    for t in range(4):
                        last = eng.transpose(bk.t[:, t * P:(t + 1) * P], sent[:, 4 * i + t, 0:P], ident[:, :])
                    last.then_inc(bk.full.sem, 1)
                for e in range(NE + 1):
                    if e < NE:
                        if e % 2 == 0:
                            FC_BANKS[e // 2].wait_drained(eng, "sent")
                        for i, bk in enumerate(tile_hidden(e)):
                            bk.wait_empty(eng, "experts", e // 2)
                            for c in range(2):
                                f = (2 * i + c) * P
                                last = eng.matmul(bk.t[:, c * 256:(c + 1) * 256], w1e[:, e, f:f + P],
                                                  sentT[:, e * CAP:(e + 1) * CAP], start=True, stop=True)
                            last.then_inc(bk.full.sem, 1)
                    if e > 0:
                        q = e - 1
                        bo = tile_out(q)
                        bo.wait_empty(eng, "experts", q // 2)
                        for bk in tile_hidden(q):
                            bk.wait_drained(eng, "experts", q // 2)
                        for c in range(NC):
                            for j in range(2):
                                col = (q % 2) * 256 + j * P
                                last = eng.matmul(bo.t[:, j * P:(j + 1) * P], hT[:, c, col:col + P], w2e[:, q, c, :],
                                                  start=c == 0 and j == 0, stop=c == NC - 1, skip_group_check=True)
                        last.then_inc(bo.full.sem, 1)
            elif name == "act":
                for i, bk in enumerate(FC_BANKS):
                    bk.wait_full(eng, "sent")
                    eng.activation(sentT[:, i * 512:(i + 1) * 512], bk.t[:, :], ACT.Copy).then_inc(bk.drained.sem, 1)
                for e in range(NE):
                    for i, bk in enumerate(tile_hidden(e)):
                        bk.wait_full(eng, "experts", e // 2)
                        for c in range(2):
                            col = (e % 2) * 256
                            last = eng.activation(hT[:, 2 * i + c, col:col + 256], bk.t[:, c * 256:(c + 1) * 256],
                                                  ACT.Gelu_apprx_tanh, bias=b1c[:, e, 2 * i + c:2 * i + c + 1])
                        last.then_inc(bk.drained.sem, 1)
            elif name == "dve":
                eng.wait_ge(sent_loaded.sem, 16)
                eng.tensor_scalar(token_of_slot, sent[:, :, P], float(2 * NTOK), None, ALU.add)\
                    .then_inc(token_known.sem, 1)
                for e in range(NE):
                    bo = tile_out(e)
                    bo.wait_full(eng, "experts", e // 2)
                    eng.tensor_tensor(expert_out[:, 2 * e:2 * e + 2, :], bo.t[:, 0:256].rearrange("p (j d) -> p j d", j=2),
                                      spread(out_b_all[:, e, :], 1, 2), ALU.add).then_inc(bo.drained.sem, 1)
            else:
                eng.wait_ge(token_known.sem, 1)
                for e in range(NE):
                    tile_out(e).wait_drained(eng, "experts", e // 2)
                    for g in range(e * CAP // P, (e + 1) * CAP // P):
                        eng.indirect_dma_start(out=returned_d,
                                               out_offset=bass.IndirectOffsetOnAxis(ap=token_of_slot[:, g:g + 1], axis=0),
                                               in_=expert_out[:, g, :], in_offset=None, bounds_check=NTOK - 1,
                                               oob_is_err=False).then_inc(returned.sem, 16)

            if name in ("pe", "act"):
                mlp(NB - 1, "L3f late", 0)
            if name == "dve":
                for b in range(NB):
                    if b == 1:
                        mlp(NB - 1, "L3f late", 0)
                    if b == NB - 1:
                        Y.wait_drained(eng, "L3f late")
                    eng.wait_ge(gathered[b].sem, 16)
                    for t in range(NT):
                        g = b * NT + t
                        last = eng.scalar_tensor_tensor(x[:, g, :], got[:, g, :], weight_of[:, g:g + 1], x[:, g, :],
                                                        ALU.mult, ALU.add)
                    last.then_inc(x_done.sem, 1)

        def route_constants_pool(pool):
            pool.wait_ge(x_done.sem, x_done.after("L2f", 0, NB - 1))
            pool.memset(earlier, 1.0).then_inc(pool_step.sem, 1)
            pool.wait_ge(pool_step.sem, POOL_STEPS + 1)
            pool.affine_select(out=earlier, in_=earlier, compare_op=ALU.is_gt, fill=0.0, base=0,
                               pattern=[[1, P]], channel_multiplier=-1).then_inc(route_made.sem, 1)
            pool.memset(onesb, 1.0).then_inc(route_made.sem, 1)
            pool.iota(token_number, pattern=[[P, NTOK // P]], base=-2 * NTOK, channel_multiplier=1).then_inc(pool_step.sem, 1)
            pool.wait_ge(pool_step.sem, POOL_STEPS + 2)
            pool.tensor_copy(normed[:, :, P], token_number).then_inc(pool_step.sem, 1)
            pool.wait_ge(pool_step.sem, POOL_STEPS + 3)

        POOL_STEPS = 7

        LOADS = {}
        MADE = 1

        TB[1].plan("phase", 11)
        plan_prep03("L0x")
        plan_attention("L0x")
        plan_ffn0()
        plan_prep1()
        plan_attention("L1x")
        plan_prep2(True)
        plan_ffn1()
        plan_prep2(False)
        plan_attention("L2x")
        plan_ffn2()
        plan_prep03("L3x")
        plan_attention("L3x")
        plan_ffn3()

        WAVES = 10
        PHB = TB[1]
        phase_d = event("phase_dve")
        phase_a = event("phase_act")

        def start_pe(pe):
            for i in range(WAVES):
                if i == 0:
                    pe.wait_ge(loaded["const"].sem, LOADS["const"])
                    pe.wait_ge(phase_d.sem, 1)
                else:
                    pe.wait_ge(phase_a.sem, i)
                PHB.wait_empty(pe, "phase", i)
                pe.matmul(PHB.t[0:H16, 0:1], phw[:, 0:H16], ph[:, 0:1], start=True, stop=True)\
                    .then_inc(PHB.full.sem, 1)
                if i < PREP03_PARTS:
                    prep03_pe(pe, "L0x", i)
            pe.wait_ge(phase_d.sem, 2 + 3 * WAVES + 4)
            PHB.wait_empty(pe, "phase", WAVES)
            pe.matmul(PHB.t[:, 0:H16], ones16[:, :], dg[:, :], start=True, stop=True).then_inc(PHB.full.sem, 1)

        def start_dve(dve):
            dve.memset(ph[:, 0:1], 0.0).then_inc(phase_d.sem, 1)
            dve.memset(ones16[:, :], 1.0)
            dve.wait_ge(loaded["const"].sem, LOADS["const"])
            dve.wait_ge(made.sem, MADE)
            n = 1

            def step(ins):
                nonlocal n
                n += 1
                ins.then_inc(phase_d.sem, 1)
                dve.wait_ge(phase_d.sem, n)

            step(dve.tensor_scalar(ph[:, 9:10], ph[:, 7:8], 0.01, None, ALU.mult))
            for i in range(WAVES):
                PHB.wait_full(dve, "phase", i)
                dve.tensor_scalar(ph[:, 2:3], PHB.t[0:H16, 0:1], ph[:, 9:10], phw[:, 16:17], ALU.mult, ALU.add)\
                    .then_inc(PHB.drained.sem, 1)
                PHB.wait_drained(dve, "phase", i)
                step(dve.tensor_scalar(ph[:, 4:5], ph[:, 2:3], 1.0 / TWO_PI, ROUND, ALU.mult, ALU.add))
                step(dve.tensor_scalar(ph[:, 5:6], ph[:, 4:5], ROUND, -TWO_PI, ALU.subtract, ALU.mult))
                if i:
                    dve.wait_ge(phase_a.sem, i)
                step(dve.tensor_tensor(ph[:, 6:7], ph[:, 5:6], ph[:, 2:3], ALU.add))
                if i < PREP03_PARTS:
                    prep03_dve(dve, "L0x", i)
                if i == 5:
                    front_dve(dve, "L0x", 0)
                if i == 6:
                    ternary_scales_dve(dve)
            step(dve.tensor_scalar(ph[:, 3:4], ph[:, 6:7], -1.0, None, ALU.mult))
            step(dve.tensor_tensor(ph[:, 1:2], ph[:, 6:7], ph[:, 3:4], ALU.min))
            step(dve.tensor_scalar(ph[:, 2:3], ph[:, 1:2], math.pi / 2, None, ALU.add))
            dve.wait_ge(phase_a.sem, WAVES + 1)
            step(dve.tensor_scalar(dg[:, :], ident[0:H16, 0:H16], ph[:, 8:9], 0.1, ALU.mult, ALU.mult))
            PHB.wait_full(dve, "phase", WAVES)
            dve.tensor_copy(head_bias[:, :], PHB.t[:, 0:H16]).then_inc(PHB.drained.sem, 1)
            PHB.wait_drained(dve, "phase", WAVES)

        def start_act(act):
            for i in range(WAVES):
                act.wait_ge(phase_d.sem, 2 + 3 * (i + 1))
                act.activation(ph[:, 0:1], ph[:, 6:7], ACT.Sin).then_inc(phase_a.sem, 1)
                if i < PREP03_PARTS:
                    prep03_act(act, "L0x", i)
            act.wait_ge(phase_d.sem, 2 + 3 * WAVES + 3)
            act.activation(ph[:, 8:9], ph[:, 2:3], ACT.Sin).then_inc(phase_a.sem, 1)

        LOADS.update({"const": 48, "w0": 80, "ctx": 16, "ffn0": 96, "attn1": 80, "mask1": 32, "ffn1": 64,
                      "attn2": 80, "attn3": 64, "ffn2": 160, "mask3": 16, "small3": 10 * 16, "ffn3": 4 * 16})

        block = ctx.enter_context(nc.Block())

        @block.sync
        def _(sp):
            load(sp, "ctx", ctx_tok[:, :, :], a["ctx_1024"].rearrange("b k d -> k b d"))
            for i, n in enumerate(("Wq", "Wk", "Wv")):
                load(sp, "w0", w0[:, i, :].rearrange("d (h k) -> d h k", h=H16),
                     a["L0_xattn_" + n].rearrange("h d k -> d h k"))
            load(sp, "x", x[:, :, :], a["x"].rearrange("b (t p) d -> p (b t) d", p=P))
            load(sp, "w0", w0[:, 3, :], a["L0_xattn_out_w"])
            load(sp, "w0", rows[0:1, 0, :], a["L0_xattn_out_b"].rearrange("(a n) -> a n", a=1))
            sp.wait_ge(zeros_made.sem, 1)
            zeros = hT[:, :, :].rearrange("p c n -> p (c n)")
            dispatched_rows = dispatched_d.rearrange("(p r) d -> p (r d)", p=P)
            sp.dma_start(dispatched_rows[:, 0:NTOK], zeros).then_inc(zeroed.sem, 16)
            sp.dma_start(dispatched_rows[:, NTOK:ROWS_SENT], zeros[:, 0:ROWS_SENT - NTOK]).then_inc(zeroed.sem, 16)
            sp.dma_start(returned_d.rearrange("(p r) d -> p (r d)", p=P), zeros).then_inc(zeroed.sem, 16)
            load(sp, "ffn0", wfc[:, :, :], a["L0_ffn_w_fc"].rearrange("(c p) d -> p c d", p=P))
            load(sp, "ffn0", wpr[:, :], a["L0_ffn_w_proj"])
            load(sp, "ffn0", lr[:, :, :], a["L0_ffn_u"].rearrange("(c p) r -> p c r", p=P))
            with nc.allow_non_contiguous_dma(reason="a 16x16 transpose"):
                load(sp, "ffn0", fbT[:, :], a["L0_ffn_fast_b"].rearrange("i j -> j i"))
            load(sp, "ffn0", vlow[:, :], a["L0_ffn_v"])
            load(sp, "ffn0", gate[:, :], a["L0_ffn_gate"].rearrange("(a n) -> a n", a=1).broadcast_to([16, 1]))
            for n, dst in (("Wq", w1q), ("Wk", w1k), ("Wv", w1v)):
                load(sp, "attn1", dst, a["L1_xattn_" + n].rearrange("(c p) d -> p c d", p=P))
            load(sp, "attn1", w1o, a["L1_xattn_Wo"])
            load(sp, "attn1", rows[0:1, 1, :], a["L1_xattn_bo"].rearrange("(a n) -> a n", a=1))
            load(sp, "mask1", mask_raw[:, :, :], a["mask_Bx1xSxS2_ik0"].rearrange("b o (t p) k -> p (b o t) k", p=P))
            load(sp, "mask1", src_raw[:, :, :].rearrange("p b k -> p (b k)"),
                 a["mask_Bx1xS2_bk0"].bitcast(U8).rearrange("(a n) -> a n", a=1).broadcast_to([P, NB * CK]))
            load(sp, "ffn1", we[:, :, :], a["L1_ffn_We"].rearrange("e d o -> d e o"))
            load(sp, "ffn1", be[:, :], a["L1_ffn_be"])
            load(sp, "ffn1", wg1[:, :], a["L1_ffn_Wg"])
            load(sp, "ffn1", bg1[:, :], a["L1_ffn_bg"].rearrange("(a n) -> a n", a=1).broadcast_to([P, NE]))
            for i, n in enumerate(("Wq", "Wk", "Wv", "Wp")):
                load(sp, "attn2", w2[:, i, :], a["L2_xattn_" + n])
            load(sp, "attn2", rows[0:1, 2, :], a["L2_xattn_bp"].rearrange("(a n) -> a n", a=1))
            for i, n in enumerate(("wq", "wk", "wv", "w_out")):
                load(sp, "attn3", w3[:, i, :], a["L3_xattn_" + n])
            load(sp, "ffn2", attn_w[:, :], a["L2_ffn_attn_w"])
            load(sp, "ffn2", next_w[:, :], a["L2_ffn_next_w"])
            load(sp, "ffn2", rows[0:1, 3, :], a["L2_ffn_next_b"].rearrange("(a n) -> a n", a=1))
            with nc.allow_non_contiguous_dma(reason="biases as columns"):
                for i, n in enumerate(("ln_g", "ln_b", "attn_b")):
                    load(sp, "ffn2", cols2[:, i:i + 1], a["L2_ffn_" + n].rearrange("(n a) -> n a", a=1))
                load(sp, "ffn2", b1c[:, :, :], a["L2_ffn_b1"].rearrange("e (c p) -> p e c", p=P))
                load(sp, "ffn2", b2c[:, :], a["L2_ffn_b2"].rearrange("e d -> d e"))
            sp.wait_ge(mask_made.sem, 2 + NB)
            load(sp, "mask3", mask_raw[:, :, :], a["mask_BxSxS2_ik1"].rearrange("b (t p) k -> p (b t) k", p=P))
            TB[1].wait_full(sp, "prepL1x", turned_bank(H16 - 1)[1])
            load(sp, "ffn2", w1e, a["L2_ffn_w1"].rearrange("e d f -> d e f"))
            load(sp, "ffn2", w2e, a["L2_ffn_w2"].rearrange("e (c p) d -> p e c d", p=P))
            sp.wait_ge(x_done.sem, x_done.after("L2f", 0, NB - 1))
            load(sp, "small3", nw_all, a["L3_ffn_attn_nw"].rearrange("(a n) -> a n", a=1).broadcast_to([P, P]))
            load(sp, "small3", nb_all, a["L3_ffn_attn_nb"].rearrange("(a n) -> a n", a=1).broadcast_to([P, P]))
            load(sp, "small3", wgc[:, 0:NE], a["L3_ffn_wg"])
            load(sp, "small3", wgc[:, NE:NE + 2], a["L3_ffn_res_coef"])
            load(sp, "small3", res_w1, a["L3_ffn_res_inter_w"])
            load(sp, "small3", res_w2[:, :, :], a["L3_ffn_res_output_w"].rearrange("(c p) d -> p c d", p=P))
            load(sp, "small3", rows[0:1, 4, :], a["L3_ffn_res_output_b"].rearrange("(a n) -> a n", a=1))
            with nc.allow_non_contiguous_dma(reason="biases as columns"):
                load(sp, "ffn3", b1c[:, :, :], a["L3_ffn_inter_b"].rearrange("e (c p) -> p e c", p=P))
                load(sp, "small3", cols3[:, 0:1], a["L3_ffn_attn_nw"].rearrange("(n a) -> n a", a=1))
                load(sp, "small3", cols3[:, 1:2], a["L3_ffn_attn_nb"].rearrange("(n a) -> n a", a=1))
                load(sp, "small3", cols3[:, 2:2 + NC], a["L3_ffn_res_inter_b"].rearrange("(c p) -> p c", p=P))
            load(sp, "ffn3", w1e, a["L3_ffn_inter_w"].rearrange("e d f -> d e f"))
            load(sp, "ffn3", w2e, a["L3_ffn_output_w"].rearrange("e (c p) d -> p e c d", p=P))
            sp.wait_ge(x_done.sem, x_done.after("L3x", 0, NB - 1))
            load(sp, "ffn3", out_b_all.rearrange("p e d -> p (e d)"),
                 a["L3_ffn_output_b"].rearrange("(a e) d -> a (e d)", a=1).broadcast_to([P, NE * P]))
            assert all(loads[k] == v for k, v in LOADS.items() if k != "const"), loads
            sp.wait_ge(scattered.sem, 16 * NB * NT)
            sp.dma_start(sent, dispatched_d.rearrange("(g p) d -> p g d", p=P)).then_inc(sent_loaded.sem, 16)
            sp.wait_ge(returned.sem, 16 * NTOK // P)
            for b in range(NB):
                sp.dma_start(got[:, b * NT:(b + 1) * NT, :],
                             returned_d[b * NT * P:(b + 1) * NT * P, :].rearrange("(t p) d -> p t d", p=P))\
                    .then_inc(gathered[b].sem, 16)
            for b in range(NB):
                sp.wait_ge(x_done.sem, x_done.after(LAYERS[-1], 0, b))
                sp.dma_start(out[b].rearrange("(t p) d -> p t d", p=P), x[:, b * NT:(b + 1) * NT, :])\
                    .then_inc(out_done.sem, 16)
            sp.wait_ge(out_done.sem, 16 * NB)
            for n in loaded:
                if loads[n] and n != "const":
                    sp.wait_ge(loaded[n].sem, loads[n])

        @block.gpsimd
        def _(pool):
            for bk in BANKS:
                pool.sem_inc(bk.drained.sem, 1)
            pool.sem_inc(pool_sum.sem, pool_sum.credit)
            pool.sem_inc(normed_ready.sem, normed_ready.credit)
            k = [0]

            def step(ins):
                k[0] += 1
                ins.then_inc(pool_step.sem, 1)
                pool.wait_ge(pool_step.sem, k[0])

            pool.memset(ident[:, :], 0.0)
            step(pool.memset(blk[:, :], 1.0))
            pool.affine_select(out=ident[:, :], in_=ident[:, :], compare_op=ALU.not_equal, fill=1.0, base=0,
                               pattern=[[-1, P]], channel_multiplier=1)
            step(pool.affine_select(out=blk[:, :], in_=blk[:, :], compare_op=ALU.is_ge, fill=0.0, base=0,
                                    pattern=[[-8, H16]], channel_multiplier=1))
            pool.affine_select(out=blk[:, :], in_=blk[:, :], compare_op=ALU.is_ge, fill=0.0, base=7,
                               pattern=[[8, H16]], channel_multiplier=-1).then_inc(made.sem, 1)
            for r in range(3):
                last = pool.tensor_copy(key_of_row[:, r * CK:(r + 1) * CK], ident[:, 0:CK])
            last.then_inc(rep_made.sem, 1)
            pool.memset(grid[:, :, :], 1.0)
            pool.memset(minus_half[:, :], -0.5)
            pool.memset(eps5[:, :], EPS)
            pool.memset(eps12[:, :], EPS3)
            pool.memset(ones[:, :], 1.0)
            pool.tensor_copy(identb[:, :], ident[:, :])
            pool.memset(V2[:, :, :, 64], 1.0)
            step(pool.memset(causal[:, :], 0.0))
            step(pool.affine_select(out=causal[:, :], in_=causal[:, :], compare_op=ALU.is_ge, fill=-1e13, base=0,
                                    pattern=[[-1, CK]], channel_multiplier=1))
            step(pool.iota(iota8[:, :], pattern=[[1, NE]], base=0, channel_multiplier=0,
                           allow_small_or_imprecise_dtypes=True))
            for c, h0 in enumerate(CHUNK_HEAD):
                last = pool.affine_select(out=grid[:, c, :], in_=grid[:, c, :], compare_op=ALU.is_ge, fill=0.0,
                                          base=P * c - CK * h0, pattern=[[-CK, 3]], channel_multiplier=1)
            step(last)
            for c, h0 in enumerate(CHUNK_HEAD):
                last = pool.affine_select(out=grid[:, c, :], in_=grid[:, c, :], compare_op=ALU.is_ge, fill=0.0,
                                          base=CK - 1 - P * c + CK * h0, pattern=[[CK, 3]], channel_multiplier=-1)
            step(last)
            pool.tensor_copy(V03[:, :, :, :, 8], spread(grid[:, :, :], 1, NB)).then_inc(grid_made.sem, 1)
            assert k[0] == POOL_STEPS, k
            pool.memset(hT[:, :, :], 0.0).then_inc(zeros_made.sem, 1)
            run_attention16(pool, "pool", "L0x")
            run_ffn0(pool, "pool")
            run_attention16(pool, "pool", "L1x")
            run_ffn1(pool, "pool")
            run_attention2(pool, "pool")
            run_ffn2(pool, "pool")
            run_attention16(pool, "pool", "L3x")
            route_constants_pool(pool)
            run_ffn3(pool, "pool")

        @block.scalar
        def _(act):
            load(act, "const", phw[:, 0:H16], a["phase_weights"])
            load(act, "const", phw[:, 16:17], a["phase_intrinsic"])
            load(act, "const", ph[:, 7:8], a["L0_xattn_coupling"].rearrange("(n a) -> n a", a=1))
            start_act(act)
            run_attention16(act, "act", "L0x")
            run_ffn0(act, "act")
            prep1_act(act)
            run_attention16(act, "act", "L1x")
            run_ffn1(act, "act")
            run_attention2(act, "act")
            run_ffn2(act, "act")
            for part in range(1, 5):
                prep03_act(act, "L3x", part)
            run_attention16(act, "act", "L3x")
            run_ffn3(act, "act")

        @block.vector
        def _(dve):
            start_dve(dve)
            run_attention16(dve, "dve", "L0x")
            run_ffn0(dve, "dve")
            prep1_dve(dve)
            run_attention16(dve, "dve", "L1x")
            dve.wait_ge(loaded["ffn1"].sem, LOADS["ffn1"])
            run_ffn1(dve, "dve")
            run_attention2(dve, "dve")
            run_ffn2(dve, "dve")
            for part in range(1, 5):
                prep03_dve(dve, "L3x", part)
            dve.wait_ge(loaded["mask3"].sem, LOADS["mask3"])
            dve.tensor_scalar(mask3[:, :, :], mask_raw[:, :, :], 1.0, MASKED, ALU.is_equal, ALU.mult)\
                .then_inc(mask_made.sem, 1)
            run_attention16(dve, "dve", "L3x")
            run_ffn3(dve, "dve")

        @block.tensor
        def _(pe):
            start_pe(pe)
            run_attention16(pe, "pe", "L0x")
            run_ffn0(pe, "pe")
            prep1_pe(pe)
            pe.wait_ge(mask_made.sem, 2 + NB)
            for h in range(H16 - 4, H16):
                bk, u = head_bank(h)
                bk.wait_drained(pe, "prepL1x", u)
            run_attention16(pe, "pe", "L1x")
            pe.wait_ge(loaded["ffn1"].sem, LOADS["ffn1"])
            run_ffn1(pe, "pe")
            prepared_pe(pe, "L2x")
            run_attention2(pe, "pe")
            run_ffn2(pe, "pe")
            for part in range(1, 5):
                prep03_pe(pe, "L3x", part)
            pe.wait_ge(mask_made.sem, 3 + NB)
            for bk, u in G_BANKS["L3x"]:
                bk.wait_drained(pe, "prepL3x", u)
            run_attention16(pe, "pe", "L3x")
            run_ffn3(pe, "pe")


def phase_tables():
    side = 4
    w = np.zeros((H16, H16), np.float32)
    for i in range(H16):
        for j in range(i):
            dr, dc = j // side - i // side, j % side - i % side
            if abs(dr) <= 1 and abs(dc) <= 1:
                w[j, i] = math.exp(-math.hypot(dr, dc))
    f = np.asarray([[0.01 * (1.0 + 0.1 * h)] for h in range(H16)], np.float32)
    return w, f


_INS = ['x', 'ctx_1024', 'mask_Bx1xSxS2_ik0', 'mask_Bx1xS2_bk0', 'mask_BxSxS2_ik1', 'L0_xattn_Wq', 'L0_xattn_Wk', 'L0_xattn_Wv', 'L0_xattn_out_w', 'L0_xattn_out_b', 'L0_xattn_coupling', 'L0_ffn_fast_b', 'L0_ffn_w_fc', 'L0_ffn_w_proj', 'L0_ffn_u', 'L0_ffn_v', 'L0_ffn_gate', 'L1_xattn_Wq', 'L1_xattn_Wk', 'L1_xattn_Wv', 'L1_xattn_Wo', 'L1_xattn_bo', 'L1_ffn_We', 'L1_ffn_be', 'L1_ffn_Wg', 'L1_ffn_bg', 'L2_xattn_Wq', 'L2_xattn_Wk', 'L2_xattn_Wv', 'L2_xattn_Wp', 'L2_xattn_bp', 'L2_ffn_ln_g', 'L2_ffn_ln_b', 'L2_ffn_attn_w', 'L2_ffn_attn_b', 'L2_ffn_w1', 'L2_ffn_b1', 'L2_ffn_w2', 'L2_ffn_b2', 'L2_ffn_next_w', 'L2_ffn_next_b', 'L3_xattn_wq', 'L3_xattn_wk', 'L3_xattn_wv', 'L3_xattn_w_out', 'L3_ffn_attn_nw', 'L3_ffn_attn_nb', 'L3_ffn_wg', 'L3_ffn_inter_w', 'L3_ffn_inter_b', 'L3_ffn_output_w', 'L3_ffn_output_b', 'L3_ffn_res_inter_w', 'L3_ffn_res_inter_b', 'L3_ffn_res_output_w', 'L3_ffn_res_output_b', 'L3_ffn_res_coef']


def kernel(**inputs):
    import numpy as _np
    import concourse.bacc as _bacc
    from concourse import mybir as _mybir
    from concourse.bass_utils import run_bass_kernel_spmd as _run

    nc = _bacc.Bacc("TRN2", target_bir_lowering=False, num_devices=1)
    arrays, args = {}, {}

    def give(name, a):
        arrays[f"in_{name}_dram"] = a
        args[name] = nc.dram_tensor(f"in_{name}_dram", a.shape, _mybir.dt.from_np(a.dtype), kind="ExternalInput").ap()

    for name in _INS:
        a = _np.ascontiguousarray(inputs[name])
        if a.dtype == _np.bool_:
            a = a.reshape(-1).view(_np.int32)
        if a.shape == ():
            a = a.reshape(1)
        give(name, a)
    w, f = phase_tables()
    give("phase_weights", w)
    give("phase_intrinsic", f)
    o = nc.dram_tensor("out_0_dram", (NB, NT * P, P), _mybir.dt.float32, kind="ExternalOutput").ap()
    four_layers(nc, args, o)
    r = _run(nc, [arrays], core_ids=[0])
    return r.results[0]["out_0_dram"]
```
